# Optimizing a Trainium2 kernel written in Bass

```python
import numpy as np
import jax
import jax.numpy as jnp

def _softmax(x, axis=-1):
    return jax.nn.softmax(x, axis=axis)

def _gelu(x):
    return jax.nn.gelu(x, approximate=True)

def _silu(x):
    return jax.nn.silu(x)

def _sigmoid(x):
    return jax.nn.sigmoid(x)

def _layernorm(x, axis=-1, eps=1e-05):
    m = jnp.mean(x, axis=axis, keepdims=True)
    v = jnp.var(x, axis=axis, keepdims=True)
    return (x - m) / jnp.sqrt(v + eps)

def _scatter_add(tgt, idx, src, axis=0):
    return tgt.at[idx].add(src)

def _segment_sum(src, seg, n):
    return jax.ops.segment_sum(src, seg, n)
kernel_name = 'mk_gnn_preln_d4_gnn_r8_a2320c'

def setup_inputs(seed: int=0):
    np.random.seed(seed)
    _w = jnp.asarray

    def _rec_inputs():
        import jax
        import jax.numpy as jnp
        _gk = jax.random.key(seed)
        x = -0.0003713 + 1 * jax.random.normal(jax.random.fold_in(_gk, 1), (12500, 128), jnp.float32)
        src = jax.random.randint(jax.random.fold_in(_gk, 2), (200000,), 0, 12500, jnp.int32)
        dst = jax.random.randint(jax.random.fold_in(_gk, 3), (200000,), 0, 12500, jnp.int32)
        _o = jnp.argsort(dst, stable=True)
        src = src[_o]
        dst = dst[_o]
        edge_attr_128 = 2.93046e-05 + 1.00006 * jax.random.normal(jax.random.fold_in(_gk, 11), (200000, 128), jnp.float32)
        return (x, src, dst, edge_attr_128)
    x, src, dst, edge_attr_128 = _rec_inputs()

    def _L0_gnn_setup():
        import jax, jax.numpy as jnp
        import numpy as np
        N = 12500
        E = 200000
        D = 128
        key = jax.random.key(seed)
        ks = jax.random.split(key, 8)
        x = jax.random.normal(ks[0], (N, D), dtype=jnp.float32)
        edge_index = jax.random.randint(ks[1], (2, E), 0, N, dtype=jnp.int32)
        scale = 1.0 / np.sqrt(2 * D)
        W0 = jax.random.normal(ks[2], (2 * D, D), dtype=jnp.float32) * scale
        b0 = jax.random.normal(ks[3], (D,), dtype=jnp.float32) * scale
        W1 = jax.random.normal(ks[4], (2 * D, D), dtype=jnp.float32) * scale
        b1 = jax.random.normal(ks[5], (D,), dtype=jnp.float32) * scale
        W2 = jax.random.normal(ks[6], (2 * D, D), dtype=jnp.float32) * scale
        b2 = jax.random.normal(ks[7], (D,), dtype=jnp.float32) * scale
        return {'x': x, 'edge_index': edge_index, 'W0': W0, 'b0': b0, 'W1': W1, 'b1': b1, 'W2': W2, 'b2': b2}
    _L0_gnn_all = _L0_gnn_setup()
    _L0_gnn_in = {k: v for k, v in _L0_gnn_all.items() if k in ('W0', 'b0', 'W1', 'b1', 'W2', 'b2')}
    del _L0_gnn_all

    def _L1_gnn_setup():
        import jax, jax.numpy as jnp
        import numpy as np
        N = 6250
        E = 100000
        DIN = 128
        H = 4
        C = 32
        EPS = 1e-05
        NEG_SLOPE = 0.2

        def layer_norm(x, g, b):
            m = jnp.mean(x, axis=-1, keepdims=True)
            v = jnp.mean((x - m) ** 2, axis=-1, keepdims=True)
            return (x - m) * jax.lax.rsqrt(v + EPS) * g + b

        def gat_conv(h, src, dst, W, att_src, att_dst, gat_b, n):
            xh = (h @ W).reshape(n, H, C)
            a_src = jnp.einsum('nhc,hc->nh', xh, att_src)
            a_dst = jnp.einsum('nhc,hc->nh', xh, att_dst)
            alpha = jax.nn.leaky_relu(a_src[src] + a_dst[dst], NEG_SLOPE)
            amax = jax.ops.segment_max(alpha, dst, num_segments=n)
            alpha = jnp.exp(alpha - amax[dst])
            denom = jax.ops.segment_sum(alpha, dst, num_segments=n)
            alpha = alpha / denom[dst]
            msg = xh[src] * alpha[:, :, None]
            out = jax.ops.segment_sum(msg, dst, num_segments=n)
            return out.reshape(n, H * C) + gat_b
        key = jax.random.key(seed)
        ks = jax.random.split(key, 14)
        s = 1.0 / np.sqrt(DIN)
        return {'x': jax.random.normal(ks[0], (N, DIN), dtype=jnp.float32), 'edge_index': jax.random.randint(ks[1], (2, E), 0, N, dtype=jnp.int64), 'ln1_g': jnp.ones((DIN,), jnp.float32), 'ln1_b': jnp.zeros((DIN,), jnp.float32), 'W': jax.random.normal(ks[2], (DIN, H * C), jnp.float32) * s, 'att_src': jax.random.normal(ks[3], (H, C), jnp.float32) * (1.0 / np.sqrt(C)), 'att_dst': jax.random.normal(ks[4], (H, C), jnp.float32) * (1.0 / np.sqrt(C)), 'gat_b': jnp.zeros((H * C,), jnp.float32), 'ln2_g': jnp.ones((H * C,), jnp.float32), 'ln2_b': jnp.zeros((H * C,), jnp.float32), 'w1': jax.random.normal(ks[5], (H * C, 2 * H * C), jnp.float32) * (1.0 / np.sqrt(H * C)), 'b1': jnp.zeros((2 * H * C,), jnp.float32), 'w2': jax.random.normal(ks[6], (2 * H * C, H * C), jnp.float32) * (1.0 / np.sqrt(2 * H * C)), 'b2': jnp.zeros((H * C,), jnp.float32)}
    _L1_gnn_all = _L1_gnn_setup()
    _L1_gnn_in = {k: v for k, v in _L1_gnn_all.items() if k in ('ln1_g', 'ln1_b', 'W', 'att_src', 'att_dst', 'gat_b', 'ln2_g', 'ln2_b', 'w1', 'b1', 'w2', 'b2')}
    del _L1_gnn_all

    def _L2_gnn_setup():
        import jax, jax.numpy as jnp
        import numpy as np
        N = 6250
        E = 80000
        D = 128
        H = 2 * D
        BN_EPS = 1e-05

        def _batchnorm(x, gamma, beta):
            mean = jnp.mean(x, axis=0)
            var = jnp.var(x, axis=0)
            return (x - mean) * jax.lax.rsqrt(var + BN_EPS) * gamma + beta
        key = jax.random.key(seed)
        ks = jax.random.split(key, 8)
        h = jax.random.normal(ks[0], (N, D), dtype=jnp.float32)
        edge_index = jax.random.randint(ks[1], (2, E), 0, N, dtype=jnp.int64)
        edge_attr = jax.random.normal(ks[2], (E, D), dtype=jnp.float32)
        W1 = jax.random.normal(ks[3], (D, H), dtype=jnp.float32) * (1.0 / np.sqrt(D))
        g1 = jnp.ones((H,), dtype=jnp.float32)
        b1 = jnp.zeros((H,), dtype=jnp.float32)
        W2 = jax.random.normal(ks[4], (H, D), dtype=jnp.float32) * (1.0 / np.sqrt(H))
        g2 = jnp.ones((D,), dtype=jnp.float32)
        b2 = jnp.zeros((D,), dtype=jnp.float32)
        eps = jnp.zeros((), dtype=jnp.float32)
        return {'h': h, 'edge_index': edge_index, 'edge_attr': edge_attr, 'eps': eps, 'W1': W1, 'g1': g1, 'b1': b1, 'W2': W2, 'g2': g2, 'b2': b2}
    _L2_gnn_all = _L2_gnn_setup()
    _L2_gnn_in = {k: v for k, v in _L2_gnn_all.items() if k in ('eps', 'W1', 'g1', 'b1', 'W2', 'g2', 'b2')}
    del _L2_gnn_all

    def _L3_gnn_setup():
        import jax, jax.numpy as jnp
        import numpy as np
        N_NODES = 12500
        N_EDGES = 75000
        D_FEAT = 128
        key = jax.random.key(seed)
        k1, k2, k3 = jax.random.split(key, 3)
        x = jax.random.normal(k1, (N_NODES, D_FEAT), dtype=jnp.float32)
        edge_attr = jax.random.normal(k2, (N_EDGES, D_FEAT), dtype=jnp.float32)
        edge_index = jax.random.randint(k3, (2, N_EDGES), 0, N_NODES, dtype=jnp.int64)
        return {'x': x, 'edge_attr': edge_attr, 'edge_index': edge_index}
    _L3_gnn_all = _L3_gnn_setup()
    _L3_gnn_in = {k: v for k, v in _L3_gnn_all.items() if k in ()}
    del _L3_gnn_all
    return {'x': x, 'src': src, 'dst': dst, 'edge_attr_128': edge_attr_128, 'L0_gnn_W0': _L0_gnn_in['W0'], 'L0_gnn_b0': _L0_gnn_in['b0'], 'L0_gnn_W1': _L0_gnn_in['W1'], 'L0_gnn_b1': _L0_gnn_in['b1'], 'L0_gnn_W2': _L0_gnn_in['W2'], 'L0_gnn_b2': _L0_gnn_in['b2'], 'L1_gnn_ln1_g': _L1_gnn_in['ln1_g'], 'L1_gnn_ln1_b': _L1_gnn_in['ln1_b'], 'L1_gnn_W': _L1_gnn_in['W'], 'L1_gnn_att_src': _L1_gnn_in['att_src'], 'L1_gnn_att_dst': _L1_gnn_in['att_dst'], 'L1_gnn_gat_b': _L1_gnn_in['gat_b'], 'L1_gnn_ln2_g': _L1_gnn_in['ln2_g'], 'L1_gnn_ln2_b': _L1_gnn_in['ln2_b'], 'L1_gnn_w1': _L1_gnn_in['w1'], 'L1_gnn_b1': _L1_gnn_in['b1'], 'L1_gnn_w2': _L1_gnn_in['w2'], 'L1_gnn_b2': _L1_gnn_in['b2'], 'L2_gnn_eps': _L2_gnn_in['eps'], 'L2_gnn_W1': _L2_gnn_in['W1'], 'L2_gnn_g1': _L2_gnn_in['g1'], 'L2_gnn_b1': _L2_gnn_in['b1'], 'L2_gnn_W2': _L2_gnn_in['W2'], 'L2_gnn_g2': _L2_gnn_in['g2'], 'L2_gnn_b2': _L2_gnn_in['b2']}

def reference(x, src, dst, edge_attr_128, L0_gnn_W0, L0_gnn_b0, L0_gnn_W1, L0_gnn_b1, L0_gnn_W2, L0_gnn_b2, L1_gnn_ln1_g, L1_gnn_ln1_b, L1_gnn_W, L1_gnn_att_src, L1_gnn_att_dst, L1_gnn_gat_b, L1_gnn_ln2_g, L1_gnn_ln2_b, L1_gnn_w1, L1_gnn_b1, L1_gnn_w2, L1_gnn_b2, L2_gnn_eps, L2_gnn_W1, L2_gnn_g1, L2_gnn_b1, L2_gnn_W2, L2_gnn_g2, L2_gnn_b2):
    import jax
    import jax.numpy as jnp

    def _L0_gnn_ref(x, edge_index, W0, b0, W1, b1, W2, b2):
        import jax, jax.numpy as jnp
        import numpy as np
        N = 12500
        E = 200000
        D = 128
        src, dst = (edge_index[0], edge_index[1])
        n = x.shape[0]
        count = jax.ops.segment_sum(jnp.ones((src.shape[0],), dtype=x.dtype), dst, num_segments=n)
        inv = 1.0 / (count + 1.0)
        for W, b in ((W0, b0), (W1, b1), (W2, b2)):
            agg = jax.ops.segment_sum(x[src], dst, num_segments=n)
            neigh = agg * inv[:, None]
            x = jax.nn.relu(jnp.concatenate([x, neigh], axis=-1) @ W + b)
        return x

    def _L1_gnn_ref(x, edge_index, ln1_g, ln1_b, W, att_src, att_dst, gat_b, ln2_g, ln2_b, w1, b1, w2, b2):
        import jax, jax.numpy as jnp
        import numpy as np
        N = 6250
        E = 100000
        DIN = 128
        H = 4
        C = 32
        EPS = 1e-05
        NEG_SLOPE = 0.2

        def layer_norm(x, g, b):
            m = jnp.mean(x, axis=-1, keepdims=True)
            v = jnp.mean((x - m) ** 2, axis=-1, keepdims=True)
            return (x - m) * jax.lax.rsqrt(v + EPS) * g + b

        def gat_conv(h, src, dst, W, att_src, att_dst, gat_b, n):
            xh = (h @ W).reshape(n, H, C)
            a_src = jnp.einsum('nhc,hc->nh', xh, att_src)
            a_dst = jnp.einsum('nhc,hc->nh', xh, att_dst)
            alpha = jax.nn.leaky_relu(a_src[src] + a_dst[dst], NEG_SLOPE)
            amax = jax.ops.segment_max(alpha, dst, num_segments=n)
            alpha = jnp.exp(alpha - amax[dst])
            denom = jax.ops.segment_sum(alpha, dst, num_segments=n)
            alpha = alpha / denom[dst]
            msg = xh[src] * alpha[:, :, None]
            out = jax.ops.segment_sum(msg, dst, num_segments=n)
            return out.reshape(n, H * C) + gat_b
        n = x.shape[0]
        loops = jnp.arange(n, dtype=edge_index.dtype)
        src = jnp.concatenate([edge_index[0], loops])
        dst = jnp.concatenate([edge_index[1], loops])
        h = layer_norm(x, ln1_g, ln1_b)
        h = gat_conv(h, src, dst, W, att_src, att_dst, gat_b, n)
        h = h + x
        hn = layer_norm(h, ln2_g, ln2_b)
        ffn = jax.nn.gelu(hn @ w1 + b1, approximate=False) @ w2 + b2
        return h + ffn

    def _L2_gnn_ref(h, edge_index, edge_attr, eps, W1, g1, b1, W2, g2, b2):
        import jax, jax.numpy as jnp
        import numpy as np
        N = 6250
        E = 80000
        D = 128
        H = 2 * D
        BN_EPS = 1e-05

        def _batchnorm(x, gamma, beta):
            mean = jnp.mean(x, axis=0)
            var = jnp.var(x, axis=0)
            return (x - mean) * jax.lax.rsqrt(var + BN_EPS) * gamma + beta
        n = h.shape[0]
        src = edge_index[0]
        dst = edge_index[1]
        msg = jax.nn.relu(h[src] + edge_attr)
        aggr = jax.ops.segment_sum(msg, dst, num_segments=n)
        z = (1.0 + eps) * h + aggr
        z = jax.nn.relu(_batchnorm(z @ W1, g1, b1))
        z = z @ W2
        z = jax.nn.relu(_batchnorm(z, g2, b2))
        return z + h

    def _L3_gnn_ref(x, edge_attr, edge_index):
        import jax, jax.numpy as jnp
        import numpy as np
        N_NODES = 12500
        N_EDGES = 75000
        D_FEAT = 128
        src, dst = (edge_index[0], edge_index[1])
        x_src = x[src]
        messages = x_src + edge_attr
        aggr = jax.ops.segment_sum(messages, dst, num_segments=x.shape[0])
        return x + aggr
    edge_index = jnp.stack([src, dst])
    h = jnp.maximum(_layernorm(x, axis=-1), 0.0)
    x = x + _L0_gnn_ref(h, edge_index, L0_gnn_W0, L0_gnn_b0, L0_gnn_W1, L0_gnn_b1, L0_gnn_W2, L0_gnn_b2)
    h = jnp.maximum(_layernorm(x, axis=-1), 0.0)
    x = x + _L1_gnn_ref(h, edge_index, L1_gnn_ln1_g, L1_gnn_ln1_b, L1_gnn_W, L1_gnn_att_src, L1_gnn_att_dst, L1_gnn_gat_b, L1_gnn_ln2_g, L1_gnn_ln2_b, L1_gnn_w1, L1_gnn_b1, L1_gnn_w2, L1_gnn_b2)
    h = jnp.maximum(_layernorm(x, axis=-1), 0.0)
    x = x + _L2_gnn_ref(h, edge_index, edge_attr_128, L2_gnn_eps, L2_gnn_W1, L2_gnn_g1, L2_gnn_b1, L2_gnn_W2, L2_gnn_g2, L2_gnn_b2)
    h = jnp.maximum(_layernorm(x, axis=-1), 0.0)
    x = x + _L3_gnn_ref(h, edge_attr_128, edge_index)
    return x

_drawn_inputs = setup_inputs


def setup_inputs(seed=0):
    import zlib

    import numpy as np

    out = dict(_drawn_inputs(seed))
    spreads = {'L1_gnn_ln1_g': (1.0, 0.2),
     'L1_gnn_ln1_b': (0.0, 0.1),
     'L1_gnn_gat_b': (0.0, 0.1),
     'L1_gnn_ln2_g': (1.0, 0.2),
     'L1_gnn_ln2_b': (0.0, 0.1),
     'L1_gnn_b1': (0.0, 0.291),
     'L1_gnn_b2': (0.0, 0.1),
     'L2_gnn_g1': (1.0, 0.6),
     'L2_gnn_b1': (0.0, 0.8),
     'L2_gnn_g2': (1.0, 0.2),
     'L2_gnn_b2': (0.0, 0.386)}
    factors = {'L0_gnn_b0': 2.728}
    for name, (base, spread) in spreads.items():
        noise = np.random.default_rng([zlib.crc32(name.encode()), seed]).standard_normal(out[name].shape)
        drawn = base * np.exp(spread * noise) if base else spread * noise
        out[name] = jnp.asarray(drawn.astype(out[name].dtype))
    for name, factor in factors.items():
        out[name] = (out[name] * factor).astype(out[name].dtype)
    return out
```

```python
from contextlib import ExitStack, contextmanager

import concourse.bass as bass
from concourse import mybir

F32 = mybir.dt.float32
I32 = mybir.dt.int32
ALU = mybir.AluOpType
ACT = mybir.ActivationFunctionType
AX_X = mybir.AxisListType.X

N = 12500
E = 200000
D = 128
P = 128
CH = 500
NCH = N // CH
SUB = 125
NSUB = N // SUB
TILE = 128
HALF = 16
GT = 4
GPH = HALF // GT
NHALF = 98
NIT = NHALF // 2
NTILE = NHALF * HALF
NGRP = NTILE // GT
EP = NTILE * TILE
GE = GT * TILE
W = 64
EPP = EP // P
H = 4
C = D // H
XW = D + 2 * H
EPS = 1e-5
BIG = 1e38
NSC = -(-(EP + N) // P) * P
REG = 12800


class Net:

    def __init__(self, nc, ctx, dram):
        self.nc, self.ctx, self.dram = nc, ctx, dram
        self.pool_sems = [ctx.enter_context(nc.semaphore(f"pool_dma{k}")) for k in range(15)]
        self.stage_sems, self.stage_ctx = [], None

    @contextmanager
    def stage(self):
        with ExitStack() as self.stage_ctx:
            yield
            sems, self.stage_sems = self.stage_sems, []
            with self.nc.Block() as block:
                @block.sync
                def _(sp):
                    for x in sems:
                        sp.sem_clear(x)

    def sem(self, name):
        x = self.stage_ctx.enter_context(self.nc.semaphore(name))
        self.stage_sems.append(x)
        return x

    def pool_sem(self):
        return self.pool_sems.pop()

    def sb(self, name, shape, dt=F32):
        return self.ctx.enter_context(self.nc.sbuf_tensor(name, shape, dt))

    def hbm(self, name, shape, dt=F32):
        return self.nc.dram_tensor(name, shape, dt, kind="Internal").ap()

    def col(self, t, c):
        return t[:, bass.ds(c * CH, CH)]

    def bank(self, first, c, n=CH):
        return self.psum[:, bass.ds((c % 2) * 512 + first * 512, n)]


def allocate(net):
    net.A = net.sb("regionA", [P, REG])
    net.B = net.sb("regionB", [P, REG])
    net.C = net.sb("regionC", [P, NSUB * XW])
    net.work = net.sb("work", [P, 2 * HALF * XW])
    net.onehot = net.sb("onehot", [P, 2, HALF, W])
    net.src_n = net.sb("src_n", [P, NTILE])
    net.rel_n = net.sb("rel_n", [P, NTILE])
    net.index = net.sb("index", [P, 2, HALF], I32)
    net.base = net.sb("base", [1, NGRP], I32)
    net.base_now = net.sb("base_now", [1, NGRP], I32)
    net.rounds = net.sb("rounds", [1, 1], I32)
    net.window0 = net.sb("window0", [P, W])
    net.window = net.sb("window", [P, W])
    net.ident = net.sb("ident", [P, P])
    net.mean_w = net.sb("mean_w", [P, P])
    net.ones = net.sb("ones", [P, P])
    net.eps = net.sb("eps", [P, 1])
    net.psum = net.ctx.enter_context(net.nc.psum_tensor("psum", [P, 8 * 512], F32))
    net.p_self = net.sb("p_self", [SUB, NSUB * H])
    net.wtmp = net.sb("weights", [P, 2 * 2 * D + 4 * D + 24])
    net.small = net.sb("small", [P, 160])

    net.XT = net.hbm("x_transposed", [D, N])
    net.HT = net.hbm("h_transposed", [D, N])
    net.ES = net.hbm("edge_sum", [D, N])
    net.TA = net.hbm("rows_a", [N, D])
    net.TB = net.hbm("rows_b", [N, D])
    net.XH = net.hbm("attention_rows", [N, XW])
    net.G = net.hbm("gathered_rows", [NHALF, P, HALF * XW])
    net.SH = net.hbm("scores_by_head", [H, EP])
    net.PH = net.hbm("probs_by_head", [H, EP])
    net.FD = net.hbm("running_max", [EP, H])
    net.SC = net.hbm("segment_starts", [NSC, 2 * H])
    net.NV = net.hbm("node_values", [N, 2 * H])
    net.DEALT = net.hbm("dealt_lists", [2, P, NTILE])
    net.DST = net.hbm("dst_padded", [EP])
    net.BASE = net.hbm("group_bases", [NGRP], I32)
    net.CUM = net.hbm("segment_ends", [2, N])


def each_chunk(eng, body, count=NCH):
    with eng.Fori(0, count // 2) as i:
        for k in range(2):
            body(eng.snap(i * 2 + k), k)
    for c in range(count // 2 * 2, count):
        body(c, c % 2)


def slot(net, k, width=CH):
    return net.work[:, k * 512:k * 512 + width]



def rows_bring(net, pool, s, region, ready, start):
    pool.sem_inc(s["turned"], 2)

    def bring(c, k):
        pool.wait_ge(ready, c + 1 + start)
        pool.wait_ge(s["turned"], c + 1)
        net.nc.gpsimd.tensor_copy(slot(net, k), net.col(region, c)).then_inc(s["brought"], 1)
    each_chunk(pool, bring)


def rows_turn(net, pe, s, first):
    def turn(c, k):
        pe.wait_ge(s["brought"], c + 1)
        pe.wait_ge(s["rows"], c + 1)
        for j in range(4):
            t = net.nc.tensor.transpose(
                net.psum[0:SUB, (first + k) * 512 + j * D:(first + k) * 512 + (j + 1) * D],
                net.work[:, k * 512 + j * SUB:k * 512 + (j + 1) * SUB], net.ident[:, :])
        t.then_inc(s["turned"], 1)
    each_chunk(pe, turn)


def rows_copy(net, eng, copy, s, first, region):
    eng.sem_inc(s["rows"], 2)

    def out(c, k):
        eng.wait_ge(s["turned"], c + 3)
        copy(region[0:SUB, bass.ds(c * 4 * D, 4 * D)],
             net.psum[0:SUB, (first + k) * 512:(first + k + 1) * 512]).then_inc(s["rows"], 1)
    each_chunk(eng, out)


def rows_store(net, sp, s, region, table, width=D):
    with sp.Fori(0, NCH) as c:
        sp.wait_ge(s["rows"], c + 3)
        sp.dma_start(table[bass.ds(c * CH, CH), :].rearrange("(t p) f -> p t f", p=SUB),
                     region[0:SUB, bass.ds(c * 4 * width, 4 * width)].rearrange("p (t f) -> p t f", f=width)
                     ).then_inc(s["stored"], 16)
    sp.wait_ge(s["stored"], 16 * NCH)


def prepare(net):
    nc = net.nc
    GP = NGRP // GPH
    built, masked, filled = net.sem("pre_built"), net.sem("pre_masked"), net.sem("pre_filled")
    loaded_d, loaded_s = net.sem("pre_dst"), net.sem("pre_src")
    step, spread, wrote = net.sem("pre_step"), net.sem("pre_spread"), net.sem("pre_wrote")
    loaded_b, turned, copied = net.sem("pre_base"), net.sem("pre_turned"), net.sem("pre_copied")
    dst_i = net.A[0:GP, 0:GPH * GE].bitcast(I32)
    dst_f = net.A[0:GP, 2048:2048 + GPH * GE]
    rel_f = net.A[0:GP, 4096:4096 + GPH * GE]
    src_i = net.B[0:GP, 0:GPH * GE].bitcast(I32)
    src_f = net.B[0:GP, 2048:2048 + GPH * GE]
    dealt = [net.B[:, 4096 + k * NTILE:4096 + (k + 1) * NTILE] for k in range(2)]
    least, most = net.small[0:GP, 0:GPH], net.small[0:GP, 4:8]
    span = net.small[0:GP, 8:9]
    least_i = net.small[0:GP, 12:16].bitcast(I32)
    row = net.small[0:1, 16:20]
    it_i = net.work[:, 0:W].bitcast(I32)
    zeros = net.C[:, 0:2 * H * NSC // P // 2]
    whole = E // (GPH * GE)
    left = E - whole * GPH * GE
    lists = [(src_f, net.src_n, False), (rel_f, net.rel_n, False), (src_f, dealt[0], True), (rel_f, dealt[1], True)]
    tiles = [(fr, to, deal, g, k) for fr, to, deal in lists for g in range(GPH) for k in range(GT)]

    with nc.Block() as block:
        @block.gpsimd
        def _(pool):
            pool.memset(net.ident[:, :], 0.0).then_inc(built, 1)
            pool.iota(it_i, pattern=[[1, W]], base=0, channel_multiplier=0).then_inc(built, 1)
            pool.wait_ge(built, 2)
            pool.affine_select(out=net.ident[:, :], in_=net.ident[:, :], compare_op=ALU.not_equal,
                               fill=1.0, base=0, pattern=[[-1, P]],
                               channel_multiplier=1).then_inc(masked, 1)

        @block.sync
        def _(sp):
            sp.wait_ge(filled, 2)
            for name, to, sem in (("dst", dst_i, loaded_d), ("src", src_i, loaded_s)):
                sp.dma_start(to[0:whole, :], net.dram[name][0:whole * GPH * GE]
                             .rearrange("(p f) -> p f", p=whole)).then_inc(sem, 16)
                sp.dma_start(to[whole:whole + 1, 0:left], net.dram[name][whole * GPH * GE:E]
                             .rearrange("(p f) -> p f", p=1)).then_inc(sem, 16)
            sp.wait_ge(step, 4)
            sp.dma_start(net.DST.rearrange("(p f) -> p f", p=GP), dst_f).then_inc(wrote, 16)
            sp.dma_start(net.BASE.rearrange("(p f) -> p f", p=GP), least_i).then_inc(loaded_b, 16)
            sp.wait_ge(filled, 3)
            flat = net.SC.rearrange("(k p r) f -> k p (r f)", k=2, p=P)
            for k in range(2):
                sp.dma_start(flat[k], zeros).then_inc(wrote, 16)
            sp.wait_ge(loaded_b, 16)
            sp.dma_start(net.base[:, :], net.BASE.rearrange("(a g) -> a g", a=1)).then_inc(loaded_b, 16)
            sp.wait_ge(copied, len(tiles))
            for k in range(2):
                sp.dma_start(net.DEALT[k], dealt[k]).then_inc(wrote, 16)
            sp.wait_ge(wrote, 80)
            sp.wait_ge(loaded_b, 32)

        @block.vector
        def _(dve):
            nc.vector.memset(dst_i, N).then_inc(filled, 1)
            nc.vector.memset(src_i, 0).then_inc(filled, 1)
            nc.vector.memset(zeros, 0.0).then_inc(filled, 1)
            nc.vector.memset(net.ones[:, :], 1.0)
            nc.vector.memset(net.mean_w[:, :], 1.0 / D)
            nc.vector.memset(net.eps[:, :], EPS)
            dve.wait_ge(built, 2)
            nc.vector.tensor_copy(net.window0[:, :], it_i)
            dve.wait_ge(loaded_d, 32)
            nc.vector.tensor_copy(dst_f, dst_i).then_inc(step, 1)
            dve.wait_ge(step, 1)
            df = dst_f.rearrange("p (g e) -> p g e", g=GPH)
            nc.vector.tensor_reduce(least, df, AX_X, ALU.min)
            nc.vector.tensor_reduce(most, df, AX_X, ALU.max).then_inc(step, 1)
            dve.wait_ge(step, 2)
            nc.vector.tensor_copy(least_i, least).then_inc(step, 1)
            nc.vector.tensor_tensor(rel_f.rearrange("p (g e) -> p g e", g=GPH), df,
                                    least.unsqueeze(2).broadcast_to([GP, GPH, GE]),
                                    ALU.subtract).then_inc(step, 1)
            nc.vector.tensor_tensor(most, most, least, ALU.subtract).then_inc(step, 1)
            dve.wait_ge(step, 5)
            nc.vector.tensor_reduce(span, most, AX_X, ALU.max).then_inc(step, 1)
            dve.wait_ge(spread, 1)
            nc.vector.tensor_reduce(row[:, 0:1], net.psum[0:1, 0:GP], AX_X, ALU.max).then_inc(step, 1)
            dve.wait_ge(step, 7)
            nc.vector.tensor_scalar(row[:, 1:2], row[:, 0:1], 1.0 / W, 0.5 + 0.5 / W,
                                    ALU.mult, ALU.add).then_inc(step, 1)
            dve.wait_ge(step, 8)
            nc.vector.tensor_copy(net.rounds[:, :], row[:, 1:2])
            dve.wait_ge(loaded_s, 32)
            nc.vector.tensor_copy(src_f, src_i).then_inc(step, 1)
            for n, (_, to, _, g, k) in enumerate(tiles):
                dve.wait_ge(turned, n + 1)
                nc.vector.tensor_copy(to[:, :].rearrange("p (a t) -> p a t", t=HALF)[:, :, g * GT + k],
                                      net.psum[:, (n % 2 + 2) * 512:(n % 2 + 2) * 512 + GP]
                                      ).then_inc(copied, 1)

        @block.tensor
        def _(pe):
            pe.wait_ge(masked, 1)
            pe.wait_ge(step, 6)
            nc.tensor.transpose(net.psum[0:1, 0:GP], span, net.ident[0:GP, 0:GP]).then_inc(spread, 1)
            pe.wait_ge(step, 9)
            for n, (fr, _, deal, g, k) in enumerate(tiles):
                if n >= 2:
                    pe.wait_ge(copied, n - 1)
                group = fr[:, g * GE:(g + 1) * GE]
                tile = (group.rearrange("a (p k) -> a k p", k=GT)[:, k, :] if deal
                        else group[:, k * TILE:(k + 1) * TILE])
                nc.tensor.transpose(net.psum[:, (n % 2 + 2) * 512:(n % 2 + 2) * 512 + GP], tile,
                                    net.ident[0:GP, 0:GP]).then_inc(turned, 1)


def normalise(net, tag, first=False, keep=False, table=None):
    nc = net.nc
    A, B, Cc = net.A, net.B, net.C
    s = {k: net.sem(f"{tag}_{k}") for k in
         ("loaded", "x_brought", "x_turned", "x_ready", "brought", "mean", "centred", "squared", "var", "dev", "carried", "inverse", "h", "turned", "rows", "saved", "stored", "kept")}

    with nc.Block() as block:
        @block.sync
        def _(sp):
            if first:
                for k in range(5):
                    sp.dma_start(A[0:SUB, k * 20 * D:(k + 1) * 20 * D].rearrange("p (t f) -> p t f", f=D),
                                 net.dram["x"][k * 2500:(k + 1) * 2500, :]
                                 .rearrange("(t p) f -> p t f", p=SUB)).then_inc(s["loaded"], 16)
            else:
                sp.dma_start(A[:, 0:N], net.XT).then_inc(s["loaded"], 16)
            sp.wait_ge(s["x_ready"], NCH + (2 if first else 0))
            sp.dma_start(net.XT, B[:, 0:N]).then_inc(s["saved"], 16)
            if keep:
                sp.wait_ge(s["h"], NCH)
                sp.dma_start(net.HT, B[:, 0:N]).then_inc(s["kept"], 16)
            if table is not None:
                rows_store(net, sp, s, Cc, table)
            sp.wait_ge(s["saved"], 16)
            if keep:
                sp.wait_ge(s["kept"], 16)

        @block.tensor
        def _(pe):
            if first:
                def turn(c, k):
                    pe.wait_ge(s["x_brought"], c + 1)
                    pe.wait_ge(s["x_ready"], c + 1)
                    for j in range(4):
                        t = nc.tensor.transpose(
                            net.psum[:, k * 512 + j * SUB:k * 512 + (j + 1) * SUB],
                            net.work[0:SUB, k * 512 + j * D:k * 512 + (j + 1) * D],
                            net.ident[0:SUB, 0:SUB])
                    t.then_inc(s["x_turned"], 1)
                each_chunk(pe, turn)
            with pe.Fori(0, NCH) as c:
                pe.wait_ge(s["x_ready"], c + (3 if first else 1))
                pe.wait_ge(s["centred"], c + 1)
                nc.tensor.matmul(net.bank(2, c), net.mean_w[:, :], net.col(B, c),
                                 start=True, stop=True).then_inc(s["mean"], 1)
            with pe.Fori(0, NCH) as c:
                pe.wait_ge(s["squared"], c + 1)
                pe.wait_ge(s["dev"], c + 1)
                nc.tensor.matmul(net.bank(4, c), net.mean_w[:, :], net.col(A, c),
                                 start=True, stop=True).then_inc(s["var"], 1)
            if table is not None:
                rows_turn(net, pe, s, 6)

        @block.vector
        def _(dve):
            dve.sem_inc(s["centred"], 2)
            if not first:
                dve.wait_ge(s["loaded"], 16)
                with dve.Fori(0, NCH) as c:
                    nc.vector.tensor_tensor(net.col(B, c), net.col(A, c), net.col(B, c),
                                            ALU.add).then_inc(s["x_ready"], 1)
            with dve.Fori(0, NCH) as c:
                dve.wait_ge(s["mean"], c + 1)
                nc.vector.tensor_tensor(net.col(Cc, c), net.col(B, c), net.bank(2, c),
                                        ALU.subtract).then_inc(s["centred"], 1)
            dve.wait_ge(s["saved"], 16)
            with dve.Fori(0, NCH) as c:
                dve.wait_ge(s["dev"], c + 3)
                dve.sem_inc(s["carried"], 1)
                nc.vector.reciprocal(net.col(A, c), net.col(A, c)).then_inc(s["inverse"], 1)
                dve.wait_ge(s["inverse"], c + 1)
                nc.vector.scalar_tensor_tensor(out=net.col(B, c), in0=net.col(Cc, c), scalar=0.0,
                                               in1=net.col(A, c), op0=ALU.max,
                                               op1=ALU.mult).then_inc(s["h"], 1)

        @block.scalar
        def _(act):
            act.sem_inc(s["dev"], 2)
            if first:
                act.sem_inc(s["x_ready"], 2)
                with act.Fori(0, NCH) as c:
                    act.wait_ge(s["x_turned"], c + 3)
                    nc.scalar.copy(net.col(B, c), net.bank(0, c)).then_inc(s["x_ready"], 1)
            with act.Fori(0, NCH) as c:
                act.wait_ge(s["centred"], c + 3)
                nc.scalar.activation(net.col(A, c), net.col(Cc, c), ACT.Square).then_inc(s["squared"], 1)
            with act.Fori(0, NCH) as c:
                act.wait_ge(s["var"], c + 1)
                nc.scalar.activation(net.col(A, c), net.bank(4, c), ACT.Sqrt,
                                     bias=net.eps[:, 0:1]).then_inc(s["dev"], 1)
            if table is not None:
                act.wait_ge(s["h"], NCH)
                rows_copy(net, act, nc.scalar.copy, s, 6, Cc)

        if first or table is not None:
            @block.gpsimd
            def _(pool):
                if first:
                    pool.sem_inc(s["x_turned"], 2)
                    pool.wait_ge(s["loaded"], 80)

                    def bring(c, k):
                        pool.wait_ge(s["x_turned"], c + 1)
                        nc.gpsimd.tensor_copy(net.work[0:SUB, k * 512:(k + 1) * 512],
                                              A[0:SUB, bass.ds(c * 4 * D, 4 * D)]
                                              ).then_inc(s["x_brought"], 1)
                    each_chunk(pool, bring)
                    pool.wait_ge(s["x_turned"], NCH + 2)
                if table is not None:
                    rows_bring(net, pool, s, B, s["h"], 0)


def aggregate(net, tag, table=None, extra=None):
    nc = net.nc
    A, Cc = net.A, net.C
    attention, edges = extra == "attention", extra == "edges"
    width = XW if attention else D
    rows = [net.work[:, h * HALF * XW:h * HALF * XW + HALF * width] for h in range(2)]
    rows3 = [r.rearrange("p (t f) -> p t f", f=width) for r in rows]
    attr = [net.B[:, h * HALF * D:(h + 1) * HALF * D] for h in range(2)]
    at0 = EPP * H if attention else 2 * HALF * D
    msgs = [net.B[:, at0 + h * HALF * width:at0 + (h + 1) * HALF * width] for h in range(2)] if (
        attention or edges) else rows
    msgs3 = [m.rearrange("p (t f) -> p t f", f=width) for m in msgs]
    high = [P, H if attention else P]
    bank_of = lambda h, q, k: net.psum[0:high[k], (h * GPH + q) * 512 + k * W:(h * GPH + q) * 512 + (k + 1) * W]
    name = lambda k: [net.sem(f"{tag}_{k}{h}") for h in range(2)]
    index_ready, onehot_ready = name("index"), name("onehot")
    gathered = name("gathered") if attention else [net.pool_sem(), net.pool_sem()]
    summed = name("summed")
    message, attr_loaded, relued = name("message"), name("attr"), name("relued")
    added = net.sem(f"{tag}_added")
    lists = net.sem(f"{tag}_lists")
    cleared, moved = net.sem(f"{tag}_cleared"), net.sem(f"{tag}_moved")
    ready = relued if edges else message if attention else gathered

    with nc.Block() as block:
        if not attention:
            if edges:
                @block.scalar
                def _(act):
                    R = act.value_load(net.rounds[0:1, 0:1], min_val=1, max_val=256)
                    with act.Fori(0, R) as r:
                        with act.Fori(0, NIT) as i:
                            n = act.snap(r * NIT + i)
                            for h in range(2):
                                act.wait_ge(message[h], n + 2)
                                nc.scalar.activation(msgs[h], msgs[h], ACT.Relu).then_inc(relued[h], 1)

            @block.gpsimd
            def _(pool):
                if edges:
                    pool.wait_ge(lists, 32)
                R = pool.value_load(net.rounds[0:1, 0:1], min_val=1, max_val=256)
                with pool.Fori(0, R) as r:
                    with pool.Fori(0, NIT) as i:
                        n = pool.snap(r * NIT + i)
                        for h in range(2):
                            if edges:
                                pool.wait_ge(message[h], n + 1)
                            else:
                                pool.wait_ge(summed[h], n * GPH + GPH)
                            nc.gpsimd.tensor_copy(net.index[:, h, :],
                                                  net.src_n[:, bass.ds(i * 2 * HALF + h * HALF, HALF)]
                                                  ).then_inc(index_ready[h], 1)
                            pool.wait_ge(index_ready[h], n + 1)
                            pool.sem_inc(moved, 1)
                            for t in range(HALF):
                                pool.indirect_dma_start(
                                    rows3[h][:, t, :], None, table,
                                    bass.IndirectOffsetOnAxis(ap=net.index[:, h, t:t + 1], axis=0)
                                ).then_inc(gathered[h], 16)

        @block.sync
        def _(sp):
            if not (attention or edges):
                return
            if edges:
                sp.dma_start(net.src_n[:, :], net.DEALT[0]).then_inc(lists, 16)
                sp.dma_start(net.rel_n[:, :], net.DEALT[1]).then_inc(lists, 16)
                sp.wait_ge(cleared, 1)
            R = sp.value_load(net.rounds[0:1, 0:1], min_val=1, max_val=256)
            with sp.Fori(0, R) as r:
                with sp.Fori(0, NIT) as i:
                    n = sp.snap(r * NIT + i)
                    for h in range(2):
                        if attention:
                            sp.wait_ge(message[h], n + 1)
                            sp.dma_start(rows[h], net.G[bass.ds(i * 2 + h, 1), :, :]
                                         .rearrange("a p f -> (a p) f")).then_inc(gathered[h], 16)
                        else:
                            sp.wait_ge(summed[h], n * GPH + GPH)
                            lane = "(q p k) f -> p q (k f)"
                            slots = attr[h].rearrange("p (q f) -> p q f", q=GPH)
                            edge = net.dram["edge_attr_128"]
                            at = (2 * i + h) * HALF * TILE
                            sp.dma_start(slots[:, 0:2, :], edge[bass.ds(at, 2 * GE), :].rearrange(
                                lane, q=2, p=P)).then_inc(attr_loaded[h], 16)
                            if h == 0:
                                sp.dma_start(slots[:, 2:4, :], edge[bass.ds(at + 2 * GE, 2 * GE), :].rearrange(
                                    lane, q=2, p=P)).then_inc(attr_loaded[h], 16)
                                continue
                            with sp.If(i < NIT - 1):
                                more = nc.s_assert_within(at + 2 * GE, 0, E - 2 * GE)
                                sp.dma_start(slots[:, 2:4, :], edge[bass.ds(more, 2 * GE), :].rearrange(
                                    lane, q=2, p=P)).then_inc(attr_loaded[h], 16)
                            with sp.Else():
                                rest = E - (NGRP - 2) * GE
                                sp.dma_start(slots[0:rest // GT, 2, :], edge[E - rest:E, :].rearrange(
                                    "(p k) f -> p (k f)", k=GT)).then_inc(attr_loaded[h], 16)

        @block.tensor
        def _(pe):
            for h in range(2):
                pe.sem_inc(summed[h], GPH)
            R = pe.value_load(net.rounds[0:1, 0:1], min_val=1, max_val=256)
            with pe.Fori(0, R) as r:
                with pe.Fori(0, NIT) as i:
                    n = pe.snap(r * NIT + i)
                    for h in range(2):
                        pe.wait_ge(onehot_ready[h], n + 1)
                        if ready is gathered:
                            pe.wait_ge(gathered[h], n * 256 + 256)
                        else:
                            pe.wait_ge(ready[h], n + (2 if ready is message else 1))
                        for q in range(GPH):
                            pe.wait_ge(added, n * 2 * GPH + h * GPH + q + 1)
                            for k in range(GT):
                                t = q * GT + k
                                last = nc.tensor.matmul(bank_of(h, q, 0),
                                                        msgs3[h][:, t, 0:D], net.onehot[:, h, t, :],
                                                        start=(k == 0), stop=(k == GT - 1))
                            if extra:
                                for k in range(GT):
                                    t = q * GT + k
                                    if extra == "count":
                                        lhs = net.ones[:, :]
                                    elif edges:
                                        lhs = attr[h][:, t * D:(t + 1) * D]
                                    else:
                                        lhs = msgs3[h][:, t, D:D + H]
                                    last = nc.tensor.matmul(bank_of(h, q, 1),
                                                            lhs, net.onehot[:, h, t, :],
                                                            start=(k == 0), stop=(k == GT - 1))
                            last.then_inc(summed[h], 1)

        @block.vector
        def _(dve):
            if not attention:
                nc.vector.memset(A[:, :], 0.0)
                if extra:
                    nc.vector.memset(Cc[:, 0:REG], 1.0 if extra == "count" else 0.0)
            if edges:
                nc.vector.memset(net.B[:, 0:2 * HALF * D], 0.0)
            nc.vector.tensor_copy(net.window[:, :], net.window0[:, :])
            nc.vector.tensor_copy(net.base_now[:, :], net.base[:, :]).then_inc(cleared, 1)
            dve.wait_ge(cleared, 1)
            if edges:
                dve.wait_ge(lists, 32)
            dve.sem_inc(added, 2 * GPH)
            if attention or edges:
                for h in range(2):
                    dve.sem_inc(message[h], 1)
            R = dve.value_load(net.rounds[0:1, 0:1], min_val=1, max_val=256)
            with dve.Fori(0, R) as r:
                def compare(i, h):
                    dve.wait_ge(summed[h], (r * NIT + i) * GPH + GPH)
                    nc.vector.tensor_tensor(
                        net.onehot[:, h, :, :],
                        net.rel_n[:, bass.ds(i * 2 * HALF + h * HALF, HALF)].unsqueeze(2)
                        .broadcast_to([P, HALF, W]),
                        net.window[:, :].unsqueeze(1).broadcast_to([P, HALF, W]),
                        ALU.is_equal).then_inc(onehot_ready[h], 1)

                def messages(i, h):
                    n = r * NIT + i
                    if attention:
                        dve.wait_ge(gathered[h], n * 16 + 16)
                        pr3 = net.B[:, bass.ds(i * 2 * HALF * H, 2 * HALF * H)].rearrange(
                            "p (h t) -> p t h", h=H)[:, h * HALF:(h + 1) * HALF, :]
                        by_head = lambda x: x[:, :, 0:D].rearrange("p t (h c) -> p t h c", h=H)
                        nc.vector.tensor_copy(msgs3[h][:, :, D:D + H], pr3)
                        nc.vector.tensor_tensor(by_head(msgs3[h]), by_head(rows3[h]),
                                                pr3.unsqueeze(3).broadcast_to([P, HALF, H, C]),
                                                ALU.mult).then_inc(message[h], 1)
                    elif edges:
                        dve.wait_ge(gathered[h], n * 256 + 256)
                        dve.wait_ge(attr_loaded[h], n * 32 + 32)
                        nc.vector.tensor_tensor(msgs[h], rows[h], attr[h], ALU.add).then_inc(message[h], 1)

                def add(i, h):
                    n = r * NIT + i
                    for q in range(GPH):
                        at = dve.value_load(net.base_now[0:1, bass.ds(i * 2 * GPH + h * GPH + q, 1)],
                                            min_val=0, max_val=N)
                        dve.wait_ge(summed[h], n * GPH + GPH + q + 1)
                        dve.wait_ge(added, n * 2 * GPH + 2 * GPH + h * GPH + q)
                        if extra:
                            nc.vector.tensor_tensor(Cc[0:high[1], bass.ds(at, W)], Cc[0:high[1], bass.ds(at, W)],
                                                    bank_of(h, q, 1),
                                                    ALU.add)
                        nc.vector.tensor_tensor(A[:, bass.ds(at, W)], A[:, bass.ds(at, W)],
                                                bank_of(h, q, 0), ALU.add
                                                ).then_inc(added, 1)

                for h in range(2):
                    compare(0, h)
                    messages(0, h)
                with dve.Fori(0, NIT - 1) as i:
                    for h in range(2):
                        add(i, h)
                        compare(dve.snap(i + 1), h)
                        messages(dve.snap(i + 1), h)
                for h in range(2):
                    add(NIT - 1, h)
                nc.vector.tensor_scalar(net.window[:, :], net.window[:, :], float(W), None, ALU.add)
                nc.vector.tensor_scalar(net.base_now[:, :], net.base_now[:, :], float(W), float(N),
                                        ALU.add, ALU.min).then_inc(cleared, 1)
                dve.wait_ge(cleared, r + 2)


def sage(net, tag, weight, bias, table=None, invert=False):
    nc = net.nc
    A, B, Cc = net.A, net.B, net.C
    w = net.wtmp[:, 0:2 * D]
    b = net.small[:, 0:1]
    s = {k: net.sem(f"{tag}_{k}") for k in
         ("weights", "inverse", "mean", "product", "h", "brought", "turned", "rows", "stored")}

    with nc.Block() as block:
        @block.sync
        def _(sp):
            sp.dma_start(w.rearrange("p (k n) -> p k n", k=2),
                         net.dram[weight].rearrange("(k p) n -> p k n", k=2)).then_inc(s["weights"], 16)
            sp.dma_start(b, net.dram[bias].rearrange("(p a) -> p a", a=1)).then_inc(s["weights"], 16)
            if table is not None:
                rows_store(net, sp, s, A, table)

        @block.vector
        def _(dve):
            if invert:
                nc.vector.reciprocal(Cc[:, 0:N], Cc[:, 0:N]).then_inc(s["inverse"], 1)
                dve.wait_ge(s["inverse"], 1)
            with dve.Fori(0, NCH) as c:
                nc.vector.tensor_tensor(net.col(A, c), net.col(A, c), net.col(Cc, c),
                                        ALU.mult).then_inc(s["mean"], 1)
            if table is not None:
                rows_copy(net, dve, nc.vector.tensor_copy, s, 2, A)

        @block.tensor
        def _(pe):
            pe.wait_ge(s["weights"], 32)
            with pe.Fori(0, NCH) as c:
                pe.wait_ge(s["h"], c + 1)
                nc.tensor.matmul(net.bank(0, c), w[:, 0:D], net.col(B, c), start=True, stop=False)
                pe.wait_ge(s["mean"], c + 1)
                nc.tensor.matmul(net.bank(0, c), w[:, D:2 * D], net.col(A, c),
                                 start=False, stop=True).then_inc(s["product"], 1)
            if table is not None:
                rows_turn(net, pe, s, 2)

        if table is not None:
            @block.gpsimd
            def _(pool):
                rows_bring(net, pool, s, B, s["h"], 2)

        @block.scalar
        def _(act):
            act.sem_inc(s["h"], 2)
            act.wait_ge(s["weights"], 32)
            with act.Fori(0, NCH) as c:
                act.wait_ge(s["product"], c + 1)
                nc.scalar.activation(net.col(B, c), net.bank(0, c), ACT.Relu,
                                     bias=b).then_inc(s["h"], 1)


def segment_ends(net):
    nc = net.nc
    part = N // 5
    row = net.work[0:1, 0:part]
    scanned, stored = net.sem("ends_scanned"), net.sem("ends_stored")
    last = net.small[0:1, 20:21]

    with nc.Block() as block:
        @block.sync
        def _(sp):
            for k in range(5):
                sp.wait_ge(scanned, 2 * k + 1)
                sp.dma_start(net.CUM[0:1, k * part:(k + 1) * part], row).then_inc(stored, 16)
            sp.dma_start(net.CUM[1:2, :], net.C[0:1, 0:N]).then_inc(stored, 16)
            sp.wait_ge(stored, 96)

        @block.vector
        def _(dve):
            for k in range(5):
                if k:
                    dve.wait_ge(stored, 16 * k)
                    dve.wait_ge(scanned, 2 * k)
                nc.vector.tensor_tensor_scan(
                    row, net.C[0:1, k * part:(k + 1) * part],
                    net.ones[0:1, 0:1].broadcast_to([1, part]), last if k else 0.0,
                    ALU.add, ALU.subtract).then_inc(scanned, 1)
                dve.wait_ge(scanned, 2 * k + 1)
                nc.vector.tensor_copy(last, row[:, part - 1:part]).then_inc(scanned, 1)


def gat_project(net):
    nc = net.nc
    A, B, Cc = net.A, net.B, net.C
    w = net.wtmp[:, 0:XW]
    wt = net.wtmp[:, 144:144 + D]
    att = net.wtmp[:, 512:512 + 2 * H]
    mask = net.wtmp[:, 520:520 + H]
    gain, bias = net.small[:, 0:1], net.small[:, 1:2]
    a_s, a_d = net.small[:, 2:3], net.small[:, 3:4]
    s = {k: net.sem(f"gp_{k}") for k in
         ("weights", "masked", "w_turned", "w_ready", "att_done", "select", "joined", "mean", "centred", "squared",
          "var", "dev", "carried", "inverse", "scaled", "normed", "brought", "used", "rows", "stored", "kept")}

    with nc.Block() as block:
        @block.sync
        def _(sp):
            sp.dma_start(w[:, 0:D], net.dram["L1_gnn_W"]).then_inc(s["weights"], 16)
            for to, name in ((gain, "L1_gnn_ln1_g"), (bias, "L1_gnn_ln1_b")):
                sp.dma_start(to, net.dram[name].rearrange("(p a) -> p a", a=1)).then_inc(s["weights"], 16)
            for to, name in ((a_s, "L1_gnn_att_src"), (a_d, "L1_gnn_att_dst")):
                sp.dma_start(to, net.dram[name].rearrange("h (c a) -> (h c) a", a=1)).then_inc(s["weights"], 16)
            rows_store(net, sp, s, Cc, net.XH, XW)

        @block.tensor
        def _(pe):
            pe.wait_ge(s["weights"], 80)
            nc.tensor.transpose(net.psum[:, 0:D], w[:, 0:D], net.ident[:, :]).then_inc(s["w_turned"], 1)
            pe.wait_ge(s["masked"], 1 + H)
            nc.tensor.transpose(net.psum[0:H, 1024:1024 + D], mask, net.ident[:, :]).then_inc(s["select"], 1)
            pe.wait_ge(s["w_ready"], 1)
            nc.tensor.matmul(net.psum[:, 512:512 + 2 * H], wt, att, start=True, stop=True
                             ).then_inc(s["att_done"], 1)
            pe.wait_ge(s["joined"], 1)
            with pe.Fori(0, NCH) as c:
                pe.wait_ge(s["centred"], c + 1)
                nc.tensor.matmul(net.bank(2, c), net.mean_w[:, :], net.col(B, c),
                                 start=True, stop=True).then_inc(s["mean"], 1)
            with pe.Fori(0, NCH) as c:
                pe.wait_ge(s["squared"], c + 1)
                pe.wait_ge(s["dev"], c + 1)
                nc.tensor.matmul(net.bank(4, c), net.mean_w[:, :], net.col(A, c),
                                 start=True, stop=True).then_inc(s["var"], 1)

            def project(c, k):
                pe.wait_ge(s["brought"], c + 1)
                pe.wait_ge(s["rows"], c + 1)
                for j in range(4):
                    m = nc.tensor.matmul(
                        net.psum[0:SUB, (2 * k + j // 2) * 512 + j % 2 * XW:(2 * k + j // 2) * 512 + (j % 2 + 1) * XW],
                        net.work[:, k * 512 + j * SUB:k * 512 + (j + 1) * SUB], w, start=True, stop=True)
                m.then_inc(s["used"], 1)
            pe.wait_ge(s["centred"], NCH + 2)
            each_chunk(pe, project)

        @block.vector
        def _(dve):
            nc.vector.memset(mask, 0.0).then_inc(s["masked"], 1)
            dve.wait_ge(s["masked"], 1)
            for h in range(H):
                nc.vector.memset(mask[h * C:(h + 1) * C, h:h + 1], 1.0).then_inc(s["masked"], 1)
            dve.wait_ge(s["masked"], 1 + H)
            dve.wait_ge(s["weights"], 80)
            nc.vector.tensor_scalar(att[:, 0:H], mask, a_s, None, ALU.mult)
            nc.vector.tensor_scalar(att[:, H:2 * H], mask, a_d, None, ALU.mult)
            dve.wait_ge(s["w_turned"], 1)
            nc.vector.tensor_copy(wt, net.psum[:, 0:D]).then_inc(s["w_ready"], 1)
            dve.wait_ge(s["select"], 1)
            nc.vector.tensor_copy(head_select(net), net.psum[0:H, 1024:1024 + D])
            dve.wait_ge(s["att_done"], 1)
            nc.vector.tensor_copy(w[:, D:XW], net.psum[:, 512:512 + 2 * H]).then_inc(s["joined"], 1)
            dve.sem_inc(s["centred"], 2)
            with dve.Fori(0, NCH) as c:
                dve.wait_ge(s["mean"], c + 1)
                nc.vector.tensor_tensor(net.col(Cc, c), net.col(B, c), net.bank(2, c),
                                        ALU.subtract).then_inc(s["centred"], 1)
            with dve.Fori(0, NCH) as c:
                dve.wait_ge(s["dev"], c + 3)
                dve.sem_inc(s["carried"], 1)
                nc.vector.reciprocal(net.col(A, c), net.col(A, c)).then_inc(s["inverse"], 1)
                dve.wait_ge(s["inverse"], c + 1)
                nc.vector.tensor_tensor(net.col(A, c), net.col(Cc, c), net.col(A, c),
                                        ALU.mult).then_inc(s["scaled"], 1)
            dve.sem_inc(s["rows"], 2)

            def out(c, k):
                dve.wait_ge(s["used"], c + 3)
                nc.vector.tensor_copy(
                    Cc[0:SUB, bass.ds(c * 4 * XW, 4 * XW)].rearrange("p (b f) -> p b f", b=2),
                    net.psum[0:SUB, 2 * k * 512:(2 * k + 2) * 512].rearrange("p (b f) -> p b f", b=2)[:, :, 0:2 * XW]
                    ).then_inc(s["rows"], 1)
            each_chunk(dve, out)
            dve.wait_ge(s["rows"], NCH + 2)
            nc.vector.tensor_copy(
                net.onehot[0:SUB, :, :, :].rearrange("p a t w -> p (a t w)")[:, 0:NSUB * 2 * H]
                .rearrange("p (t f) -> p t f", f=2 * H),
                Cc[0:SUB, :].rearrange("p (t f) -> p t f", f=XW)[:, :, D:XW]).then_inc(s["kept"], 1)

        @block.scalar
        def _(act):
            act.sem_inc(s["dev"], 2)
            with act.Fori(0, NCH) as c:
                act.wait_ge(s["centred"], c + 3)
                nc.scalar.activation(net.col(A, c), net.col(Cc, c), ACT.Square).then_inc(s["squared"], 1)
            with act.Fori(0, NCH) as c:
                act.wait_ge(s["var"], c + 1)
                nc.scalar.activation(net.col(A, c), net.bank(4, c), ACT.Sqrt,
                                     bias=net.eps[:, 0:1]).then_inc(s["dev"], 1)
            act.wait_ge(s["weights"], 80)
            with act.Fori(0, NCH) as c:
                act.wait_ge(s["scaled"], c + 1)
                nc.scalar.activation(net.col(A, c), net.col(A, c), ACT.Identity,
                                     bias=bias, scale=gain).then_inc(s["normed"], 1)

        @block.gpsimd
        def _(pool):
            pool.sem_inc(s["used"], 2)

            def bring(c, k):
                pool.wait_ge(s["normed"], c + 1)
                pool.wait_ge(s["used"], c + 1)
                nc.gpsimd.tensor_copy(slot(net, k), net.col(A, c)).then_inc(s["brought"], 1)
            each_chunk(pool, bring)


def gat_gather(net):
    nc = net.nc
    rows = [net.work[:, h * HALF * XW:(h + 1) * HALF * XW] for h in range(2)]
    rows3 = [r.rearrange("p (t f) -> p t f", f=XW) for r in rows]
    name = lambda k: [net.sem(f"gg_{k}{h}") for h in range(2)]
    index_ready, stored, free, copied = name("index"), name("stored"), name("free"), name("copied")
    gathered = [net.pool_sem(), net.pool_sem()]
    moved = net.sem("gg_moved")

    with nc.Block() as block:
        @block.gpsimd
        def _(pool):
            with pool.Fori(0, NIT) as i:
                for h in range(2):
                    pool.wait_ge(free[h], i + 1)
                    pool.wait_ge(copied[h], i + 1)
                    nc.gpsimd.tensor_copy(net.index[:, h, :],
                                          net.src_n[:, bass.ds(i * 2 * HALF + h * HALF, HALF)]
                                          ).then_inc(index_ready[h], 1)
                    pool.wait_ge(index_ready[h], i + 1)
                    pool.sem_inc(moved, 1)
                    for t in range(HALF):
                        pool.indirect_dma_start(
                            rows3[h][:, t, :], None, net.XH,
                            bass.IndirectOffsetOnAxis(ap=net.index[:, h, t:t + 1], axis=0)
                        ).then_inc(gathered[h], 16)

        @block.sync
        def _(sp):
            for h in range(2):
                sp.sem_inc(free[h], 1)
            with sp.Fori(0, NIT) as i:
                for h in range(2):
                    sp.wait_ge(gathered[h], i * 256 + 256)
                    sp.dma_start(net.G[bass.ds(i * 2 + h, 1), :, :].rearrange("a p f -> (a p) f"),
                                 rows[h]).then_inc(stored[h], 16)
                    sp.wait_ge(stored[h], i * 16 + 16)
                    sp.sem_inc(free[h], 1)

        @block.scalar
        def _(act):
            for h in range(2):
                act.sem_inc(copied[h], 1)
            with act.Fori(0, NIT) as i:
                for h in range(2):
                    act.wait_ge(gathered[h], i * 256 + 256)
                    nc.scalar.copy(
                        net.B[:, bass.ds(i * 2 * HALF * H, 2 * HALF * H)].rearrange(
                            "p (h t) -> p h t", h=H)[:, :, h * HALF:(h + 1) * HALF],
                        rows3[h][:, :, D:D + H].rearrange("p t h -> p h t")).then_inc(copied[h], 1)


def gat_softmax(net):
    nc = net.nc
    B, Cc = net.B, net.C
    SEG = 4 * EPP
    turned_rows = Cc[:, 0:SEG]
    score = Cc[:, SEG:2 * SEG].rearrange("p (h k) -> p h k", h=H)
    trial = Cc[:, 0:SEG].rearrange("p (h k) -> p h k", h=H)
    running = Cc[:, 0:SEG].rearrange("p (k h) -> p k h", h=H)
    dst = net.work[:, 1024:1024 + EPP]
    flag = net.work[:, 1024 + EPP:1024 + 2 * EPP]
    scratch = net.onehot[:, :, :, :].rearrange("p a t w -> p (a t w)")
    a_own = scratch[0:SUB, 0:NSUB * 2 * H].rearrange("p (t f) -> p t f", f=2 * H)
    ends3 = scratch[0:H, 800:800 + 3 * P]
    e_first, e_last, e_max = (ends3[:, k * P:(k + 1) * P] for k in range(3))
    before, value = scratch[0:H, 1184:1184 + P], scratch[0:H, 1312:1312 + P]
    joins, single = scratch[0:H, 1440:1440 + P - 1], scratch[0:H, 1568:1568 + P - 1]
    carry_row = scratch[0:H, 1696:1696 + P]
    first4, last4, max4 = (net.small[:, 24 + 4 * k:28 + 4 * k] for k in range(3))
    carry = net.small[:, 36:40]
    fix_i = net.small[:, 40:41].bitcast(I32)
    fix = net.small[:, 48:56]
    at = [Cc[0:SUB, k * NSUB:(k + 1) * NSUB] for k in range(8)]
    ends, counts, some, node, pos = at[0], at[1], at[2], at[3], at[4]
    last_i, start_i, node_i = (at[k].bitcast(I32) for k in (5, 6, 7))
    four = lambda k: Cc[0:SUB, 800 + k * 400:1200 + k * 400].rearrange("p (t h) -> p t h", h=H)
    found, peak, own = four(0), four(1), four(2)
    values = Cc[0:SUB, 2000:2800].rearrange("p (t f) -> p t f", f=2 * H)
    wide = lambda a: a.unsqueeze(2).broadcast_to([SUB, NSUB, H])
    BATCH = 10
    idx10 = net.small[0:SUB, 60:60 + BATCH].bitcast(I32)
    got10 = net.small[0:SUB, 72:72 + BATCH * H]
    put10 = net.work[0:SUB, 0:BATCH * 2 * H]
    p_self = net.p_self[:, :].rearrange("p (t h) -> p t h", h=H)

    s = {k: net.sem(f"gs_{k}") for k in
         ("brought", "turned", "copied", "by_head", "loaded", "dve", "ends", "carried", "stored",
          "positions", "index", "go", "kept", "values", "put_ready", "fix_ready",
          "starts", "exps", "exps_stored", "rows_loaded", "brought2", "turned2", "copied2")}
    s.update(found=net.pool_sem(), put=net.pool_sem(), fixed=net.pool_sem())
    v = [0]

    with nc.Block() as block:
        @block.gpsimd
        def _(pool):
            pool.iota(node_like(net), pattern=[[SUB, NSUB]], base=0, channel_multiplier=1).then_inc(s["go"], 1)
            pool.sem_inc(s["turned"], 2)

            def bring(c, k):
                pool.wait_ge(s["turned"], c + 1)
                nc.gpsimd.tensor_copy(slot(net, k, P), B[:, bass.ds(c * P, P)]).then_inc(s["brought"], 1)
            each_chunk(pool, bring, NIT)
            pool.wait_ge(s["positions"], 1)
            pool.wait_ge(s["stored"], 16)
            with pool.Fori(0, NSUB // BATCH) as i:
                pool.wait_ge(s["kept"], i + 1)
                nc.gpsimd.tensor_copy(idx10, last_i[:, bass.ds(i * BATCH, BATCH)]).then_inc(s["index"], 1)
                pool.wait_ge(s["index"], i + 1)
                pool.sem_inc(s["go"], 1)
                for t in range(BATCH):
                    pool.indirect_dma_start(
                        got10[:, t * H:(t + 1) * H], None, net.FD,
                        bass.IndirectOffsetOnAxis(ap=idx10[:, t:t + 1], axis=0)).then_inc(s["found"], 16)
            pool.wait_ge(s["kept"], NSUB // BATCH + 1)
            with pool.Fori(0, NSUB // BATCH) as i:
                nc.gpsimd.tensor_copy(idx10, start_i[:, bass.ds(i * BATCH, BATCH)]).then_inc(s["index"], 1)
                pool.wait_ge(s["index"], i + 1 + NSUB // BATCH)
                pool.wait_ge(s["put_ready"], i + 1)
                pool.sem_inc(s["go"], 1)
                for t in range(BATCH):
                    pool.indirect_dma_start(
                        net.SC, bass.IndirectOffsetOnAxis(ap=idx10[:, t:t + 1], axis=0),
                        put10[:, t * 2 * H:(t + 1) * 2 * H], None).then_inc(s["put"], 16)
                pool.wait_ge(s["put"], i * 16 * BATCH + 16 * BATCH)
            pool.wait_ge(s["values"], 16)
            pool.wait_ge(s["fix_ready"], 1)
            pool.indirect_dma_start(fix, None, net.NV, bass.IndirectOffsetOnAxis(ap=fix_i, axis=0)
                                    ).then_inc(s["fixed"], 16)
            pool.sem_inc(s["turned2"], 2)
            pool.wait_ge(s["rows_loaded"], 16 * H)

            def back(c, k):
                pool.wait_ge(s["turned2"], c + 1)
                nc.gpsimd.tensor_copy(slot(net, k, P), turned_rows[:, bass.ds(c * P, P)]
                                      ).then_inc(s["brought2"], 1)
            each_chunk(pool, back, NIT)

        @block.tensor
        def _(pe):
            def turn(c, k):
                pe.wait_ge(s["brought"], c + 1)
                pe.wait_ge(s["copied"], c + 1)
                nc.tensor.transpose(net.psum[:, k * 512:k * 512 + P], slot(net, k, P),
                                    net.ident[:, :]).then_inc(s["turned"], 1)
            each_chunk(pe, turn, NIT)
            pe.wait_ge(s["ends"], 1)
            for k, x in enumerate((first4, last4, max4)):
                t = nc.tensor.transpose(net.psum[0:H, 1024 + k * P:1024 + (k + 1) * P], x, net.ident[:, :])
            t.then_inc(s["carried"], 1)
            pe.wait_ge(s["ends"], 2)
            nc.tensor.transpose(net.psum[:, 1536:1536 + H], carry_row, net.ident[0:H, 0:H]
                                ).then_inc(s["carried"], 1)

            def turn2(c, k):
                pe.wait_ge(s["brought2"], c + 1)
                pe.wait_ge(s["copied2"], c + 1)
                nc.tensor.transpose(net.psum[:, k * 512:k * 512 + P], slot(net, k, P),
                                    net.ident[:, :]).then_inc(s["turned2"], 1)
            each_chunk(pe, turn2, NIT)

        @block.scalar
        def _(act):
            act.sem_inc(s["copied"], 2)

            def out(c, k):
                act.wait_ge(s["turned"], c + 3)
                nc.scalar.copy(turned_rows[:, bass.ds(c * P, P)], net.psum[:, k * 512:k * 512 + P]
                               ).then_inc(s["copied"], 1)
            each_chunk(act, out, NIT)
            act.sem_inc(s["copied2"], 2)
            act.wait_ge(s["fixed"], 16)

            def out2(c, k):
                act.wait_ge(s["turned2"], c + 3)
                nc.scalar.copy(B[:, bass.ds(c * P, P)], net.psum[:, k * 512:k * 512 + P]
                               ).then_inc(s["copied2"], 1)
            act.wait_ge(s["exps"], 2)
            nc.scalar.activation(p_self, own, ACT.Exp).then_inc(s["exps"], 1)
            nc.scalar.activation(Cc[:, SEG:2 * SEG], Cc[:, SEG:2 * SEG], ACT.Exp).then_inc(s["exps"], 1)
            each_chunk(act, out2, NIT)

        @block.sync
        def _(sp):
            sp.wait_ge(s["copied"], NIT + 2)
            for h in range(H):
                sp.dma_start(net.SH[h, :].rearrange("(b t e) -> t b e", t=2 * HALF, e=TILE),
                             turned_rows[h * 2 * HALF:(h + 1) * 2 * HALF, :]
                             .rearrange("t (b e) -> t b e", e=TILE)).then_inc(s["by_head"], 16)
            sp.dma_start(dst, net.DST.rearrange("(p k) -> p k", p=P)).then_inc(s["loaded"], 16)
            sp.wait_ge(s["by_head"], 16 * H)
            sp.dma_start(score, net.SH.rearrange("h (p k) -> p h k", p=P)).then_inc(s["loaded"], 16)
            sp.wait_ge(s["ends"], 3)
            sp.dma_start(net.FD.rearrange("(p k) h -> p (k h)", p=P), Cc[:, 0:SEG]).then_inc(s["stored"], 16)
            sp.wait_ge(s["stored"], 16)
            with nc.allow_non_contiguous_dma(reason="one node per element"):
                for k, x in enumerate((ends, counts)):
                    sp.dma_start(x, net.CUM[k, :].rearrange("(t p) -> p t", p=SUB),
                                 allow_slow_non_contiguous=True).then_inc(s["loaded"], 16)
            sp.wait_ge(s["ends"], 4)
            sp.dma_start(net.NV.rearrange("(t p) f -> p t f", p=SUB), values).then_inc(s["values"], 16)
            sp.wait_ge(s["put"], 16 * NSUB)
            sp.dma_start(B[:, 0:EPP * 2 * H], net.SC[0:EP, :].rearrange("(p k) f -> p (k f)", p=P)
                         ).then_inc(s["starts"], 16)
            sp.wait_ge(s["exps"], 4)
            sp.dma_start(net.PH.rearrange("h (p k) -> p h k", p=P), score).then_inc(s["exps_stored"], 16)
            sp.wait_ge(s["exps_stored"], 16)
            for h in range(H):
                sp.dma_start(turned_rows[h * 2 * HALF:(h + 1) * 2 * HALF, :].rearrange("t (b e) -> t b e", e=TILE),
                             net.PH[h, :].rearrange("(b t e) -> t b e", t=2 * HALF, e=TILE)
                             ).then_inc(s["rows_loaded"], 16)

        @block.vector
        def _(dve):
            def done(ins):
                v[0] += 1
                ins.then_inc(s["dve"], 1)
                dve.wait_ge(s["dve"], v[0])

            V = nc.vector
            dve.wait_ge(s["loaded"], 32)
            done(V.tensor_tensor(flag[:, 1:], dst[:, 1:], dst[:, 0:EPP - 1], ALU.is_equal))
            done(V.tensor_scalar(flag[:, 1:], flag[:, 1:], -1.0, BIG, ALU.add, ALU.mult))
            done(V.memset(flag[:, 0:1], 0.0))
            for h in range(H):
                done(V.tensor_tensor_scan(trial[:, h, :], flag, score[:, h, :], -BIG, ALU.add, ALU.max))
            done(V.tensor_copy(first4, dst[:, 0:1].broadcast_to([P, H])))
            done(V.tensor_copy(last4, dst[:, EPP - 1:EPP].broadcast_to([P, H])))
            V.tensor_copy(max4, trial[:, :, EPP - 1]).then_inc(s["ends"], 1)
            dve.wait_ge(s["carried"], 1)
            done(V.tensor_copy(ends3, net.psum[0:H, 1024:1024 + 3 * P]))
            done(V.memset(before, -BIG))
            done(V.memset(value, -BIG))
            for out, a in ((joins, e_first[:, 1:]), (single, e_first[:, 0:P - 1])):
                done(V.tensor_tensor(out, a, e_last[:, 0:P - 1], ALU.is_equal))
                done(V.tensor_scalar(out, out, -1.0, BIG, ALU.add, ALU.mult))
            done(V.tensor_tensor(before[:, 1:], joins, single, ALU.add))
            done(V.tensor_tensor(value[:, 1:], joins, e_max[:, 0:P - 1], ALU.add))
            V.tensor_tensor_scan(carry_row, before, value, -BIG, ALU.add, ALU.max).then_inc(s["ends"], 1)
            dve.wait_ge(s["carried"], 2)
            done(V.tensor_copy(carry, net.psum[:, 1536:1536 + H]))
            for h in range(H):
                done(V.tensor_tensor_scan(running[:, :, h], flag, score[:, h, :], carry[:, h:h + 1],
                                          ALU.add, ALU.max))
            dve.sem_inc(s["ends"], 1)
            dve.wait_ge(s["loaded"], 64)
            done(V.tensor_scalar(counts, counts, -1.0, None, ALU.add))
            done(V.tensor_scalar(pos, ends, -1.0, 0.0, ALU.add, ALU.max))
            done(V.tensor_copy(last_i, pos))
            done(V.tensor_scalar(some, counts, 0.0, None, ALU.is_gt))
            done(V.tensor_tensor(ends, ends, counts, ALU.subtract))
            done(V.tensor_copy(node, node_like(net)))
            done(V.tensor_scalar(node, node, float(EP), None, ALU.add))
            done(V.tensor_tensor(ends, ends, node, ALU.subtract))
            done(V.tensor_tensor(ends, ends, some, ALU.mult))
            done(V.tensor_tensor(ends, ends, node, ALU.add))
            done(V.tensor_copy(start_i, ends))
            dve.sem_inc(s["positions"], 1)
            dve.sem_inc(s["kept"], 1)
            with dve.Fori(0, NSUB // BATCH) as i:
                dve.wait_ge(s["found"], i * 16 * BATCH + 16 * BATCH)
                V.tensor_copy(Cc[0:SUB, bass.ds(i * BATCH * H + 800, BATCH * H)], got10).then_inc(s["kept"], 1)
            dve.wait_ge(s["kept"], NSUB // BATCH + 1)
            a_src, a_dst = a_own[:, :, 0:H], a_own[:, :, H:2 * H]
            done(V.tensor_tensor(found, found, wide(some), ALU.mult))
            done(V.tensor_scalar(some, some, -1.0, BIG, ALU.add, ALU.mult))
            done(V.tensor_tensor(found, found, wide(some), ALU.add))
            done(V.tensor_tensor(found, found, a_src, ALU.max))
            done(V.tensor_tensor(found, found, a_dst, ALU.add))
            done(V.scalar_tensor_tensor(out=peak, in0=found, scalar=0.2, in1=found, op0=ALU.mult, op1=ALU.max))
            done(V.tensor_tensor(own, a_src, a_dst, ALU.add))
            done(V.scalar_tensor_tensor(out=own, in0=own, scalar=0.2, in1=own, op0=ALU.mult, op1=ALU.max))
            done(V.tensor_tensor(own, own, peak, ALU.subtract))
            done(V.tensor_copy(values[:, :, 0:H], a_dst))
            done(V.tensor_copy(values[:, :, H:2 * H], peak))
            dve.sem_inc(s["ends"], 1)
            dve.sem_inc(s["exps"], 1)
            with dve.Fori(0, NSUB // BATCH) as i:
                dve.wait_ge(s["put"], i * 16 * BATCH) if False else None
                dve.wait_ge(s["index"], i + 1 + NSUB // BATCH)
                V.tensor_copy(put10, Cc[0:SUB, bass.ds(i * BATCH * 2 * H + 2000, BATCH * 2 * H)]
                              ).then_inc(s["put_ready"], 1)
            done(V.tensor_copy(fix_i, dst[:, 0:1]))
            dve.sem_inc(s["fix_ready"], 1)
            done(V.tensor_tensor(flag[:, 1:], dst[:, 1:], dst[:, 0:EPP - 1], ALU.is_equal))
            spread = B[:, 0:EPP * 2 * H].rearrange("p (k f) -> p k f", f=2 * H)
            dve.wait_ge(s["starts"], 16)
            dve.wait_ge(s["fixed"], 16)
            done(V.tensor_copy(spread[:, 0, :], fix))
            for f in range(2 * H):
                done(V.tensor_tensor_scan(spread[:, :, f], flag, spread[:, :, f], 0.0, ALU.mult, ALU.add))
            sp_dst = spread[:, :, 0:H].rearrange("p k h -> p h k")
            sp_max = spread[:, :, H:2 * H].rearrange("p k h -> p h k")
            done(V.tensor_tensor(score, score, sp_dst, ALU.add))
            done(V.scalar_tensor_tensor(out=score, in0=score, scalar=0.2, in1=score, op0=ALU.mult, op1=ALU.max))
            done(V.tensor_tensor(score, score, sp_max, ALU.subtract))
            done(V.tensor_scalar(score, score, 0.0, None, ALU.min))
            dve.sem_inc(s["exps"], 1)


def node_like(net):
    return net.wtmp[0:SUB, 700:700 + NSUB].bitcast(I32)


def head_select(net):
    return net.wtmp[0:H, 540:540 + D]


def gat_begin(net):
    nc = net.nc
    A, Cc = net.A, net.C
    s = {k: net.sem(f"gb_{k}") for k in ("brought", "used", "spread", "product", "begun")}

    with nc.Block() as block:
        @block.gpsimd
        def _(pool):
            pool.sem_inc(s["used"], 2)

            def bring(c, k):
                pool.wait_ge(s["used"], c + 1)
                own = net.p_self[:, bass.ds(c * 4 * H, 4 * H)]
                nc.gpsimd.tensor_copy(net.work[0:SUB, 1024 + k * 4 * H:1024 + (k + 1) * 4 * H], own)
                nc.gpsimd.tensor_copy(net.work[0:SUB, k * 512:(k + 1) * 512].rearrange("p (t c) -> p t c", c=C),
                                      own.unsqueeze(2).broadcast_to([SUB, 4 * H, C])).then_inc(s["brought"], 1)
            each_chunk(pool, bring)

        @block.tensor
        def _(pe):
            def products(c, k):
                pe.wait_ge(s["brought"], c + 1)
                pe.wait_ge(s["begun"], c + 1)
                nc.tensor.matmul(net.bank(2, c), net.wtmp[:, 0:D], net.col(A, c), start=True, stop=True)
                for j in range(4):
                    m = nc.tensor.matmul(
                        net.psum[:, k * 512 + j * SUB:k * 512 + (j + 1) * SUB],
                        net.work[0:SUB, k * 512 + j * D:k * 512 + (j + 1) * D],
                        net.ident[0:SUB, 0:SUB], start=True, stop=True)
                for j in range(4):
                    m = nc.tensor.matmul(
                        net.psum[0:H, (4 + k) * 512 + j * SUB:(4 + k) * 512 + (j + 1) * SUB],
                        net.work[0:SUB, 1024 + (4 * k + j) * H:1024 + (4 * k + j + 1) * H],
                        net.ident[0:SUB, 0:SUB], start=True, stop=True)
                m.then_inc(s["used"], 1)
            each_chunk(pe, products)

        @block.scalar
        def _(act):
            with act.Fori(0, NCH) as c:
                act.wait_ge(s["used"], c + 3)
                nc.scalar.copy(net.work[:, bass.ds((c % 2) * 512 + 1536, CH)], net.bank(0, c))
                nc.scalar.copy(Cc[0:H, bass.ds(c * CH, CH)],
                               net.psum[0:H, bass.ds((c % 2) * 512 + 4 * 512, CH)]).then_inc(s["spread"], 1)

        @block.vector
        def _(dve):
            nc.vector.memset(A[:, N:REG], 0.0)
            nc.vector.memset(Cc[:, N:REG], 1.0)
            dve.sem_inc(s["begun"], 2)
            with dve.Fori(0, NCH) as c:
                dve.wait_ge(s["spread"], c + 1)
                nc.vector.tensor_tensor(net.col(A, c), net.bank(2, c),
                                        net.work[:, bass.ds((c % 2) * 512 + 1536, CH)],
                                        ALU.mult).then_inc(s["begun"], 1)


def gat_output(net):
    nc = net.nc
    A, B, Cc = net.A, net.B, net.C
    w1, w2 = net.wtmp[:, 0:2 * D], net.wtmp[:, 2 * D:4 * D]
    gain, bias, gat_b, b1, b2 = (net.small[:, 0:1], net.small[:, 1:2], net.small[:, 2:3],
                                 net.small[:, 4:6], net.small[:, 3:4])
    s = {k: net.sem(f"go_{k}") for k in
         ("weights", "h", "spread", "inverse", "ratio", "sum", "mean", "centred", "squared", "var", "dev",
          "carried", "inverse2", "scaled", "normed", "up", "gelu", "down", "out")}
    hidden = [net.work[:, k * 1024:(k + 1) * 1024] for k in range(2)]

    with nc.Block() as block:
        @block.sync
        def _(sp):
            sp.dma_start(B[:, 0:N], net.HT).then_inc(s["h"], 16)
            sp.dma_start(w1, net.dram["L1_gnn_w1"]).then_inc(s["weights"], 16)
            sp.dma_start(w2.rearrange("p (k n) -> p k n", k=2),
                         net.dram["L1_gnn_w2"].rearrange("(k p) n -> p k n", k=2)).then_inc(s["weights"], 16)
            for to, name in ((gain, "L1_gnn_ln2_g"), (bias, "L1_gnn_ln2_b"), (gat_b, "L1_gnn_gat_b"),
                             (b2, "L1_gnn_b2")):
                sp.dma_start(to, net.dram[name].rearrange("(p a) -> p a", a=1)).then_inc(s["weights"], 16)
            for k in range(2):
                sp.dma_start(b1[:, k:k + 1], net.dram["L1_gnn_b1"][k * D:(k + 1) * D]
                             .rearrange("(p a) -> p a", a=1)).then_inc(s["weights"], 16)

        @block.tensor
        def _(pe):
            with pe.Fori(0, NCH) as c:
                pe.wait_ge(s["inverse"], c + 1)
                nc.tensor.matmul(net.bank(0, c), head_select(net), Cc[0:H, bass.ds(c * CH, CH)],
                                 start=True, stop=True).then_inc(s["spread"], 1)
            with pe.Fori(0, NCH) as c:
                pe.wait_ge(s["sum"], c + 1)
                pe.wait_ge(s["centred"], c + 1)
                nc.tensor.matmul(net.bank(2, c), net.mean_w[:, :], net.col(B, c),
                                 start=True, stop=True).then_inc(s["mean"], 1)
            with pe.Fori(0, NCH) as c:
                pe.wait_ge(s["squared"], c + 1)
                pe.wait_ge(s["dev"], c + 1)
                nc.tensor.matmul(net.bank(4, c), net.mean_w[:, :], net.col(A, c),
                                 start=True, stop=True).then_inc(s["var"], 1)
            pe.wait_ge(s["centred"], NCH + 2)
            pe.wait_ge(s["dev"], NCH + 2)

            def up(c, k):
                pe.wait_ge(s["normed"], c + 1)
                pe.wait_ge(s["gelu"], c + 1)
                for j in range(2):
                    m = nc.tensor.matmul(net.psum[:, (2 * k + j) * 512:(2 * k + j) * 512 + CH],
                                         w1[:, j * D:(j + 1) * D], net.col(A, c), start=True, stop=True)
                m.then_inc(s["up"], 1)

            def down(c, k):
                pe.wait_ge(s["gelu"], c + 3)
                pe.wait_ge(s["out"], c + 1)
                for j in range(2):
                    m = nc.tensor.matmul(net.psum[:, (4 + k) * 512:(4 + k) * 512 + CH],
                                         w2[:, j * D:(j + 1) * D],
                                         hidden[k][:, j * 512:j * 512 + CH], start=(j == 0), stop=(j == 1))
                m.then_inc(s["down"], 1)

            up(0, 0)
            with pe.Fori(0, NCH // 2) as i:
                c = pe.snap(i * 2)
                up(c + 1, 1)
                down(c, 0)
                up(c + 2, 0)
                down(c + 1, 1)
            down(NCH - 1, 0)

        @block.vector
        def _(dve):
            dve.sem_inc(s["inverse"], 2)
            dve.wait_ge(s["weights"], 128)
            dve.wait_ge(s["h"], 16)
            with dve.Fori(0, NCH) as c:
                dve.wait_ge(s["spread"], c + 1)
                dve.sem_inc(s["carried"], 1)
                nc.vector.reciprocal(net.col(Cc, c), net.bank(0, c)).then_inc(s["inverse"], 1)
                dve.wait_ge(s["inverse"], c + 3)
                nc.vector.tensor_tensor(net.col(A, c), net.col(A, c), net.col(Cc, c),
                                        ALU.mult).then_inc(s["ratio"], 1)
                dve.wait_ge(s["ratio"], c + 1)
                nc.vector.scalar_tensor_tensor(out=net.col(B, c), in0=net.col(A, c), scalar=gat_b,
                                               in1=net.col(B, c), op0=ALU.add,
                                               op1=ALU.add).then_inc(s["sum"], 1)
            dve.sem_inc(s["centred"], 2)
            with dve.Fori(0, NCH) as c:
                dve.wait_ge(s["mean"], c + 1)
                nc.vector.tensor_tensor(net.col(Cc, c), net.col(B, c), net.bank(2, c),
                                        ALU.subtract).then_inc(s["centred"], 1)
            with dve.Fori(0, NCH) as c:
                dve.wait_ge(s["dev"], c + 3)
                dve.sem_inc(s["carried"], 1)
                nc.vector.reciprocal(net.col(A, c), net.col(A, c)).then_inc(s["inverse2"], 1)
                dve.wait_ge(s["inverse2"], c + 1)
                nc.vector.tensor_tensor(net.col(A, c), net.col(Cc, c), net.col(A, c),
                                        ALU.mult).then_inc(s["scaled"], 1)
            dve.sem_inc(s["out"], 2)

            def out(c, k):
                dve.wait_ge(s["down"], c + 1)
                nc.vector.scalar_tensor_tensor(out=net.col(B, c), in0=net.psum[:, (4 + k) * 512:(4 + k) * 512 + CH],
                                               scalar=b2, in1=net.col(B, c), op0=ALU.add,
                                               op1=ALU.add).then_inc(s["out"], 1)
            each_chunk(dve, out)

        @block.scalar
        def _(act):
            act.sem_inc(s["dev"], 2)
            act.wait_ge(s["weights"], 128)
            with act.Fori(0, NCH) as c:
                act.wait_ge(s["centred"], c + 3)
                nc.scalar.activation(net.col(A, c), net.col(Cc, c), ACT.Square).then_inc(s["squared"], 1)
            with act.Fori(0, NCH) as c:
                act.wait_ge(s["var"], c + 1)
                nc.scalar.activation(net.col(A, c), net.bank(4, c), ACT.Sqrt,
                                     bias=net.eps[:, 0:1]).then_inc(s["dev"], 1)
            with act.Fori(0, NCH) as c:
                act.wait_ge(s["scaled"], c + 1)
                nc.scalar.activation(net.col(A, c), net.col(A, c), ACT.Identity,
                                     bias=bias, scale=gain).then_inc(s["normed"], 1)
            act.sem_inc(s["gelu"], 2)

            def gelu(c, k):
                act.wait_ge(s["up"], c + 1)
                act.wait_ge(s["out"], c + 1)
                nc.scalar.activation(hidden[k][:, 0:CH], net.psum[:, 2 * k * 512:2 * k * 512 + CH],
                                     ACT.Gelu, bias=b1[:, 0:1])
                nc.scalar.activation(hidden[k][:, 512:512 + CH],
                                     net.psum[:, (2 * k + 1) * 512:(2 * k + 1) * 512 + CH],
                                     ACT.Gelu, bias=b1[:, 1:2]).then_inc(s["gelu"], 1)
            each_chunk(act, gelu)


def gin_output(net):
    nc = net.nc
    A, B, Cc = net.A, net.B, net.C
    w1, w2 = net.wtmp[:, 0:2 * D], net.wtmp[:, 2 * D:4 * D]
    vec = net.small
    g1, b1, g2, b2, onep = vec[:, 0:2], vec[:, 2:4], vec[:, 4:5], vec[:, 5:6], vec[:, 6:7]
    mv = [vec[:, 8 + 2 * k:10 + 2 * k] for k in range(3)]
    scale, shift = vec[:, 16:19], vec[:, 20:23]
    stats = [net.onehot[:, :, :, :].rearrange("p a t w -> p (a t w)")[:, k * 6 * NCH:(k + 1) * 6 * NCH]
             for k in range(3)]
    hidden = [net.work[:, k * 1024:(k + 1) * 1024] for k in range(2)]
    s = {k: net.sem(f"gi_{k}") for k in
         ("weights", "h", "step", "z", "first", "stat", "deviation", "up", "hid", "down", "out", "last",
          "sum", "kept")}

    def fold(dve, k, gain, bias, wait, count):
        V = nc.vector
        V.bn_aggr(mv[k], stats[k]).then_inc(s["step"], 1)
        dve.wait_ge(s["step"], count + 1)
        dve.sem_inc(s["deviation"], 1)
        dve.wait_ge(s["deviation"], wait)
        V.reciprocal(scale[:, k:k + 1], scale[:, k:k + 1]).then_inc(s["step"], 1)
        dve.wait_ge(s["step"], count + 2)
        V.tensor_tensor(scale[:, k:k + 1], scale[:, k:k + 1], gain, ALU.mult).then_inc(s["step"], 1)
        dve.wait_ge(s["step"], count + 3)
        V.tensor_tensor(shift[:, k:k + 1], mv[k][:, 0:1], scale[:, k:k + 1], ALU.mult).then_inc(s["step"], 1)
        dve.wait_ge(s["step"], count + 4)
        V.tensor_tensor(shift[:, k:k + 1], bias, shift[:, k:k + 1], ALU.subtract).then_inc(s["step"], 1)

    with nc.Block() as block:
        @block.sync
        def _(sp):
            sp.dma_start(net.ES, Cc[:, 0:N]).then_inc(s["kept"], 16)
            sp.dma_start(B[:, 0:N], net.HT).then_inc(s["h"], 16)
            sp.dma_start(w1, net.dram["L2_gnn_W1"]).then_inc(s["weights"], 16)
            sp.dma_start(w2.rearrange("p (k n) -> p k n", k=2),
                         net.dram["L2_gnn_W2"].rearrange("(k p) n -> p k n", k=2)).then_inc(s["weights"], 16)
            for to, name in ((g1, "L2_gnn_g1"), (b1, "L2_gnn_b1")):
                for k in range(2):
                    sp.dma_start(to[:, k:k + 1], net.dram[name][k * D:(k + 1) * D]
                                 .rearrange("(p a) -> p a", a=1)).then_inc(s["weights"], 16)
            for to, name in ((g2, "L2_gnn_g2"), (b2, "L2_gnn_b2")):
                sp.dma_start(to, net.dram[name].rearrange("(p a) -> p a", a=1)).then_inc(s["weights"], 16)
            sp.dma_start(onep, net.dram["L2_gnn_eps"].rearrange("(a b) -> a b", a=1)
                         .broadcast_to([P, 1])).then_inc(s["weights"], 16)
            sp.wait_ge(s["kept"], 16)

        @block.vector
        def _(dve):
            dve.wait_ge(s["weights"], 144)
            nc.vector.tensor_scalar(onep, onep, 1.0, None, ALU.add).then_inc(s["step"], 1)
            dve.wait_ge(s["step"], 1)
            dve.wait_ge(s["h"], 16)
            with dve.Fori(0, NCH) as c:
                nc.vector.scalar_tensor_tensor(out=net.col(A, c), in0=net.col(B, c), scalar=onep,
                                               in1=net.col(A, c), op0=ALU.mult,
                                               op1=ALU.add).then_inc(s["z"], 1)
            dve.sem_inc(s["stat"], 2)

            def statistics(c, k):
                dve.wait_ge(s["first"], c + 1)
                for j in range(2):
                    last = nc.vector.bn_stats(stats[j][:, bass.ds(c * 6, 6)],
                                              net.psum[:, (2 * k + j) * 512:(2 * k + j) * 512 + CH])
                last.then_inc(s["stat"], 1)
            each_chunk(dve, statistics)
            dve.wait_ge(s["stat"], NCH + 2)
            fold(dve, 0, g1[:, 0:1], b1[:, 0:1], 2, 1)
            fold(dve, 1, g1[:, 1:2], b1[:, 1:2], 4, 6)
            dve.sem_inc(s["out"], 2)

            def out(c, k):
                dve.wait_ge(s["down"], c + 1)
                bank = net.psum[:, (4 + k) * 512:(4 + k) * 512 + CH]
                nc.vector.tensor_copy(net.col(A, c), bank)
                nc.vector.bn_stats(stats[2][:, bass.ds(c * 6, 6)], bank).then_inc(s["out"], 1)
            each_chunk(dve, out)
            dve.wait_ge(s["out"], NCH + 2)
            fold(dve, 2, g2, b2, 6, 11)
            with dve.Fori(0, NCH) as c:
                dve.wait_ge(s["last"], c + 1)
                nc.vector.tensor_tensor(net.col(B, c), net.col(A, c), net.col(B, c),
                                        ALU.add).then_inc(s["sum"], 1)

        @block.scalar
        def _(act):
            for k in range(3):
                if k == 2:
                    act.wait_ge(s["step"], 11)
                    act.sem_inc(s["hid"], 2)

                    def normed(c, kk):
                        act.wait_ge(s["up"], c + 1)
                        act.wait_ge(s["out"], c + 1)
                        for j in range(2):
                            last = nc.scalar.activation(
                                hidden[kk][:, j * 512:j * 512 + CH],
                                net.psum[:, (2 * kk + j) * 512:(2 * kk + j) * 512 + CH], ACT.Relu,
                                bias=shift[:, j:j + 1], scale=scale[:, j:j + 1])
                        last.then_inc(s["hid"], 1)
                    each_chunk(act, normed)
                act.wait_ge(s["deviation"], 2 * k + 1)
                nc.scalar.activation(scale[:, k:k + 1], mv[k][:, 1:2], ACT.Sqrt,
                                     bias=net.eps[:, 0:1]).then_inc(s["deviation"], 1)
            act.wait_ge(s["step"], 16)
            with act.Fori(0, NCH) as c:
                nc.scalar.activation(net.col(A, c), net.col(A, c), ACT.Relu,
                                     bias=shift[:, 2:3], scale=scale[:, 2:3]).then_inc(s["last"], 1)

        @block.tensor
        def _(pe):
            pe.wait_ge(s["weights"], 144)

            def up(c, k, done, free):
                pe.wait_ge(s["z"], c + 1)
                pe.wait_ge(free, c + 1)
                for j in range(2):
                    m = nc.tensor.matmul(net.psum[:, (2 * k + j) * 512:(2 * k + j) * 512 + CH],
                                         w1[:, j * D:(j + 1) * D], net.col(A, c), start=True, stop=True)
                m.then_inc(done, 1)

            def down(c, k):
                pe.wait_ge(s["hid"], c + 3)
                pe.wait_ge(s["out"], c + 1)
                for j in range(2):
                    m = nc.tensor.matmul(net.psum[:, (4 + k) * 512:(4 + k) * 512 + CH],
                                         w2[:, j * D:(j + 1) * D],
                                         hidden[k][:, j * 512:j * 512 + CH], start=(j == 0), stop=(j == 1))
                m.then_inc(s["down"], 1)

            each_chunk(pe, lambda c, k: up(c, k, s["first"], s["stat"]))
            pe.wait_ge(s["stat"], NCH + 2)
            up(0, 0, s["up"], s["hid"])
            with pe.Fori(0, NCH // 2) as i:
                c = pe.snap(i * 2)
                up(c + 1, 1, s["up"], s["hid"])
                down(c, 0)
                up(c + 2, 0, s["up"], s["hid"])
                down(c + 1, 1)
            down(NCH - 1, 0)


def finish(net, out):
    nc = net.nc
    A, B, Cc = net.A, net.B, net.C
    s = {k: net.sem(f"f_{k}") for k in
         ("x", "edges", "half", "twice", "sum", "freed", "brought", "turned", "rows", "stored")}

    with nc.Block() as block:
        @block.sync
        def _(sp):
            sp.dma_start(Cc[:, 0:N], net.XT).then_inc(s["x"], 16)
            sp.wait_ge(s["twice"], NCH)
            sp.dma_start(Cc[:, 0:N], net.ES).then_inc(s["edges"], 16)
            rows_store(net, sp, s, B, out)

        @block.vector
        def _(dve):
            with dve.Fori(0, NCH) as c:
                nc.vector.tensor_tensor(net.col(A, c), net.col(A, c), net.col(B, c),
                                        ALU.add).then_inc(s["half"], 1)
            dve.wait_ge(s["x"], 16)
            dve.wait_ge(s["half"], NCH)
            with dve.Fori(0, NCH) as c:
                nc.vector.tensor_tensor(net.col(A, c), net.col(A, c), net.col(Cc, c),
                                        ALU.add).then_inc(s["twice"], 1)
            dve.wait_ge(s["edges"], 16)
            dve.wait_ge(s["twice"], NCH)
            with dve.Fori(0, NCH) as c:
                nc.vector.tensor_tensor(net.col(A, c), net.col(A, c), net.col(Cc, c),
                                        ALU.add).then_inc(s["sum"], 1)

        @block.gpsimd
        def _(pool):
            rows_bring(net, pool, s, A, s["sum"], 0)

        @block.tensor
        def _(pe):
            rows_turn(net, pe, s, 2)

        @block.scalar
        def _(act):
            rows_copy(net, act, nc.scalar.copy, s, 2, B)


def program(nc, dram, out):
    with ExitStack() as ctx:
        net = Net(nc, ctx, dram)
        allocate(net)
        for step in (
                lambda: prepare(net),
                lambda: normalise(net, "n0", first=True, table=net.TA),
                lambda: aggregate(net, "agg0", net.TA, "count"),
                lambda: segment_ends(net),
                lambda: sage(net, "sage0", "L0_gnn_W0", "L0_gnn_b0", net.TB, invert=True),
                lambda: aggregate(net, "agg1", net.TB),
                lambda: sage(net, "sage1", "L0_gnn_W1", "L0_gnn_b1", net.TA),
                lambda: aggregate(net, "agg2", net.TA),
                lambda: sage(net, "sage2", "L0_gnn_W2", "L0_gnn_b2"),
                lambda: normalise(net, "n1", keep=True),
                lambda: gat_project(net),
                lambda: gat_gather(net),
                lambda: gat_softmax(net),
                lambda: gat_begin(net),
                lambda: aggregate(net, "agg3", extra="attention"),
                lambda: gat_output(net),
                lambda: normalise(net, "n2", keep=True, table=net.TB),
                lambda: aggregate(net, "agg4", net.TB, "edges"),
                lambda: gin_output(net),
                lambda: normalise(net, "n3", table=net.TA),
                lambda: aggregate(net, "agg5", net.TA),
                lambda: finish(net, out)):
            with net.stage():
                step()


INPUTS = ["x", "src", "dst", "edge_attr_128", "L0_gnn_W0", "L0_gnn_b0", "L0_gnn_W1", "L0_gnn_b1",
          "L0_gnn_W2", "L0_gnn_b2", "L1_gnn_ln1_g", "L1_gnn_ln1_b", "L1_gnn_W", "L1_gnn_att_src",
          "L1_gnn_att_dst", "L1_gnn_gat_b", "L1_gnn_ln2_g", "L1_gnn_ln2_b", "L1_gnn_w1", "L1_gnn_b1",
          "L1_gnn_w2", "L1_gnn_b2", "L2_gnn_eps", "L2_gnn_W1", "L2_gnn_g1", "L2_gnn_b1", "L2_gnn_W2",
          "L2_gnn_g2", "L2_gnn_b2"]


def kernel(**inputs):
    import numpy as np
    import concourse.bacc as bacc
    from concourse.bass_utils import run_bass_kernel_spmd

    nc = bacc.Bacc("TRN2", target_bir_lowering=False, num_devices=1)
    arrays, dram = {}, {}
    for name in INPUTS:
        a = np.ascontiguousarray(inputs[name])
        if a.ndim == 0:
            a = a.reshape(1)
        arrays[f"in_{name}"] = a
        dram[name] = nc.dram_tensor(f"in_{name}", a.shape, mybir.dt.from_np(a.dtype),
                                    kind="ExternalInput").ap()
    out = nc.dram_tensor("out", [N, D], F32, kind="ExternalOutput").ap()
    program(nc, dram, out)
    r = run_bass_kernel_spmd(nc, [arrays], core_ids=[0])
    return r.results[0]["out"]
```

```python
from contextlib import ExitStack, contextmanager

import concourse.bass as bass
from concourse import mybir

F32 = mybir.dt.float32
I32 = mybir.dt.int32
ALU = mybir.AluOpType
ACT = mybir.ActivationFunctionType
AX_X = mybir.AxisListType.X

N = 12500
E = 200000
D = 128
P = 128
CH = 500
NCH = N // CH
SUB = 125
NSUB = N // SUB
TILE = 128
HALF = 16
GT = 4
GPH = HALF // GT
NHALF = 98
NIT = NHALF // 2
NTILE = NHALF * HALF
NGRP = NTILE // GT
EP = NTILE * TILE
GE = GT * TILE
W = 64
EPP = EP // P
H = 4
C = D // H
XW = D + 2 * H
EPS = 1e-5
BIG = 1e38
NSC = -(-(EP + N) // P) * P
REG = 12800


class Net:

    def __init__(self, nc, ctx, dram):
        self.nc, self.ctx, self.dram = nc, ctx, dram
        self.pool_sems = [ctx.enter_context(nc.semaphore(f"pool_dma{k}")) for k in range(23)]
        self.stage_sems, self.stage_ctx = [], None

    @contextmanager
    def stage(self):
        with ExitStack() as self.stage_ctx:
            yield
            sems, self.stage_sems = self.stage_sems, []
            with self.nc.Block() as block:
                @block.sync
                def _(sp):
                    for x in sems:
                        sp.sem_clear(x)

    def sem(self, name):
        x = self.stage_ctx.enter_context(self.nc.semaphore(name))
        self.stage_sems.append(x)
        return x

    def pool_sem(self):
        return self.pool_sems.pop()

    def sb(self, name, shape, dt=F32):
        return self.ctx.enter_context(self.nc.sbuf_tensor(name, shape, dt))

    def hbm(self, name, shape, dt=F32):
        return self.nc.dram_tensor(name, shape, dt, kind="Internal").ap()

    def col(self, t, c):
        return t[:, bass.ds(c * CH, CH)]

    def bank(self, first, c, n=CH):
        return self.psum[:, bass.ds((c % 2) * 512 + first * 512, n)]


def allocate(net):
    net.A = net.sb("regionA", [P, REG])
    net.B = net.sb("regionB", [P, REG])
    net.C = net.sb("regionC", [P, NSUB * XW])
    net.work = net.sb("work", [P, 2 * HALF * XW])
    net.onehot = net.sb("onehot", [P, 2, HALF, W])
    net.src_n = net.sb("src_n", [P, NTILE])
    net.rel_n = net.sb("rel_n", [P, NTILE])
    net.index = net.sb("index", [P, 2, HALF], I32)
    net.base = net.sb("base", [1, NGRP], I32)
    net.base_now = net.sb("base_now", [1, NGRP], I32)
    net.rounds = net.sb("rounds", [1, 1], I32)
    net.due = net.sb("due", [1, NIT + 1], I32)
    net.window0 = net.sb("window0", [P, W])
    net.window = net.sb("window", [P, W])
    net.ident = net.sb("ident", [P, P])
    net.mean_w = net.sb("mean_w", [P, P])
    net.ones = net.sb("ones", [P, P])
    net.eps = net.sb("eps", [P, 1])
    net.psum = net.ctx.enter_context(net.nc.psum_tensor("psum", [P, 8 * 512], F32))
    net.p_self = net.sb("p_self", [SUB, NSUB * H])
    net.wtmp = net.sb("weights", [P, 2 * 2 * D + 4 * D + 24])
    net.small = net.sb("small", [P, 160])
    net.turn = net.sb("turn", [P, CH])
    net.rows = net.sb("rows", [P, 4 * XW])

    net.XT = net.hbm("x_transposed", [D, N])
    net.HT = net.hbm("h_transposed", [D, N])
    net.ES = net.hbm("edge_sum", [D, N])
    net.TA = net.hbm("rows_a", [N, D])
    net.TB = net.hbm("rows_b", [N, D])
    net.XH = net.hbm("attention_rows", [N, XW])
    net.G = net.hbm("gathered_rows", [NHALF, P, HALF * XW])
    net.SH = net.hbm("scores_by_head", [H, EP])
    net.PH = net.hbm("probs_by_head", [H, EP])
    net.FD = net.hbm("running_max", [EP, H])
    net.SC = net.hbm("segment_starts", [NSC, 2 * H])
    net.NV = net.hbm("node_values", [N, 2 * H])
    net.DEALT = net.hbm("dealt_lists", [2, P, NTILE])
    net.DST = net.hbm("dst_padded", [EP])
    net.BASE = net.hbm("group_bases", [NGRP], I32)
    net.CUM = net.hbm("segment_ends", [2, N])


def each_chunk(eng, body, count=NCH):
    with eng.Fori(0, count // 2) as i:
        for k in range(2):
            body(eng.snap(i * 2 + k), k)
    for c in range(count // 2 * 2, count):
        body(c, c % 2)


def slot(net, k, width=CH):
    return net.work[:, k * 512:k * 512 + width]



def rows_bring(net, pool, s, region, ready, start):
    pool.sem_inc(s["turned"], 2)

    def bring(c, k):
        pool.wait_ge(ready, c + 1 + start)
        pool.wait_ge(s["turned"], c + 1)
        net.nc.gpsimd.tensor_copy(slot(net, k), net.col(region, c)).then_inc(s["brought"], 1)
    each_chunk(pool, bring)


def rows_turn(net, pe, s, first):
    def turn(c, k):
        pe.wait_ge(s["brought"], c + 1)
        pe.wait_ge(s["rows"], c + 1)
        for j in range(4):
            t = net.nc.tensor.transpose(
                net.psum[0:SUB, (first + k) * 512 + j * D:(first + k) * 512 + (j + 1) * D],
                net.work[:, k * 512 + j * SUB:k * 512 + (j + 1) * SUB], net.ident[:, :])
        t.then_inc(s["turned"], 1)
    each_chunk(pe, turn)


def rows_copy(net, eng, copy, s, first, region):
    eng.sem_inc(s["rows"], 2)

    def out(c, k):
        eng.wait_ge(s["turned"], c + 3)
        copy(region[0:SUB, bass.ds(c * 4 * D, 4 * D)],
             net.psum[0:SUB, (first + k) * 512:(first + k + 1) * 512]).then_inc(s["rows"], 1)
    each_chunk(eng, out)


def rows_store(net, sp, s, region, table, width=D):
    with sp.Fori(0, NCH) as c:
        sp.wait_ge(s["rows"], c + 3)
        sp.dma_start(table[bass.ds(c * CH, CH), :].rearrange("(t p) f -> p t f", p=SUB),
                     region[0:SUB, bass.ds(c * 4 * width, 4 * width)].rearrange("p (t f) -> p t f", f=width)
                     ).then_inc(s["stored"], 16)
    sp.wait_ge(s["stored"], 16 * NCH)


def prepare(net):
    nc = net.nc
    GP = NGRP // GPH
    built, masked, filled = net.sem("pre_built"), net.sem("pre_masked"), net.sem("pre_filled")
    loaded_d, loaded_s = net.sem("pre_dst"), net.sem("pre_src")
    step, spread, wrote = net.sem("pre_step"), net.sem("pre_spread"), net.sem("pre_wrote")
    loaded_b, turned, copied = net.sem("pre_base"), net.sem("pre_turned"), net.sem("pre_copied")
    dst_i = net.A[0:GP, 0:GPH * GE].bitcast(I32)
    dst_f = net.A[0:GP, 2048:2048 + GPH * GE]
    rel_f = net.A[0:GP, 4096:4096 + GPH * GE]
    src_i = net.B[0:GP, 0:GPH * GE].bitcast(I32)
    src_f = net.B[0:GP, 2048:2048 + GPH * GE]
    dealt = [net.B[:, 4096 + k * NTILE:4096 + (k + 1) * NTILE] for k in range(2)]
    least, most = net.small[0:GP, 0:GPH], net.small[0:GP, 4:8]
    span = net.small[0:GP, 8:9]
    least_i = net.small[0:GP, 12:16].bitcast(I32)
    row = net.small[0:1, 16:20]
    it_i = net.work[:, 0:W].bitcast(I32)
    zeros = net.C[:, 0:2 * H * NSC // P // 2]
    whole = E // (GPH * GE)
    left = E - whole * GPH * GE
    lists = [(src_f, net.src_n, False), (rel_f, net.rel_n, False), (src_f, dealt[0], True), (rel_f, dealt[1], True)]
    tiles = [(fr, to, deal, g, k) for fr, to, deal in lists for g in range(GPH) for k in range(GT)]

    with nc.Block() as block:
        @block.gpsimd
        def _(pool):
            pool.memset(net.ident[:, :], 0.0).then_inc(built, 1)
            pool.iota(it_i, pattern=[[1, W]], base=0, channel_multiplier=0).then_inc(built, 1)
            pool.wait_ge(built, 2)
            pool.affine_select(out=net.ident[:, :], in_=net.ident[:, :], compare_op=ALU.not_equal,
                               fill=1.0, base=0, pattern=[[-1, P]],
                               channel_multiplier=1).then_inc(masked, 1)

        @block.sync
        def _(sp):
            sp.wait_ge(filled, 2)
            for name, to, sem in (("dst", dst_i, loaded_d), ("src", src_i, loaded_s)):
                sp.dma_start(to[0:whole, :], net.dram[name][0:whole * GPH * GE]
                             .rearrange("(p f) -> p f", p=whole)).then_inc(sem, 16)
                sp.dma_start(to[whole:whole + 1, 0:left], net.dram[name][whole * GPH * GE:E]
                             .rearrange("(p f) -> p f", p=1)).then_inc(sem, 16)
            sp.wait_ge(step, 4)
            sp.dma_start(net.DST.rearrange("(p f) -> p f", p=GP), dst_f).then_inc(wrote, 16)
            sp.dma_start(net.BASE.rearrange("(p f) -> p f", p=GP), least_i).then_inc(loaded_b, 16)
            sp.wait_ge(filled, 3)
            flat = net.SC.rearrange("(k p r) f -> k p (r f)", k=2, p=P)
            for k in range(2):
                sp.dma_start(flat[k], zeros).then_inc(wrote, 16)
            sp.wait_ge(loaded_b, 16)
            sp.dma_start(net.base[:, :], net.BASE.rearrange("(a g) -> a g", a=1)).then_inc(loaded_b, 16)
            sp.wait_ge(copied, len(tiles))
            for k in range(2):
                sp.dma_start(net.DEALT[k], dealt[k]).then_inc(wrote, 16)
            sp.wait_ge(wrote, 80)
            sp.wait_ge(loaded_b, 32)

        @block.vector
        def _(dve):
            nc.vector.memset(dst_i, N).then_inc(filled, 1)
            nc.vector.memset(src_i, 0).then_inc(filled, 1)
            nc.vector.memset(zeros, 0.0).then_inc(filled, 1)
            nc.vector.memset(net.ones[:, :], 1.0)
            nc.vector.memset(net.mean_w[:, :], 1.0 / D)
            nc.vector.memset(net.eps[:, :], EPS)
            dve.wait_ge(built, 2)
            nc.vector.tensor_copy(net.window0[:, :], it_i)
            dve.wait_ge(loaded_d, 32)
            nc.vector.tensor_copy(dst_f, dst_i).then_inc(step, 1)
            dve.wait_ge(step, 1)
            df = dst_f.rearrange("p (g e) -> p g e", g=GPH)
            nc.vector.tensor_reduce(least, df, AX_X, ALU.min)
            nc.vector.tensor_reduce(most, df, AX_X, ALU.max).then_inc(step, 1)
            dve.wait_ge(step, 2)
            nc.vector.tensor_copy(least_i, least).then_inc(step, 1)
            nc.vector.tensor_tensor(rel_f.rearrange("p (g e) -> p g e", g=GPH), df,
                                    least.unsqueeze(2).broadcast_to([GP, GPH, GE]),
                                    ALU.subtract).then_inc(step, 1)
            nc.vector.tensor_tensor(most, most, least, ALU.subtract).then_inc(step, 1)
            dve.wait_ge(step, 5)
            nc.vector.tensor_reduce(span, most, AX_X, ALU.max).then_inc(step, 1)
            dve.wait_ge(spread, 1)
            nc.vector.tensor_reduce(row[:, 0:1], net.psum[0:1, 0:GP], AX_X, ALU.max).then_inc(step, 1)
            dve.wait_ge(step, 7)
            nc.vector.tensor_scalar(row[:, 1:2], row[:, 0:1], 1.0 / W, 0.5 + 0.5 / W,
                                    ALU.mult, ALU.add).then_inc(step, 1)
            dve.wait_ge(step, 8)
            nc.vector.tensor_copy(net.rounds[:, :], row[:, 1:2])
            dve.wait_ge(loaded_s, 32)
            nc.vector.tensor_copy(src_f, src_i).then_inc(step, 1)
            dve.wait_ge(loaded_b, 32)
            low = [net.work[0:1, 512 * k:512 * k + 128] for k in range(2)]
            bases = net.work[0:1, 1024:1024 + NGRP]
            nc.vector.tensor_copy(bases, net.base[:, :])
            nc.vector.memset(low[0], N)
            nc.vector.memset(low[1], N).then_inc(step, 1)
            dve.wait_ge(step, 10)
            nc.vector.tensor_reduce(low[0][:, 0:NIT], bases.rearrange("a (i g) -> a i g", i=NIT), AX_X,
                                    ALU.min).then_inc(step, 1)
            for j in range(6):
                dve.wait_ge(step, 11 + j)
                nc.vector.tensor_tensor(low[(j + 1) % 2][:, 0:NIT], low[j % 2][:, 0:NIT],
                                        low[j % 2][:, 2 ** j:2 ** j + NIT], ALU.min).then_inc(step, 1)
            nc.vector.tensor_scalar(row[:, 2:3], row[:, 0:1], float(W), None, ALU.is_lt)
            dve.wait_ge(step, 17)
            nc.vector.tensor_scalar(low[1][:, 0:NIT], low[0][:, 0:NIT], 1.0 / CH, 0.5 / CH - 0.5,
                                    ALU.mult, ALU.add).then_inc(step, 1)
            dve.wait_ge(step, 18)
            nc.vector.tensor_copy(net.due[:, 0:NIT], low[1][:, 0:NIT]).then_inc(step, 1)
            dve.wait_ge(step, 19)
            nc.vector.tensor_copy(low[1][:, 0:NIT], net.due[:, 0:NIT]).then_inc(step, 1)
            dve.wait_ge(step, 20)
            nc.vector.tensor_scalar(low[1][:, 0:NIT], low[1][:, 0:NIT], row[:, 2:3], None,
                                    ALU.mult).then_inc(step, 1)
            dve.wait_ge(step, 21)
            nc.vector.tensor_copy(net.due[:, 0:NIT], low[1][:, 0:NIT])
            for n, (_, to, _, g, k) in enumerate(tiles):
                dve.wait_ge(turned, n + 1)
                nc.vector.tensor_copy(to[:, :].rearrange("p (a t) -> p a t", t=HALF)[:, :, g * GT + k],
                                      net.psum[:, (n % 2 + 2) * 512:(n % 2 + 2) * 512 + GP]
                                      ).then_inc(copied, 1)

        @block.tensor
        def _(pe):
            pe.wait_ge(masked, 1)
            pe.wait_ge(step, 6)
            nc.tensor.transpose(net.psum[0:1, 0:GP], span, net.ident[0:GP, 0:GP]).then_inc(spread, 1)
            pe.wait_ge(step, 9)
            for n, (fr, _, deal, g, k) in enumerate(tiles):
                if n >= 2:
                    pe.wait_ge(copied, n - 1)
                group = fr[:, g * GE:(g + 1) * GE]
                tile = (group.rearrange("a (p k) -> a k p", k=GT)[:, k, :] if deal
                        else group[:, k * TILE:(k + 1) * TILE])
                nc.tensor.transpose(net.psum[:, (n % 2 + 2) * 512:(n % 2 + 2) * 512 + GP], tile,
                                    net.ident[0:GP, 0:GP]).then_inc(turned, 1)


def normalise(net, tag, first=False, keep=False, table=None):
    nc = net.nc
    A, B, Cc = net.A, net.B, net.C
    s = {k: net.sem(f"{tag}_{k}") for k in
         ("loaded", "x_brought", "x_turned", "x_ready", "brought", "mean", "centred", "squared", "var", "dev", "carried", "inverse", "h", "turned", "rows", "saved", "stored", "kept")}

    with nc.Block() as block:
        @block.sync
        def _(sp):
            if first:
                for k in range(5):
                    sp.dma_start(A[0:SUB, k * 20 * D:(k + 1) * 20 * D].rearrange("p (t f) -> p t f", f=D),
                                 net.dram["x"][k * 2500:(k + 1) * 2500, :]
                                 .rearrange("(t p) f -> p t f", p=SUB)).then_inc(s["loaded"], 16)
            else:
                sp.dma_start(A[:, 0:N], net.XT).then_inc(s["loaded"], 16)
            sp.wait_ge(s["x_ready"], NCH + (2 if first else 0))
            sp.dma_start(net.XT, B[:, 0:N]).then_inc(s["saved"], 16)
            if keep:
                sp.wait_ge(s["h"], NCH)
                sp.dma_start(net.HT, B[:, 0:N]).then_inc(s["kept"], 16)
            if table is not None:
                rows_store(net, sp, s, Cc, table)
            sp.wait_ge(s["saved"], 16)
            if keep:
                sp.wait_ge(s["kept"], 16)

        @block.tensor
        def _(pe):
            if first:
                def turn(c, k):
                    pe.wait_ge(s["x_brought"], c + 1)
                    pe.wait_ge(s["x_ready"], c + 1)
                    for j in range(4):
                        t = nc.tensor.transpose(
                            net.psum[:, k * 512 + j * SUB:k * 512 + (j + 1) * SUB],
                            net.work[0:SUB, k * 512 + j * D:k * 512 + (j + 1) * D],
                            net.ident[0:SUB, 0:SUB])
                    t.then_inc(s["x_turned"], 1)
                each_chunk(pe, turn)
            with pe.Fori(0, NCH) as c:
                pe.wait_ge(s["x_ready"], c + (3 if first else 1))
                pe.wait_ge(s["centred"], c + 1)
                nc.tensor.matmul(net.bank(2, c), net.mean_w[:, :], net.col(B, c),
                                 start=True, stop=True).then_inc(s["mean"], 1)
            with pe.Fori(0, NCH) as c:
                pe.wait_ge(s["squared"], c + 1)
                pe.wait_ge(s["dev"], c + 1)
                nc.tensor.matmul(net.bank(4, c), net.mean_w[:, :], net.col(A, c),
                                 start=True, stop=True).then_inc(s["var"], 1)
            if table is not None:
                rows_turn(net, pe, s, 6)

        @block.vector
        def _(dve):
            dve.sem_inc(s["centred"], 2)
            if not first:
                dve.wait_ge(s["loaded"], 16)
                with dve.Fori(0, NCH) as c:
                    nc.vector.tensor_tensor(net.col(B, c), net.col(A, c), net.col(B, c),
                                            ALU.add).then_inc(s["x_ready"], 1)
            with dve.Fori(0, NCH) as c:
                dve.wait_ge(s["mean"], c + 1)
                nc.vector.tensor_tensor(net.col(Cc, c), net.col(B, c), net.bank(2, c),
                                        ALU.subtract).then_inc(s["centred"], 1)
            dve.wait_ge(s["saved"], 16)
            with dve.Fori(0, NCH) as c:
                dve.wait_ge(s["dev"], c + 3)
                dve.sem_inc(s["carried"], 1)
                nc.vector.reciprocal(net.col(A, c), net.col(A, c)).then_inc(s["inverse"], 1)
                dve.wait_ge(s["inverse"], c + 1)
                nc.vector.scalar_tensor_tensor(out=net.col(B, c), in0=net.col(Cc, c), scalar=0.0,
                                               in1=net.col(A, c), op0=ALU.max,
                                               op1=ALU.mult).then_inc(s["h"], 1)

        @block.scalar
        def _(act):
            act.sem_inc(s["dev"], 2)
            if first:
                act.sem_inc(s["x_ready"], 2)
                with act.Fori(0, NCH) as c:
                    act.wait_ge(s["x_turned"], c + 3)
                    nc.scalar.copy(net.col(B, c), net.bank(0, c)).then_inc(s["x_ready"], 1)
            with act.Fori(0, NCH) as c:
                act.wait_ge(s["centred"], c + 3)
                nc.scalar.activation(net.col(A, c), net.col(Cc, c), ACT.Square).then_inc(s["squared"], 1)
            with act.Fori(0, NCH) as c:
                act.wait_ge(s["var"], c + 1)
                nc.scalar.activation(net.col(A, c), net.bank(4, c), ACT.Sqrt,
                                     bias=net.eps[:, 0:1]).then_inc(s["dev"], 1)
            if table is not None:
                act.wait_ge(s["h"], NCH)
                rows_copy(net, act, nc.scalar.copy, s, 6, Cc)

        if first or table is not None:
            @block.gpsimd
            def _(pool):
                if first:
                    pool.sem_inc(s["x_turned"], 2)
                    pool.wait_ge(s["loaded"], 80)

                    def bring(c, k):
                        pool.wait_ge(s["x_turned"], c + 1)
                        nc.gpsimd.tensor_copy(net.work[0:SUB, k * 512:(k + 1) * 512],
                                              A[0:SUB, bass.ds(c * 4 * D, 4 * D)]
                                              ).then_inc(s["x_brought"], 1)
                    each_chunk(pool, bring)
                    pool.wait_ge(s["x_turned"], NCH + 2)
                if table is not None:
                    rows_bring(net, pool, s, B, s["h"], 0)


def due_chunks(net, eng, first, past, body, before=None):
    lo = eng.value_load(net.due[0:1, bass.ds(first, 1)], min_val=0, max_val=NCH)
    hi = NCH if past is None else eng.value_load(net.due[0:1, bass.ds(past, 1)], min_val=0, max_val=NCH)
    if before:
        before()
    with eng.If(lo < hi):
        with eng.Fori(lo, hi) as c:
            body(c)


def aggregate(net, tag, table=None, extra=None, follow=None):
    nc = net.nc
    A, Cc = net.A, net.C
    attention, edges = extra == "attention", extra == "edges"
    width = XW if attention else D
    S = 2 if attention or edges else 4
    ST, SG = 2 * HALF // S, 2 * GPH // S
    rows = [net.work[:, h * ST * XW:h * ST * XW + ST * width] for h in range(S)]
    rows3 = [r.rearrange("p (t f) -> p t f", f=width) for r in rows]
    attr = [net.B[:, h * HALF * D:(h + 1) * HALF * D] for h in range(2)]
    piles = [net.C[:, REG + h * SG * W:REG + (h + 1) * SG * W] for h in range(S)]
    onehot = net.onehot[:, :, :, :].rearrange("p a t w -> p (a t) w")
    at0 = EPP * H if attention else 2 * HALF * D
    msgs = [net.B[:, at0 + h * HALF * width:at0 + (h + 1) * HALF * width] for h in range(2)] if (
        attention or edges) else rows
    msgs3 = [m.rearrange("p (t f) -> p t f", f=width) for m in msgs]
    high = [P, H if attention else P]
    NB = 4 if follow else 8
    bank_of = lambda h, q, k: net.psum[0:high[k], (h * SG + q) % NB * 512 + k * W:(h * SG + q) % NB * 512 + (k + 1) * W]
    name = lambda k: [net.sem(f"{tag}_{k}{h}") for h in range(S)]
    index_ready, onehot_ready = name("index"), name("onehot")
    gathered = name("gathered") if attention else [net.pool_sem() for _ in range(S)]
    summed = name("summed")
    message, attr_loaded, relued = name("message"), name("attr"), name("relued")
    added = net.sem(f"{tag}_added")
    lists = net.sem(f"{tag}_lists")
    cleared, moved = net.sem(f"{tag}_cleared"), net.sem(f"{tag}_moved")
    piled = name("piled") if extra == "count" else onehot_ready
    ready = relued if edges else message if attention else gathered

    with nc.Block() as block:
        if follow:
            @block.scalar
            def _(act):
                follow.scalar(act)

        if not attention:
            if edges:
                @block.scalar
                def _(act):
                    R = act.value_load(net.rounds[0:1, 0:1], min_val=1, max_val=256)
                    with act.Fori(0, R) as r:
                        with act.Fori(0, NIT) as i:
                            n = act.snap(r * NIT + i)
                            for h in range(2):
                                act.wait_ge(message[h], n + 2)
                                nc.scalar.activation(msgs[h], msgs[h], ACT.Relu).then_inc(relued[h], 1)

            @block.gpsimd
            def _(pool):
                if edges:
                    pool.wait_ge(lists, 32)
                R = pool.value_load(net.rounds[0:1, 0:1], min_val=1, max_val=256)
                with pool.Fori(0, R) as r:
                    with pool.Fori(0, NIT) as i:
                        n = pool.snap(r * NIT + i)
                        for h in range(S):
                            if edges:
                                pool.wait_ge(message[h], n + 1)
                            else:
                                pool.wait_ge(summed[h], n * SG + SG)
                            index = net.index[:, :, :].rearrange("p a t -> p (a t)")[:, h * ST:(h + 1) * ST]
                            nc.gpsimd.tensor_copy(index, net.src_n[:, bass.ds(i * 2 * HALF + h * ST, ST)]
                                                  ).then_inc(index_ready[h], 1)
                            pool.wait_ge(index_ready[h], n + 1)
                            pool.sem_inc(moved, 1)
                            for t in range(ST):
                                pool.indirect_dma_start(
                                    rows3[h][:, t, :], None, table,
                                    bass.IndirectOffsetOnAxis(ap=index[:, t:t + 1], axis=0)
                                ).then_inc(gathered[h], 16)

        @block.sync
        def _(sp):
            if not (attention or edges):
                if follow:
                    follow.sync(sp)
                return
            if edges:
                sp.dma_start(net.src_n[:, :], net.DEALT[0]).then_inc(lists, 16)
                sp.dma_start(net.rel_n[:, :], net.DEALT[1]).then_inc(lists, 16)
                sp.wait_ge(cleared, 1)
            R = sp.value_load(net.rounds[0:1, 0:1], min_val=1, max_val=256)
            with sp.Fori(0, R) as r:
                with sp.Fori(0, NIT) as i:
                    n = sp.snap(r * NIT + i)
                    for h in range(2):
                        if attention:
                            sp.wait_ge(message[h], n + 1)
                            sp.dma_start(rows[h], net.G[bass.ds(i * 2 + h, 1), :, :]
                                         .rearrange("a p f -> (a p) f")).then_inc(gathered[h], 16)
                        else:
                            sp.wait_ge(summed[h], n * GPH + GPH)
                            lane = "(q p k) f -> p q (k f)"
                            slots = attr[h].rearrange("p (q f) -> p q f", q=GPH)
                            edge = net.dram["edge_attr_128"]
                            at = (2 * i + h) * HALF * TILE
                            sp.dma_start(slots[:, 0:2, :], edge[bass.ds(at, 2 * GE), :].rearrange(
                                lane, q=2, p=P)).then_inc(attr_loaded[h], 16)
                            if h == 0:
                                sp.dma_start(slots[:, 2:4, :], edge[bass.ds(at + 2 * GE, 2 * GE), :].rearrange(
                                    lane, q=2, p=P)).then_inc(attr_loaded[h], 16)
                                continue
                            with sp.If(i < NIT - 1):
                                more = nc.s_assert_within(at + 2 * GE, 0, E - 2 * GE)
                                sp.dma_start(slots[:, 2:4, :], edge[bass.ds(more, 2 * GE), :].rearrange(
                                    lane, q=2, p=P)).then_inc(attr_loaded[h], 16)
                            with sp.Else():
                                rest = E - (NGRP - 2) * GE
                                sp.dma_start(slots[0:rest // GT, 2, :], edge[E - rest:E, :].rearrange(
                                    "(p k) f -> p (k f)", k=GT)).then_inc(attr_loaded[h], 16)

        @block.tensor
        def _(pe):
            for h in range(S):
                pe.sem_inc(summed[h], SG)
            if follow:
                follow.tensor_begin(pe)
            R = pe.value_load(net.rounds[0:1, 0:1], min_val=1, max_val=256)
            with pe.Fori(0, R) as r:
                with pe.Fori(0, NIT) as i:
                    n = pe.snap(r * NIT + i)
                    for h in range(S):
                        pe.wait_ge(piled[h], n + 1)
                        if ready is gathered:
                            pe.wait_ge(gathered[h], n * 16 * ST + 16 * ST)
                        else:
                            pe.wait_ge(ready[h], n + (2 if ready is message else 1))
                        for q in range(SG):
                            pe.wait_ge(added, n * 2 * GPH + h * SG + q + 1 + 2 * GPH - NB)
                            for k in range(GT):
                                t = q * GT + k
                                last = nc.tensor.matmul(bank_of(h, q, 0),
                                                        msgs3[h][:, t, 0:D], onehot[:, h * ST + t, :],
                                                        start=(k == 0), stop=(k == GT - 1))
                            if extra:
                                if extra == "count":
                                    last = nc.tensor.matmul(bank_of(h, q, 1), net.ones[:, :],
                                                            piles[h][:, q * W:(q + 1) * W],
                                                            start=True, stop=True)
                                for k in range(0 if extra == "count" else GT):
                                    t = q * GT + k
                                    if edges:
                                        lhs = attr[h][:, t * D:(t + 1) * D]
                                    else:
                                        lhs = msgs3[h][:, t, D:D + H]
                                    last = nc.tensor.matmul(bank_of(h, q, 1),
                                                            lhs, onehot[:, h * ST + t, :],
                                                            start=(k == 0), stop=(k == GT - 1))
                            last.then_inc(summed[h], 1)
                    if follow:
                        with pe.If(i < NIT - 1):
                            due_chunks(net, pe, i, i + 1, lambda c: follow.tensor(pe, c))
            if follow:
                due_chunks(net, pe, NIT - 1, None, lambda c: follow.tensor(pe, c))

        @block.vector
        def _(dve):
            if not attention:
                nc.vector.memset(A[:, :], 0.0)
                if extra:
                    nc.vector.memset(Cc[:, 0:REG], 1.0 if extra == "count" else 0.0)
            if edges:
                nc.vector.memset(net.B[:, 0:2 * HALF * D], 0.0)
            nc.vector.tensor_copy(net.window[:, :], net.window0[:, :])
            nc.vector.tensor_copy(net.base_now[:, :], net.base[:, :]).then_inc(cleared, 1)
            dve.wait_ge(cleared, 1)
            if edges:
                dve.wait_ge(lists, 32)
            dve.sem_inc(added, 2 * GPH)
            if attention or edges:
                for h in range(S):
                    dve.sem_inc(message[h], 1)
            if follow:
                follow.vector_begin(dve)
            R = dve.value_load(net.rounds[0:1, 0:1], min_val=1, max_val=256)
            with dve.Fori(0, R) as r:
                def compare(i, h):
                    dve.wait_ge(summed[h], (r * NIT + i) * SG + SG)
                    nc.vector.tensor_tensor(
                        onehot[:, h * ST:(h + 1) * ST, :],
                        net.rel_n[:, bass.ds(i * 2 * HALF + h * ST, ST)].unsqueeze(2)
                        .broadcast_to([P, ST, W]),
                        net.window[:, :].unsqueeze(1).broadcast_to([P, ST, W]),
                        ALU.is_equal).then_inc(onehot_ready[h], 1)
                    if extra == "count":
                        dve.wait_ge(onehot_ready[h], r * NIT + i + 1)
                        nc.vector.tensor_reduce(
                            piles[h].rearrange("p (q w) -> p q w", w=W),
                            onehot[:, h * ST:(h + 1) * ST, :].rearrange("p (q k) w -> p q w k", k=GT),
                            AX_X, ALU.add).then_inc(piled[h], 1)

                def messages(i, h):
                    n = r * NIT + i
                    if attention:
                        dve.wait_ge(gathered[h], n * 16 + 16)
                        pr3 = net.B[:, bass.ds(i * 2 * HALF * H, 2 * HALF * H)].rearrange(
                            "p (h t) -> p t h", h=H)[:, h * HALF:(h + 1) * HALF, :]
                        by_head = lambda x: x[:, :, 0:D].rearrange("p t (h c) -> p t h c", h=H)
                        nc.vector.tensor_copy(msgs3[h][:, :, D:D + H], pr3)
                        nc.vector.tensor_tensor(by_head(msgs3[h]), by_head(rows3[h]),
                                                pr3.unsqueeze(3).broadcast_to([P, HALF, H, C]),
                                                ALU.mult).then_inc(message[h], 1)
                    elif edges:
                        dve.wait_ge(gathered[h], n * 16 * ST + 16 * ST)
                        dve.wait_ge(attr_loaded[h], n * 32 + 32)
                        nc.vector.tensor_tensor(msgs[h], rows[h], attr[h], ALU.add).then_inc(message[h], 1)

                def add(i, h):
                    n = r * NIT + i
                    for q in range(SG):
                        at = dve.value_load(net.base_now[0:1, bass.ds(i * 2 * GPH + h * SG + q, 1)],
                                            min_val=0, max_val=N)
                        dve.wait_ge(summed[h], n * SG + SG + q + 1)
                        dve.wait_ge(added, n * 2 * GPH + 2 * GPH + h * SG + q)
                        if extra:
                            nc.vector.tensor_tensor(Cc[0:high[1], bass.ds(at, W)], Cc[0:high[1], bass.ds(at, W)],
                                                    bank_of(h, q, 1),
                                                    ALU.add)
                        nc.vector.tensor_tensor(A[:, bass.ds(at, W)], A[:, bass.ds(at, W)],
                                                bank_of(h, q, 0), ALU.add
                                                ).then_inc(added, 1)

                def all_added(count):
                    dve.wait_ge(added, count + 2 * GPH)
                    dve.sem_inc(moved, 1)

                for h in range(S):
                    compare(0, h)
                    messages(0, h)
                with dve.Fori(0, NIT - 1) as i:
                    for h in range(S):
                        add(i, h)
                        if follow and h == S - 1:
                            due_chunks(net, dve, i, i + 1, lambda c: follow.vector(dve, c),
                                       lambda: all_added((r * NIT + i) * 2 * GPH + 2 * GPH))
                        compare(dve.snap(i + 1), h)
                        messages(dve.snap(i + 1), h)
                for h in range(S):
                    add(NIT - 1, h)
                nc.vector.tensor_scalar(net.window[:, :], net.window[:, :], float(W), None, ALU.add)
                nc.vector.tensor_scalar(net.base_now[:, :], net.base_now[:, :], float(W), float(N),
                                        ALU.add, ALU.min).then_inc(cleared, 1)
                dve.wait_ge(cleared, r + 2)
            if follow:
                due_chunks(net, dve, NIT - 1, None, lambda c: follow.vector(dve, c),
                           lambda: all_added(R * (NIT * 2 * GPH)))


class Sage:

    def __init__(self, net, tag, weight, bias, table, first=False):
        self.net, self.table, self.first = net, table, first
        self.weight, self.bias = net.dram[weight], net.dram[bias]
        self.w, self.b = net.wtmp[:, 0:2 * D], net.small[:, 0:1]
        self.last = net.small[0:1, 20:21]
        self.ends, self.count = net.wtmp[0:1, 512:512 + CH], net.wtmp[32:33, 512:512 + CH]
        s = lambda k: net.sem(f"{tag}_{k}")
        self.weights, self.scanned, self.counted = s("weights"), s("scanned"), s("counted")
        self.ends_free, self.ends_stored, self.counts_stored = s("ends_free"), s("ends_stored"), s("counts_stored")
        self.carried, self.inverse, self.mean, self.product = s("carried"), s("inverse"), s("mean"), s("product")
        self.h, self.brought, self.turned, self.rows = s("h"), s("brought"), s("turned"), s("rows")
        self.rows_free, self.stored = s("rows_free"), s("stored")

    def sync(self, sp):
        net = self.net
        sp.dma_start(self.w.rearrange("p (k n) -> p k n", k=2),
                     self.weight.rearrange("(k p) n -> p k n", k=2)).then_inc(self.weights, 16)
        sp.dma_start(self.b, self.bias.rearrange("(p a) -> p a", a=1)).then_inc(self.weights, 16)
        sp.sem_inc(self.rows_free, 1)
        sp.sem_inc(self.ends_free, 1)
        with sp.Fori(0, NCH) as c:
            if self.first:
                sp.wait_ge(self.counted, c + 1)
                sp.dma_start(net.CUM[0:1, bass.ds(c * CH, CH)], self.ends).then_inc(self.ends_stored, 16)
                sp.dma_start(net.CUM[1:2, bass.ds(c * CH, CH)], self.count).then_inc(self.counts_stored, 16)
                sp.wait_ge(self.ends_stored, c * 16 + 16)
                sp.wait_ge(self.counts_stored, c * 16 + 16)
                sp.sem_inc(self.ends_free, 1)
            store_rows(sp, self, c, self.table, D)

    def vector_begin(self, dve):
        if self.first:
            self.net.nc.vector.memset(self.last, 0.0).then_inc(self.scanned, 1)

    def vector(self, dve, c):
        net = self.net
        V = net.nc.vector
        if self.first:
            dve.wait_ge(self.ends_free, c + 1)
            dve.wait_ge(self.scanned, c + 1)
            V.tensor_copy(self.count, net.C[32:33, bass.ds(c * CH, CH)])
            V.tensor_tensor_scan(self.ends, net.C[0:1, bass.ds(c * CH, CH)],
                                 net.ones[0:1, 0:1].broadcast_to([1, CH]), self.last,
                                 ALU.add, ALU.subtract).then_inc(self.carried, 1)
            dve.wait_ge(self.carried, c + 1)
            V.tensor_copy(self.last, self.ends[:, CH - 1:CH]).then_inc(self.scanned, 1)
            dve.sem_inc(self.counted, 1)
            V.reciprocal(net.col(net.C, c), net.col(net.C, c)).then_inc(self.inverse, 1)
            dve.wait_ge(self.inverse, c + 1)
        V.tensor_tensor(net.col(net.A, c), net.col(net.A, c), net.col(net.C, c),
                        ALU.mult).then_inc(self.mean, 1)

    def tensor_begin(self, pe):
        pe.wait_ge(self.weights, 32)

    def tensor(self, pe, c):
        net = self.net
        pe.wait_ge(self.mean, c + 1)
        pe.wait_ge(self.brought, c + 1)
        net.nc.tensor.matmul(dense(net, 0), self.w[:, 0:D], net.col(net.B, c), start=True, stop=False)
        net.nc.tensor.matmul(dense(net, 0), self.w[:, D:2 * D], net.col(net.A, c),
                             start=False, stop=True).then_inc(self.product, 1)
        pe.wait_ge(self.brought, c + 2)
        turn_rows(net, pe, self, c)

    def scalar(self, act):
        net = self.net
        act.sem_inc(self.brought, 1)
        act.sem_inc(self.turned, 1)
        act.sem_inc(self.rows, 1)
        act.wait_ge(self.weights, 32)
        with act.Fori(0, NCH) as c:
            act.wait_ge(self.product, c + 1)
            act.wait_ge(self.turned, c + 1)
            net.nc.scalar.activation(net.turn[:, :], dense(net, 0), ACT.Relu, bias=self.b)
            net.nc.scalar.activation(net.col(net.B, c), dense(net, 0), ACT.Relu,
                                     bias=self.b).then_inc(self.brought, 1)
            copy_rows(net, act, self, c)



def dense(net, k, n=CH, high=P):
    return net.psum[0:high, (4 + k) * 512:(4 + k) * 512 + n]


def turn_rows(net, pe, f, c, k=3):
    pe.wait_ge(f.rows, c + 1)
    for j in range(4):
        t = net.nc.tensor.transpose(net.psum[0:SUB, (4 + k) * 512 + j * D:(4 + k) * 512 + (j + 1) * D],
                                    net.turn[:, j * SUB:(j + 1) * SUB], net.ident[:, :])
    t.then_inc(f.turned, 1)


def copy_rows(net, act, f, c, k=3):
    act.wait_ge(f.turned, c + 2)
    act.wait_ge(f.rows_free, c + 1)
    net.nc.scalar.copy(net.rows[0:SUB, 0:4 * D], dense(net, k, 4 * D, SUB)).then_inc(f.rows, 1)


def store_rows(sp, f, c, table, width):
    sp.wait_ge(f.rows, c + 2)
    sp.dma_start(table[bass.ds(c * CH, CH), :].rearrange("(t p) f -> p t f", p=SUB),
                 f.net.rows[0:SUB, 0:4 * width].rearrange("p (t f) -> p t f", f=width)
                 ).then_inc(f.stored, 16)
    sp.wait_ge(f.stored, c * 16 + 16)
    sp.sem_inc(f.rows_free, 1)


class Project:

    def __init__(self, net, tag):
        self.net = net
        s = lambda k: net.sem(f"{tag}_{k}")
        self.weights, self.masked, self.w_turned, self.select = s("weights"), s("masked"), s("w_turned"), s("select")
        self.w_ready, self.att_done, self.joined, self.average = s("w_ready"), s("att_done"), s("joined"), s("average")
        self.product, self.y, self.x_loaded, self.x = s("product"), s("y"), s("x_loaded"), s("x")
        self.x_saved, self.mean1, self.centred1, self.squared1 = s("x_saved"), s("mean1"), s("centred1"), s("squared1")
        self.var1, self.dev1, self.inverse1, self.h = s("var1"), s("dev1"), s("inverse1"), s("h")
        self.h_saved, self.mean2, self.centred2, self.squared2 = s("h_saved"), s("mean2"), s("centred2"), s("squared2")
        self.var2, self.dev2, self.inverse2, self.scaled = s("var2"), s("dev2"), s("inverse2"), s("scaled")
        self.brought, self.turned, self.rows, self.rows_free = s("brought"), s("turned"), s("rows"), s("rows_free")
        self.stored, self.carried = s("stored"), s("carried")
        self.ws, self.bs = net.wtmp[:, 0:2 * D], net.small[:, 5:6]
        self.w = net.wtmp[:, 264:264 + XW]
        self.wt = net.wtmp[:, 400:400 + D]
        self.att = net.wtmp[:, 528:528 + 2 * H]
        self.mask = net.wtmp[:, 536:536 + H]
        self.gain, self.shift = net.small[:, 0:1], net.small[:, 1:2]
        self.a_s, self.a_d = net.small[:, 2:3], net.small[:, 3:4]

    def sync(self, sp):
        net = self.net
        sp.dma_start(self.ws.rearrange("p (k n) -> p k n", k=2),
                     net.dram["L0_gnn_W2"].rearrange("(k p) n -> p k n", k=2)).then_inc(self.weights, 16)
        sp.dma_start(self.w[:, 0:D], net.dram["L1_gnn_W"]).then_inc(self.weights, 16)
        for to, name in ((self.bs, "L0_gnn_b2"), (self.gain, "L1_gnn_ln1_g"), (self.shift, "L1_gnn_ln1_b")):
            sp.dma_start(to, net.dram[name].rearrange("(p a) -> p a", a=1)).then_inc(self.weights, 16)
        for to, name in ((self.a_s, "L1_gnn_att_src"), (self.a_d, "L1_gnn_att_dst")):
            sp.dma_start(to, net.dram[name].rearrange("h (c a) -> (h c) a", a=1)).then_inc(self.weights, 16)
        sp.sem_inc(self.rows_free, 1)
        with sp.Fori(0, NCH) as c:
            at = sp.snap(c * CH)
            sp.wait_ge(self.average, c + 1)
            sp.dma_start(net.C[:, bass.ds(at, CH)], net.XT[:, bass.ds(at, CH)]).then_inc(self.x_loaded, 16)
            sp.wait_ge(self.x, c + 1)
            sp.sem_inc(self.carried, 1)
            sp.dma_start(net.XT[:, bass.ds(at, CH)], net.B[:, bass.ds(at, CH)]).then_inc(self.x_saved, 16)
            sp.wait_ge(self.h, c + 1)
            sp.dma_start(net.HT[:, bass.ds(at, CH)], net.B[:, bass.ds(at, CH)]).then_inc(self.h_saved, 16)
            sp.wait_ge(self.h_saved, c * 16 + 16)
            sp.sem_inc(self.carried, 1)
            store_rows(sp, self, c, net.XH, XW)

    def vector_begin(self, dve):
        V, net = self.net.nc.vector, self.net
        V.memset(self.mask, 0.0).then_inc(self.masked, 1)
        dve.wait_ge(self.masked, 1)
        for h in range(H):
            V.memset(self.mask[h * C:(h + 1) * C, h:h + 1], 1.0).then_inc(self.masked, 1)
        dve.wait_ge(self.masked, 1 + H)
        dve.wait_ge(self.weights, 112)
        V.tensor_scalar(self.att[:, 0:H], self.mask, self.a_s, None, ALU.mult)
        V.tensor_scalar(self.att[:, H:2 * H], self.mask, self.a_d, None, ALU.mult)
        dve.wait_ge(self.w_turned, 1)
        V.tensor_copy(self.wt, dense(net, 0, D)).then_inc(self.w_ready, 1)
        dve.wait_ge(self.select, 1)
        V.tensor_copy(head_select(net), dense(net, 1, D, H))
        dve.wait_ge(self.att_done, 1)
        V.tensor_copy(self.w[:, D:XW], dense(net, 2, 2 * H)).then_inc(self.joined, 1)

    def vector(self, dve, c):
        net = self.net
        V, A, B, Cc = net.nc.vector, net.col(net.A, c), net.col(net.B, c), net.col(net.C, c)
        V.tensor_tensor(A, A, Cc, ALU.mult).then_inc(self.average, 1)
        dve.wait_ge(self.y, c + 1)
        dve.wait_ge(self.x_loaded, c * 16 + 16)
        V.tensor_tensor(B, B, Cc, ALU.add).then_inc(self.x, 1)
        dve.wait_ge(self.mean1, c + 1)
        V.tensor_tensor(Cc, B, dense(net, 1), ALU.subtract).then_inc(self.centred1, 1)
        dve.wait_ge(self.dev1, c + 1)
        dve.wait_ge(self.x_saved, c * 16 + 16)
        dve.sem_inc(self.carried, 1)
        V.reciprocal(A, A).then_inc(self.inverse1, 1)
        dve.wait_ge(self.inverse1, c + 1)
        V.scalar_tensor_tensor(out=B, in0=Cc, scalar=0.0, in1=A, op0=ALU.max, op1=ALU.mult).then_inc(self.h, 1)
        dve.wait_ge(self.mean2, c + 1)
        V.tensor_tensor(Cc, B, dense(net, 1), ALU.subtract).then_inc(self.centred2, 1)
        dve.wait_ge(self.dev2, c + 1)
        dve.sem_inc(self.carried, 1)
        V.reciprocal(A, A).then_inc(self.inverse2, 1)
        dve.wait_ge(self.inverse2, c + 1)
        V.tensor_tensor(A, Cc, A, ALU.mult).then_inc(self.scaled, 1)

    def tensor_begin(self, pe):
        T, net = self.net.nc.tensor, self.net
        pe.wait_ge(self.weights, 112)
        T.transpose(dense(net, 0, D), self.w[:, 0:D], net.ident[:, :]).then_inc(self.w_turned, 1)
        pe.wait_ge(self.masked, 1 + H)
        T.transpose(dense(net, 1, D, H), self.mask, net.ident[:, :]).then_inc(self.select, 1)
        pe.wait_ge(self.w_ready, 1)
        T.matmul(dense(net, 2, 2 * H), self.wt, self.att, start=True, stop=True).then_inc(self.att_done, 1)
        pe.wait_ge(self.joined, 1)

    def tensor(self, pe, c):
        net = self.net
        T, A, B = net.nc.tensor, net.col(net.A, c), net.col(net.B, c)
        pe.wait_ge(self.average, c + 1)
        pe.wait_ge(self.rows, c + 1)
        T.matmul(dense(net, 0), self.ws[:, 0:D], B, start=True, stop=False)
        T.matmul(dense(net, 0), self.ws[:, D:2 * D], A, start=False, stop=True).then_inc(self.product, 1)
        for operand, result, mean, squared, var in ((self.x, 1, self.mean1, self.squared1, self.var1),
                                                    (self.h, 1, self.mean2, self.squared2, self.var2)):
            pe.wait_ge(operand, c + 1)
            T.matmul(dense(net, 1), net.mean_w[:, :], B, start=True, stop=True).then_inc(mean, 1)
            pe.wait_ge(squared, c + 1)
            T.matmul(dense(net, 2), net.mean_w[:, :], A, start=True, stop=True).then_inc(var, 1)
        pe.wait_ge(self.brought, c + 1)
        for j in range(4):
            bank = 4 + j // 2 * 3
            m = T.matmul(net.psum[0:SUB, bank * 512 + j % 2 * XW:bank * 512 + (j % 2 + 1) * XW],
                         net.turn[:, j * SUB:(j + 1) * SUB], self.w, start=True, stop=True)
        m.then_inc(self.turned, 1)

    def scalar(self, act):
        net = self.net
        S = net.nc.scalar
        act.sem_inc(self.turned, 1)
        act.sem_inc(self.rows, 1)
        act.wait_ge(self.weights, 112)
        with act.Fori(0, NCH) as c:
            act.wait_ge(self.product, c + 1)
            S.activation(net.col(net.B, c), dense(net, 0), ACT.Relu, bias=self.bs).then_inc(self.y, 1)
            for centred, squared, var, dev in ((self.centred1, self.squared1, self.var1, self.dev1),
                                               (self.centred2, self.squared2, self.var2, self.dev2)):
                act.wait_ge(centred, c + 1)
                act.sem_inc(self.carried, 1)
                S.activation(net.col(net.A, c), net.col(net.C, c), ACT.Square).then_inc(squared, 1)
                act.wait_ge(var, c + 1)
                act.sem_inc(self.carried, 1)
                S.activation(net.col(net.A, c), dense(net, 2), ACT.Sqrt, bias=net.eps[:, 0:1]).then_inc(dev, 1)
            act.wait_ge(self.scaled, c + 1)
            act.wait_ge(self.turned, c + 1)
            act.sem_inc(self.carried, 1)
            S.activation(net.turn[:, :], net.col(net.A, c), ACT.Identity, bias=self.shift, scale=self.gain)
            S.activation(net.col(net.A, c), net.col(net.A, c), ACT.Identity, bias=self.shift, scale=self.gain).then_inc(self.brought, 1)
            act.wait_ge(self.turned, c + 2)
            act.wait_ge(self.rows_free, c + 1)
            S.copy(net.rows[0:SUB, 0:2 * XW], dense(net, 0, 2 * XW, SUB))
            S.copy(net.rows[0:SUB, 2 * XW:4 * XW], dense(net, 3, 2 * XW, SUB)).then_inc(self.rows, 1)


def gat_gather(net):
    nc = net.nc
    rows = [net.work[:, h * HALF * XW:(h + 1) * HALF * XW] for h in range(2)]
    rows3 = [r.rearrange("p (t f) -> p t f", f=XW) for r in rows]
    name = lambda k: [net.sem(f"gg_{k}{h}") for h in range(2)]
    index_ready, stored, free, copied = name("index"), name("stored"), name("free"), name("copied")
    gathered = [net.pool_sem(), net.pool_sem()]
    moved, own = net.sem("gg_moved"), net.sem("gg_own")

    with nc.Block() as block:
        @block.gpsimd
        def _(pool):
            with pool.Fori(0, NIT) as i:
                for h in range(2):
                    pool.wait_ge(free[h], i + 1)
                    pool.wait_ge(copied[h], i + 1)
                    nc.gpsimd.tensor_copy(net.index[:, h, :],
                                          net.src_n[:, bass.ds(i * 2 * HALF + h * HALF, HALF)]
                                          ).then_inc(index_ready[h], 1)
                    pool.wait_ge(index_ready[h], i + 1)
                    pool.sem_inc(moved, 1)
                    for t in range(HALF):
                        pool.indirect_dma_start(
                            rows3[h][:, t, :], None, net.XH,
                            bass.IndirectOffsetOnAxis(ap=net.index[:, h, t:t + 1], axis=0)
                        ).then_inc(gathered[h], 16)

        @block.sync
        def _(sp):
            sp.dma_start(net.onehot[0:SUB, :, :, :].rearrange("p a t w -> p (a t w)")[:, 0:NSUB * 2 * H]
                         .rearrange("p (t f) -> p t f", f=2 * H),
                         net.XH[:, D:XW].rearrange("(t p) f -> p t f", p=SUB)).then_inc(own, 16)
            for h in range(2):
                sp.sem_inc(free[h], 1)
            with sp.Fori(0, NIT) as i:
                for h in range(2):
                    sp.wait_ge(gathered[h], i * 256 + 256)
                    sp.dma_start(net.G[bass.ds(i * 2 + h, 1), :, :].rearrange("a p f -> (a p) f"),
                                 rows[h]).then_inc(stored[h], 16)
                    sp.wait_ge(stored[h], i * 16 + 16)
                    sp.sem_inc(free[h], 1)
            sp.wait_ge(own, 16)

        @block.scalar
        def _(act):
            for h in range(2):
                act.sem_inc(copied[h], 1)
            with act.Fori(0, NIT) as i:
                for h in range(2):
                    act.wait_ge(gathered[h], i * 256 + 256)
                    nc.scalar.copy(
                        net.B[:, bass.ds(i * 2 * HALF * H, 2 * HALF * H)].rearrange(
                            "p (h t) -> p h t", h=H)[:, :, h * HALF:(h + 1) * HALF],
                        rows3[h][:, :, D:D + H].rearrange("p t h -> p h t")).then_inc(copied[h], 1)


def gat_softmax(net):
    nc = net.nc
    B, Cc = net.B, net.C
    SEG = 4 * EPP
    turned_rows = Cc[:, 0:SEG]
    score = Cc[:, SEG:2 * SEG].rearrange("p (h k) -> p h k", h=H)
    trial = Cc[:, 0:SEG].rearrange("p (h k) -> p h k", h=H)
    running = Cc[:, 0:SEG].rearrange("p (k h) -> p k h", h=H)
    dst = net.work[:, 1024:1024 + EPP]
    flag = net.work[:, 1024 + EPP:1024 + 2 * EPP]
    scratch = net.onehot[:, :, :, :].rearrange("p a t w -> p (a t w)")
    a_own = scratch[0:SUB, 0:NSUB * 2 * H].rearrange("p (t f) -> p t f", f=2 * H)
    ends3 = scratch[0:H, 800:800 + 3 * P]
    e_first, e_last, e_max = (ends3[:, k * P:(k + 1) * P] for k in range(3))
    before, value = scratch[0:H, 1184:1184 + P], scratch[0:H, 1312:1312 + P]
    joins, single = scratch[0:H, 1440:1440 + P - 1], scratch[0:H, 1568:1568 + P - 1]
    carry_row = scratch[0:H, 1696:1696 + P]
    first4, last4, max4 = (net.small[:, 24 + 4 * k:28 + 4 * k] for k in range(3))
    carry = net.small[:, 36:40]
    fix_i = net.small[:, 40:41].bitcast(I32)
    fix = net.small[:, 48:56]
    at = [Cc[0:SUB, k * NSUB:(k + 1) * NSUB] for k in range(8)]
    ends, counts, some, node, pos = at[0], at[1], at[2], at[3], at[4]
    last_i, start_i, node_i = (at[k].bitcast(I32) for k in (5, 6, 7))
    four = lambda k: Cc[0:SUB, 800 + k * 400:1200 + k * 400].rearrange("p (t h) -> p t h", h=H)
    found, peak, own = four(0), four(1), four(2)
    values = Cc[0:SUB, 2000:2800].rearrange("p (t f) -> p t f", f=2 * H)
    wide = lambda a: a.unsqueeze(2).broadcast_to([SUB, NSUB, H])
    BATCH = 10
    idx10 = net.small[0:SUB, 60:60 + BATCH].bitcast(I32)
    got10 = net.small[0:SUB, 72:72 + BATCH * H]
    put10 = net.work[0:SUB, 0:BATCH * 2 * H]
    p_self = net.p_self[:, :].rearrange("p (t h) -> p t h", h=H)

    s = {k: net.sem(f"gs_{k}") for k in
         ("brought", "turned", "copied", "by_head", "loaded", "dve", "ends", "carried", "stored",
          "positions", "index", "go", "kept", "values", "put_ready", "fix_ready",
          "starts", "exps", "exps_stored", "rows_loaded", "brought2", "turned2", "copied2")}
    s.update(found=net.pool_sem(), put=net.pool_sem(), fixed=net.pool_sem())
    v = [0]

    with nc.Block() as block:
        @block.gpsimd
        def _(pool):
            pool.iota(node_like(net), pattern=[[SUB, NSUB]], base=0, channel_multiplier=1).then_inc(s["go"], 1)
            pool.sem_inc(s["turned"], 2)

            def bring(c, k):
                pool.wait_ge(s["turned"], c + 1)
                nc.gpsimd.tensor_copy(slot(net, k, P), B[:, bass.ds(c * P, P)]).then_inc(s["brought"], 1)
            each_chunk(pool, bring, NIT)
            pool.wait_ge(s["positions"], 1)
            pool.wait_ge(s["stored"], 16)
            with pool.Fori(0, NSUB // BATCH) as i:
                pool.wait_ge(s["kept"], i + 1)
                nc.gpsimd.tensor_copy(idx10, last_i[:, bass.ds(i * BATCH, BATCH)]).then_inc(s["index"], 1)
                pool.wait_ge(s["index"], i + 1)
                pool.sem_inc(s["go"], 1)
                for t in range(BATCH):
                    pool.indirect_dma_start(
                        got10[:, t * H:(t + 1) * H], None, net.FD,
                        bass.IndirectOffsetOnAxis(ap=idx10[:, t:t + 1], axis=0)).then_inc(s["found"], 16)
            pool.wait_ge(s["kept"], NSUB // BATCH + 1)
            with pool.Fori(0, NSUB // BATCH) as i:
                nc.gpsimd.tensor_copy(idx10, start_i[:, bass.ds(i * BATCH, BATCH)]).then_inc(s["index"], 1)
                pool.wait_ge(s["index"], i + 1 + NSUB // BATCH)
                pool.wait_ge(s["put_ready"], i + 1)
                pool.sem_inc(s["go"], 1)
                for t in range(BATCH):
                    pool.indirect_dma_start(
                        net.SC, bass.IndirectOffsetOnAxis(ap=idx10[:, t:t + 1], axis=0),
                        put10[:, t * 2 * H:(t + 1) * 2 * H], None).then_inc(s["put"], 16)
                pool.wait_ge(s["put"], i * 16 * BATCH + 16 * BATCH)
            pool.wait_ge(s["values"], 16)
            pool.wait_ge(s["fix_ready"], 1)
            pool.indirect_dma_start(fix, None, net.NV, bass.IndirectOffsetOnAxis(ap=fix_i, axis=0)
                                    ).then_inc(s["fixed"], 16)
            pool.sem_inc(s["turned2"], 2)
            pool.wait_ge(s["rows_loaded"], 16 * H)

            def back(c, k):
                pool.wait_ge(s["turned2"], c + 1)
                nc.gpsimd.tensor_copy(slot(net, k, P), turned_rows[:, bass.ds(c * P, P)]
                                      ).then_inc(s["brought2"], 1)
            each_chunk(pool, back, NIT)

        @block.tensor
        def _(pe):
            def turn(c, k):
                pe.wait_ge(s["brought"], c + 1)
                pe.wait_ge(s["copied"], c + 1)
                nc.tensor.transpose(net.psum[:, k * 512:k * 512 + P], slot(net, k, P),
                                    net.ident[:, :]).then_inc(s["turned"], 1)
            each_chunk(pe, turn, NIT)
            pe.wait_ge(s["ends"], 1)
            for k, x in enumerate((first4, last4, max4)):
                t = nc.tensor.transpose(net.psum[0:H, 1024 + k * P:1024 + (k + 1) * P], x, net.ident[:, :])
            t.then_inc(s["carried"], 1)
            pe.wait_ge(s["ends"], 2)
            nc.tensor.transpose(net.psum[:, 1536:1536 + H], carry_row, net.ident[0:H, 0:H]
                                ).then_inc(s["carried"], 1)

            def turn2(c, k):
                pe.wait_ge(s["brought2"], c + 1)
                pe.wait_ge(s["copied2"], c + 1)
                nc.tensor.transpose(net.psum[:, k * 512:k * 512 + P], slot(net, k, P),
                                    net.ident[:, :]).then_inc(s["turned2"], 1)
            each_chunk(pe, turn2, NIT)

        @block.scalar
        def _(act):
            act.sem_inc(s["copied"], 2)

            def out(c, k):
                act.wait_ge(s["turned"], c + 3)
                nc.scalar.copy(turned_rows[:, bass.ds(c * P, P)], net.psum[:, k * 512:k * 512 + P]
                               ).then_inc(s["copied"], 1)
            each_chunk(act, out, NIT)
            act.sem_inc(s["copied2"], 2)
            act.wait_ge(s["fixed"], 16)

            def out2(c, k):
                act.wait_ge(s["turned2"], c + 3)
                nc.scalar.copy(B[:, bass.ds(c * P, P)], net.psum[:, k * 512:k * 512 + P]
                               ).then_inc(s["copied2"], 1)
            act.wait_ge(s["exps"], 2)
            nc.scalar.activation(p_self, own, ACT.Exp).then_inc(s["exps"], 1)
            nc.scalar.activation(Cc[:, SEG:2 * SEG], Cc[:, SEG:2 * SEG], ACT.Exp).then_inc(s["exps"], 1)
            each_chunk(act, out2, NIT)

        @block.sync
        def _(sp):
            sp.wait_ge(s["copied"], NIT + 2)
            for h in range(H):
                sp.dma_start(net.SH[h, :].rearrange("(b t e) -> t b e", t=2 * HALF, e=TILE),
                             turned_rows[h * 2 * HALF:(h + 1) * 2 * HALF, :]
                             .rearrange("t (b e) -> t b e", e=TILE)).then_inc(s["by_head"], 16)
            sp.dma_start(dst, net.DST.rearrange("(p k) -> p k", p=P)).then_inc(s["loaded"], 16)
            sp.wait_ge(s["by_head"], 16 * H)
            sp.dma_start(score, net.SH.rearrange("h (p k) -> p h k", p=P)).then_inc(s["loaded"], 16)
            sp.wait_ge(s["ends"], 3)
            sp.dma_start(net.FD.rearrange("(p k) h -> p (k h)", p=P), Cc[:, 0:SEG]).then_inc(s["stored"], 16)
            sp.wait_ge(s["stored"], 16)
            with nc.allow_non_contiguous_dma(reason="one node per element"):
                for k, x in enumerate((ends, counts)):
                    sp.dma_start(x, net.CUM[k, :].rearrange("(t p) -> p t", p=SUB),
                                 allow_slow_non_contiguous=True).then_inc(s["loaded"], 16)
            sp.wait_ge(s["ends"], 4)
            sp.dma_start(net.NV.rearrange("(t p) f -> p t f", p=SUB), values).then_inc(s["values"], 16)
            sp.wait_ge(s["put"], 16 * NSUB)
            sp.dma_start(B[:, 0:EPP * 2 * H], net.SC[0:EP, :].rearrange("(p k) f -> p (k f)", p=P)
                         ).then_inc(s["starts"], 16)
            sp.wait_ge(s["exps"], 4)
            sp.dma_start(net.PH.rearrange("h (p k) -> p h k", p=P), score).then_inc(s["exps_stored"], 16)
            sp.wait_ge(s["exps_stored"], 16)
            for h in range(H):
                sp.dma_start(turned_rows[h * 2 * HALF:(h + 1) * 2 * HALF, :].rearrange("t (b e) -> t b e", e=TILE),
                             net.PH[h, :].rearrange("(b t e) -> t b e", t=2 * HALF, e=TILE)
                             ).then_inc(s["rows_loaded"], 16)

        @block.vector
        def _(dve):
            def done(ins):
                v[0] += 1
                ins.then_inc(s["dve"], 1)
                dve.wait_ge(s["dve"], v[0])

            V = nc.vector
            dve.wait_ge(s["loaded"], 32)
            done(V.tensor_tensor(flag[:, 1:], dst[:, 1:], dst[:, 0:EPP - 1], ALU.is_equal))
            done(V.tensor_scalar(flag[:, 1:], flag[:, 1:], -1.0, BIG, ALU.add, ALU.mult))
            done(V.memset(flag[:, 0:1], 0.0))
            for h in range(H):
                done(V.tensor_tensor_scan(trial[:, h, :], flag, score[:, h, :], -BIG, ALU.add, ALU.max))
            done(V.tensor_copy(first4, dst[:, 0:1].broadcast_to([P, H])))
            done(V.tensor_copy(last4, dst[:, EPP - 1:EPP].broadcast_to([P, H])))
            V.tensor_copy(max4, trial[:, :, EPP - 1]).then_inc(s["ends"], 1)
            dve.wait_ge(s["carried"], 1)
            done(V.tensor_copy(ends3, net.psum[0:H, 1024:1024 + 3 * P]))
            done(V.memset(before, -BIG))
            done(V.memset(value, -BIG))
            for out, a in ((joins, e_first[:, 1:]), (single, e_first[:, 0:P - 1])):
                done(V.tensor_tensor(out, a, e_last[:, 0:P - 1], ALU.is_equal))
                done(V.tensor_scalar(out, out, -1.0, BIG, ALU.add, ALU.mult))
            done(V.tensor_tensor(before[:, 1:], joins, single, ALU.add))
            done(V.tensor_tensor(value[:, 1:], joins, e_max[:, 0:P - 1], ALU.add))
            V.tensor_tensor_scan(carry_row, before, value, -BIG, ALU.add, ALU.max).then_inc(s["ends"], 1)
            dve.wait_ge(s["carried"], 2)
            done(V.tensor_copy(carry, net.psum[:, 1536:1536 + H]))
            for h in range(H):
                done(V.tensor_tensor_scan(running[:, :, h], flag, score[:, h, :], carry[:, h:h + 1],
                                          ALU.add, ALU.max))
            dve.sem_inc(s["ends"], 1)
            dve.wait_ge(s["loaded"], 64)
            done(V.tensor_scalar(counts, counts, -1.0, None, ALU.add))
            done(V.tensor_scalar(pos, ends, -1.0, 0.0, ALU.add, ALU.max))
            done(V.tensor_copy(last_i, pos))
            done(V.tensor_scalar(some, counts, 0.0, None, ALU.is_gt))
            done(V.tensor_tensor(ends, ends, counts, ALU.subtract))
            done(V.tensor_copy(node, node_like(net)))
            done(V.tensor_scalar(node, node, float(EP), None, ALU.add))
            done(V.tensor_tensor(ends, ends, node, ALU.subtract))
            done(V.tensor_tensor(ends, ends, some, ALU.mult))
            done(V.tensor_tensor(ends, ends, node, ALU.add))
            done(V.tensor_copy(start_i, ends))
            dve.sem_inc(s["positions"], 1)
            dve.sem_inc(s["kept"], 1)
            with dve.Fori(0, NSUB // BATCH) as i:
                dve.wait_ge(s["found"], i * 16 * BATCH + 16 * BATCH)
                V.tensor_copy(Cc[0:SUB, bass.ds(i * BATCH * H + 800, BATCH * H)], got10).then_inc(s["kept"], 1)
            dve.wait_ge(s["kept"], NSUB // BATCH + 1)
            a_src, a_dst = a_own[:, :, 0:H], a_own[:, :, H:2 * H]
            done(V.tensor_tensor(found, found, wide(some), ALU.mult))
            done(V.tensor_scalar(some, some, -1.0, BIG, ALU.add, ALU.mult))
            done(V.tensor_tensor(found, found, wide(some), ALU.add))
            done(V.tensor_tensor(found, found, a_src, ALU.max))
            done(V.tensor_tensor(found, found, a_dst, ALU.add))
            done(V.scalar_tensor_tensor(out=peak, in0=found, scalar=0.2, in1=found, op0=ALU.mult, op1=ALU.max))
            done(V.tensor_tensor(own, a_src, a_dst, ALU.add))
            done(V.scalar_tensor_tensor(out=own, in0=own, scalar=0.2, in1=own, op0=ALU.mult, op1=ALU.max))
            done(V.tensor_tensor(own, own, peak, ALU.subtract))
            done(V.tensor_copy(values[:, :, 0:H], a_dst))
            done(V.tensor_copy(values[:, :, H:2 * H], peak))
            dve.sem_inc(s["ends"], 1)
            dve.sem_inc(s["exps"], 1)
            with dve.Fori(0, NSUB // BATCH) as i:
                dve.wait_ge(s["put"], i * 16 * BATCH) if False else None
                dve.wait_ge(s["index"], i + 1 + NSUB // BATCH)
                V.tensor_copy(put10, Cc[0:SUB, bass.ds(i * BATCH * 2 * H + 2000, BATCH * 2 * H)]
                              ).then_inc(s["put_ready"], 1)
            done(V.tensor_copy(fix_i, dst[:, 0:1]))
            dve.sem_inc(s["fix_ready"], 1)
            done(V.tensor_tensor(flag[:, 1:], dst[:, 1:], dst[:, 0:EPP - 1], ALU.is_equal))
            spread = B[:, 0:EPP * 2 * H].rearrange("p (k f) -> p k f", f=2 * H)
            dve.wait_ge(s["starts"], 16)
            dve.wait_ge(s["fixed"], 16)
            done(V.tensor_copy(spread[:, 0, :], fix))
            for f in range(2 * H):
                done(V.tensor_tensor_scan(spread[:, :, f], flag, spread[:, :, f], 0.0, ALU.mult, ALU.add))
            sp_dst = spread[:, :, 0:H].rearrange("p k h -> p h k")
            sp_max = spread[:, :, H:2 * H].rearrange("p k h -> p h k")
            done(V.tensor_tensor(score, score, sp_dst, ALU.add))
            done(V.scalar_tensor_tensor(out=score, in0=score, scalar=0.2, in1=score, op0=ALU.mult, op1=ALU.max))
            done(V.tensor_tensor(score, score, sp_max, ALU.subtract))
            done(V.tensor_scalar(score, score, 0.0, None, ALU.min))
            dve.sem_inc(s["exps"], 1)


def node_like(net):
    return net.wtmp[0:SUB, 700:700 + NSUB].bitcast(I32)


def head_select(net):
    return net.wtmp[0:H, 540:540 + D]


def gat_begin(net):
    nc = net.nc
    A, Cc = net.A, net.C
    s = {k: net.sem(f"gb_{k}") for k in ("brought", "used", "spread", "product", "begun")}

    with nc.Block() as block:
        @block.gpsimd
        def _(pool):
            pool.sem_inc(s["used"], 2)

            def bring(c, k):
                pool.wait_ge(s["used"], c + 1)
                own = net.p_self[:, bass.ds(c * 4 * H, 4 * H)]
                nc.gpsimd.tensor_copy(net.work[0:SUB, 1024 + k * 4 * H:1024 + (k + 1) * 4 * H], own)
                nc.gpsimd.tensor_copy(net.work[0:SUB, k * 512:(k + 1) * 512].rearrange("p (t c) -> p t c", c=C),
                                      own.unsqueeze(2).broadcast_to([SUB, 4 * H, C])).then_inc(s["brought"], 1)
            each_chunk(pool, bring)

        @block.tensor
        def _(pe):
            def products(c, k):
                pe.wait_ge(s["brought"], c + 1)
                pe.wait_ge(s["begun"], c + 1)
                nc.tensor.matmul(net.bank(2, c), net.wtmp[:, 264:264 + D], net.col(A, c), start=True, stop=True)
                for j in range(4):
                    m = nc.tensor.matmul(
                        net.psum[:, k * 512 + j * SUB:k * 512 + (j + 1) * SUB],
                        net.work[0:SUB, k * 512 + j * D:k * 512 + (j + 1) * D],
                        net.ident[0:SUB, 0:SUB], start=True, stop=True)
                for j in range(4):
                    m = nc.tensor.matmul(
                        net.psum[0:H, (4 + k) * 512 + j * SUB:(4 + k) * 512 + (j + 1) * SUB],
                        net.work[0:SUB, 1024 + (4 * k + j) * H:1024 + (4 * k + j + 1) * H],
                        net.ident[0:SUB, 0:SUB], start=True, stop=True)
                m.then_inc(s["used"], 1)
            each_chunk(pe, products)

        @block.scalar
        def _(act):
            with act.Fori(0, NCH) as c:
                act.wait_ge(s["used"], c + 3)
                nc.scalar.copy(net.work[:, bass.ds((c % 2) * 512 + 1536, CH)], net.bank(0, c))
                nc.scalar.copy(Cc[0:H, bass.ds(c * CH, CH)],
                               net.psum[0:H, bass.ds((c % 2) * 512 + 4 * 512, CH)]).then_inc(s["spread"], 1)

        @block.vector
        def _(dve):
            nc.vector.memset(A[:, N:REG], 0.0)
            nc.vector.memset(Cc[:, N:REG], 1.0)
            dve.sem_inc(s["begun"], 2)
            with dve.Fori(0, NCH) as c:
                dve.wait_ge(s["spread"], c + 1)
                nc.vector.tensor_tensor(net.col(A, c), net.bank(2, c),
                                        net.work[:, bass.ds((c % 2) * 512 + 1536, CH)],
                                        ALU.mult).then_inc(s["begun"], 1)


def gat_output(net):
    nc = net.nc
    A, B, Cc = net.A, net.B, net.C
    w1, w2 = net.wtmp[:, 0:2 * D], net.wtmp[:, 2 * D:4 * D]
    gain, bias, gat_b, b1, b2 = (net.small[:, 0:1], net.small[:, 1:2], net.small[:, 2:3],
                                 net.small[:, 4:6], net.small[:, 3:4])
    s = {k: net.sem(f"go_{k}") for k in
         ("weights", "h", "spread", "inverse", "ratio", "sum", "mean", "centred", "squared", "var", "dev",
          "carried", "inverse2", "scaled", "normed", "up", "gelu", "down", "out")}
    hidden = [net.work[:, k * 1024:(k + 1) * 1024] for k in range(2)]

    with nc.Block() as block:
        @block.sync
        def _(sp):
            sp.dma_start(B[:, 0:N], net.HT).then_inc(s["h"], 16)
            sp.dma_start(w1, net.dram["L1_gnn_w1"]).then_inc(s["weights"], 16)
            sp.dma_start(w2.rearrange("p (k n) -> p k n", k=2),
                         net.dram["L1_gnn_w2"].rearrange("(k p) n -> p k n", k=2)).then_inc(s["weights"], 16)
            for to, name in ((gain, "L1_gnn_ln2_g"), (bias, "L1_gnn_ln2_b"), (gat_b, "L1_gnn_gat_b"),
                             (b2, "L1_gnn_b2")):
                sp.dma_start(to, net.dram[name].rearrange("(p a) -> p a", a=1)).then_inc(s["weights"], 16)
            for k in range(2):
                sp.dma_start(b1[:, k:k + 1], net.dram["L1_gnn_b1"][k * D:(k + 1) * D]
                             .rearrange("(p a) -> p a", a=1)).then_inc(s["weights"], 16)

        @block.tensor
        def _(pe):
            with pe.Fori(0, NCH) as c:
                pe.wait_ge(s["inverse"], c + 1)
                nc.tensor.matmul(net.bank(0, c), head_select(net), Cc[0:H, bass.ds(c * CH, CH)],
                                 start=True, stop=True).then_inc(s["spread"], 1)
            with pe.Fori(0, NCH) as c:
                pe.wait_ge(s["sum"], c + 1)
                pe.wait_ge(s["centred"], c + 1)
                nc.tensor.matmul(net.bank(2, c), net.mean_w[:, :], net.col(B, c),
                                 start=True, stop=True).then_inc(s["mean"], 1)
            with pe.Fori(0, NCH) as c:
                pe.wait_ge(s["squared"], c + 1)
                pe.wait_ge(s["dev"], c + 1)
                nc.tensor.matmul(net.bank(4, c), net.mean_w[:, :], net.col(A, c),
                                 start=True, stop=True).then_inc(s["var"], 1)
            pe.wait_ge(s["centred"], NCH + 2)
            pe.wait_ge(s["dev"], NCH + 2)

            def up(c, k):
                pe.wait_ge(s["normed"], c + 1)
                pe.wait_ge(s["gelu"], c + 1)
                for j in range(2):
                    m = nc.tensor.matmul(net.psum[:, (2 * k + j) * 512:(2 * k + j) * 512 + CH],
                                         w1[:, j * D:(j + 1) * D], net.col(A, c), start=True, stop=True)
                m.then_inc(s["up"], 1)

            def down(c, k):
                pe.wait_ge(s["gelu"], c + 3)
                pe.wait_ge(s["out"], c + 1)
                for j in range(2):
                    m = nc.tensor.matmul(net.psum[:, (4 + k) * 512:(4 + k) * 512 + CH],
                                         w2[:, j * D:(j + 1) * D],
                                         hidden[k][:, j * 512:j * 512 + CH], start=(j == 0), stop=(j == 1))
                m.then_inc(s["down"], 1)

            up(0, 0)
            with pe.Fori(0, NCH // 2) as i:
                c = pe.snap(i * 2)
                up(c + 1, 1)
                down(c, 0)
                up(c + 2, 0)
                down(c + 1, 1)
            down(NCH - 1, 0)

        @block.vector
        def _(dve):
            dve.sem_inc(s["inverse"], 2)
            dve.wait_ge(s["weights"], 128)
            dve.wait_ge(s["h"], 16)
            with dve.Fori(0, NCH) as c:
                dve.wait_ge(s["spread"], c + 1)
                dve.sem_inc(s["carried"], 1)
                nc.vector.reciprocal(net.col(Cc, c), net.bank(0, c)).then_inc(s["inverse"], 1)
                dve.wait_ge(s["inverse"], c + 3)
                nc.vector.tensor_tensor(net.col(A, c), net.col(A, c), net.col(Cc, c),
                                        ALU.mult).then_inc(s["ratio"], 1)
                dve.wait_ge(s["ratio"], c + 1)
                nc.vector.scalar_tensor_tensor(out=net.col(B, c), in0=net.col(A, c), scalar=gat_b,
                                               in1=net.col(B, c), op0=ALU.add,
                                               op1=ALU.add).then_inc(s["sum"], 1)
            dve.sem_inc(s["centred"], 2)
            with dve.Fori(0, NCH) as c:
                dve.wait_ge(s["mean"], c + 1)
                nc.vector.tensor_tensor(net.col(Cc, c), net.col(B, c), net.bank(2, c),
                                        ALU.subtract).then_inc(s["centred"], 1)
            with dve.Fori(0, NCH) as c:
                dve.wait_ge(s["dev"], c + 3)
                dve.sem_inc(s["carried"], 1)
                nc.vector.reciprocal(net.col(A, c), net.col(A, c)).then_inc(s["inverse2"], 1)
                dve.wait_ge(s["inverse2"], c + 1)
                nc.vector.tensor_tensor(net.col(A, c), net.col(Cc, c), net.col(A, c),
                                        ALU.mult).then_inc(s["scaled"], 1)
            dve.sem_inc(s["out"], 2)

            def out(c, k):
                dve.wait_ge(s["down"], c + 1)
                nc.vector.scalar_tensor_tensor(out=net.col(B, c), in0=net.psum[:, (4 + k) * 512:(4 + k) * 512 + CH],
                                               scalar=b2, in1=net.col(B, c), op0=ALU.add,
                                               op1=ALU.add).then_inc(s["out"], 1)
            each_chunk(dve, out)

        @block.scalar
        def _(act):
            act.sem_inc(s["dev"], 2)
            act.wait_ge(s["weights"], 128)
            with act.Fori(0, NCH) as c:
                act.wait_ge(s["centred"], c + 3)
                nc.scalar.activation(net.col(A, c), net.col(Cc, c), ACT.Square).then_inc(s["squared"], 1)
            with act.Fori(0, NCH) as c:
                act.wait_ge(s["var"], c + 1)
                nc.scalar.activation(net.col(A, c), net.bank(4, c), ACT.Sqrt,
                                     bias=net.eps[:, 0:1]).then_inc(s["dev"], 1)
            with act.Fori(0, NCH) as c:
                act.wait_ge(s["scaled"], c + 1)
                nc.scalar.activation(net.col(A, c), net.col(A, c), ACT.Identity,
                                     bias=bias, scale=gain).then_inc(s["normed"], 1)
            act.sem_inc(s["gelu"], 2)

            def gelu(c, k):
                act.wait_ge(s["up"], c + 1)
                act.wait_ge(s["out"], c + 1)
                nc.scalar.activation(hidden[k][:, 0:CH], net.psum[:, 2 * k * 512:2 * k * 512 + CH],
                                     ACT.Gelu, bias=b1[:, 0:1])
                nc.scalar.activation(hidden[k][:, 512:512 + CH],
                                     net.psum[:, (2 * k + 1) * 512:(2 * k + 1) * 512 + CH],
                                     ACT.Gelu, bias=b1[:, 1:2]).then_inc(s["gelu"], 1)
            each_chunk(act, gelu)


def gin_output(net):
    nc = net.nc
    A, B, Cc = net.A, net.B, net.C
    w1, w2 = net.wtmp[:, 0:2 * D], net.wtmp[:, 2 * D:4 * D]
    vec = net.small
    g1, b1, g2, b2, onep = vec[:, 0:2], vec[:, 2:4], vec[:, 4:5], vec[:, 5:6], vec[:, 6:7]
    mv = [vec[:, 8 + 2 * k:10 + 2 * k] for k in range(3)]
    scale, shift = vec[:, 16:19], vec[:, 20:23]
    stats = [net.onehot[:, :, :, :].rearrange("p a t w -> p (a t w)")[:, k * 6 * NCH:(k + 1) * 6 * NCH]
             for k in range(3)]
    hidden = [net.work[:, k * 1024:(k + 1) * 1024] for k in range(2)]
    s = {k: net.sem(f"gi_{k}") for k in
         ("weights", "h", "step", "z", "first", "stat", "deviation", "up", "hid", "down", "out", "last",
          "sum", "kept")}

    def fold(dve, k, gain, bias, wait, count):
        V = nc.vector
        V.bn_aggr(mv[k], stats[k]).then_inc(s["step"], 1)
        dve.wait_ge(s["step"], count + 1)
        dve.sem_inc(s["deviation"], 1)
        dve.wait_ge(s["deviation"], wait)
        V.reciprocal(scale[:, k:k + 1], scale[:, k:k + 1]).then_inc(s["step"], 1)
        dve.wait_ge(s["step"], count + 2)
        V.tensor_tensor(scale[:, k:k + 1], scale[:, k:k + 1], gain, ALU.mult).then_inc(s["step"], 1)
        dve.wait_ge(s["step"], count + 3)
        V.tensor_tensor(shift[:, k:k + 1], mv[k][:, 0:1], scale[:, k:k + 1], ALU.mult).then_inc(s["step"], 1)
        dve.wait_ge(s["step"], count + 4)
        V.tensor_tensor(shift[:, k:k + 1], bias, shift[:, k:k + 1], ALU.subtract).then_inc(s["step"], 1)

    with nc.Block() as block:
        @block.sync
        def _(sp):
            sp.dma_start(net.ES, Cc[:, 0:N]).then_inc(s["kept"], 16)
            sp.dma_start(B[:, 0:N], net.HT).then_inc(s["h"], 16)
            sp.dma_start(w1, net.dram["L2_gnn_W1"]).then_inc(s["weights"], 16)
            sp.dma_start(w2.rearrange("p (k n) -> p k n", k=2),
                         net.dram["L2_gnn_W2"].rearrange("(k p) n -> p k n", k=2)).then_inc(s["weights"], 16)
            for to, name in ((g1, "L2_gnn_g1"), (b1, "L2_gnn_b1")):
                for k in range(2):
                    sp.dma_start(to[:, k:k + 1], net.dram[name][k * D:(k + 1) * D]
                                 .rearrange("(p a) -> p a", a=1)).then_inc(s["weights"], 16)
            for to, name in ((g2, "L2_gnn_g2"), (b2, "L2_gnn_b2")):
                sp.dma_start(to, net.dram[name].rearrange("(p a) -> p a", a=1)).then_inc(s["weights"], 16)
            sp.dma_start(onep, net.dram["L2_gnn_eps"].rearrange("(a b) -> a b", a=1)
                         .broadcast_to([P, 1])).then_inc(s["weights"], 16)
            sp.wait_ge(s["kept"], 16)

        @block.vector
        def _(dve):
            dve.wait_ge(s["weights"], 144)
            nc.vector.tensor_scalar(onep, onep, 1.0, None, ALU.add).then_inc(s["step"], 1)
            dve.wait_ge(s["step"], 1)
            dve.wait_ge(s["h"], 16)
            with dve.Fori(0, NCH) as c:
                nc.vector.scalar_tensor_tensor(out=net.col(A, c), in0=net.col(B, c), scalar=onep,
                                               in1=net.col(A, c), op0=ALU.mult,
                                               op1=ALU.add).then_inc(s["z"], 1)
            dve.sem_inc(s["stat"], 2)

            def statistics(c, k):
                dve.wait_ge(s["first"], c + 1)
                for j in range(2):
                    last = nc.vector.bn_stats(stats[j][:, bass.ds(c * 6, 6)],
                                              net.psum[:, (2 * k + j) * 512:(2 * k + j) * 512 + CH])
                last.then_inc(s["stat"], 1)
            each_chunk(dve, statistics)
            dve.wait_ge(s["stat"], NCH + 2)
            fold(dve, 0, g1[:, 0:1], b1[:, 0:1], 2, 1)
            fold(dve, 1, g1[:, 1:2], b1[:, 1:2], 4, 6)
            dve.sem_inc(s["out"], 2)

            def out(c, k):
                dve.wait_ge(s["down"], c + 1)
                bank = net.psum[:, (4 + k) * 512:(4 + k) * 512 + CH]
                nc.vector.tensor_copy(net.col(A, c), bank)
                nc.vector.bn_stats(stats[2][:, bass.ds(c * 6, 6)], bank).then_inc(s["out"], 1)
            each_chunk(dve, out)
            dve.wait_ge(s["out"], NCH + 2)
            fold(dve, 2, g2, b2, 6, 11)
            with dve.Fori(0, NCH) as c:
                dve.wait_ge(s["last"], c + 1)
                nc.vector.tensor_tensor(net.col(B, c), net.col(A, c), net.col(B, c),
                                        ALU.add).then_inc(s["sum"], 1)

        @block.scalar
        def _(act):
            for k in range(3):
                if k == 2:
                    act.wait_ge(s["step"], 11)
                    act.sem_inc(s["hid"], 2)

                    def normed(c, kk):
                        act.wait_ge(s["up"], c + 1)
                        act.wait_ge(s["out"], c + 1)
                        for j in range(2):
                            last = nc.scalar.activation(
                                hidden[kk][:, j * 512:j * 512 + CH],
                                net.psum[:, (2 * kk + j) * 512:(2 * kk + j) * 512 + CH], ACT.Relu,
                                bias=shift[:, j:j + 1], scale=scale[:, j:j + 1])
                        last.then_inc(s["hid"], 1)
                    each_chunk(act, normed)
                act.wait_ge(s["deviation"], 2 * k + 1)
                nc.scalar.activation(scale[:, k:k + 1], mv[k][:, 1:2], ACT.Sqrt,
                                     bias=net.eps[:, 0:1]).then_inc(s["deviation"], 1)
            act.wait_ge(s["step"], 16)
            with act.Fori(0, NCH) as c:
                nc.scalar.activation(net.col(A, c), net.col(A, c), ACT.Relu,
                                     bias=shift[:, 2:3], scale=scale[:, 2:3]).then_inc(s["last"], 1)

        @block.tensor
        def _(pe):
            pe.wait_ge(s["weights"], 144)

            def up(c, k, done, free):
                pe.wait_ge(s["z"], c + 1)
                pe.wait_ge(free, c + 1)
                for j in range(2):
                    m = nc.tensor.matmul(net.psum[:, (2 * k + j) * 512:(2 * k + j) * 512 + CH],
                                         w1[:, j * D:(j + 1) * D], net.col(A, c), start=True, stop=True)
                m.then_inc(done, 1)

            def down(c, k):
                pe.wait_ge(s["hid"], c + 3)
                pe.wait_ge(s["out"], c + 1)
                for j in range(2):
                    m = nc.tensor.matmul(net.psum[:, (4 + k) * 512:(4 + k) * 512 + CH],
                                         w2[:, j * D:(j + 1) * D],
                                         hidden[k][:, j * 512:j * 512 + CH], start=(j == 0), stop=(j == 1))
                m.then_inc(s["down"], 1)

            each_chunk(pe, lambda c, k: up(c, k, s["first"], s["stat"]))
            pe.wait_ge(s["stat"], NCH + 2)
            up(0, 0, s["up"], s["hid"])
            with pe.Fori(0, NCH // 2) as i:
                c = pe.snap(i * 2)
                up(c + 1, 1, s["up"], s["hid"])
                down(c, 0)
                up(c + 2, 0, s["up"], s["hid"])
                down(c + 1, 1)
            down(NCH - 1, 0)


class Finish:

    def __init__(self, net, tag, out):
        self.net, self.out = net, out
        s = lambda k: net.sem(f"{tag}_{k}")
        self.x_loaded, self.es_loaded, self.summed, self.half = s("x"), s("edge_sum"), s("summed"), s("half")
        self.brought, self.turned, self.rows = s("brought"), s("turned"), s("rows")
        self.rows_free, self.stored = s("rows_free"), s("stored")
        self.x, self.es = net.wtmp[:, 0:CH], net.wtmp[:, 512:512 + CH]

    def sync(self, sp):
        net = self.net
        sp.sem_inc(self.rows_free, 1)
        with sp.Fori(0, NCH) as c:
            sp.wait_ge(self.summed, c + 1)
            sp.dma_start(self.x, net.XT[:, bass.ds(c * CH, CH)]).then_inc(self.x_loaded, 16)
            sp.dma_start(self.es, net.ES[:, bass.ds(c * CH, CH)]).then_inc(self.es_loaded, 16)
            store_rows(sp, self, c, self.out, D)

    def vector_begin(self, dve):
        dve.sem_inc(self.summed, 1)

    def vector(self, dve, c):
        net = self.net
        V = net.nc.vector
        V.tensor_tensor(net.col(net.A, c), net.col(net.A, c), net.col(net.B, c), ALU.add).then_inc(self.half, 1)
        dve.wait_ge(self.x_loaded, c * 16 + 16)
        dve.wait_ge(self.es_loaded, c * 16 + 16)
        V.tensor_tensor(self.x, self.x, self.es, ALU.add).then_inc(self.half, 1)
        dve.wait_ge(self.half, c * 2 + 2)
        dve.wait_ge(self.turned, c + 1)
        V.tensor_tensor(net.turn[:, :], net.col(net.A, c), self.x, ALU.add).then_inc(self.summed, 1)

    def tensor_begin(self, pe):
        pe.sem_inc(self.turned, 1)

    def tensor(self, pe, c):
        pe.wait_ge(self.summed, c + 2)
        turn_rows(self.net, pe, self, c)

    def scalar(self, act):
        act.sem_inc(self.rows, 1)
        with act.Fori(0, NCH) as c:
            copy_rows(self.net, act, self, c)


def program(nc, dram, out):
    with ExitStack() as ctx:
        net = Net(nc, ctx, dram)
        allocate(net)
        for step in (
                lambda: prepare(net),
                lambda: normalise(net, "n0", first=True, table=net.TA),
                lambda: aggregate(net, "agg0", net.TA, "count",
                                  Sage(net, "sage0", "L0_gnn_W0", "L0_gnn_b0", net.TB, first=True)),
                lambda: aggregate(net, "agg1", net.TB, None,
                                  Sage(net, "sage1", "L0_gnn_W1", "L0_gnn_b1", net.TA)),
                lambda: aggregate(net, "agg2", net.TA, None, Project(net, "project")),
                lambda: gat_gather(net),
                lambda: gat_softmax(net),
                lambda: gat_begin(net),
                lambda: aggregate(net, "agg3", extra="attention"),
                lambda: gat_output(net),
                lambda: normalise(net, "n2", keep=True, table=net.TB),
                lambda: aggregate(net, "agg4", net.TB, "edges"),
                lambda: gin_output(net),
                lambda: normalise(net, "n3", table=net.TA),
                lambda: aggregate(net, "agg5", net.TA, None, Finish(net, "finish", out))):
            with net.stage():
                step()


INPUTS = ["x", "src", "dst", "edge_attr_128", "L0_gnn_W0", "L0_gnn_b0", "L0_gnn_W1", "L0_gnn_b1",
          "L0_gnn_W2", "L0_gnn_b2", "L1_gnn_ln1_g", "L1_gnn_ln1_b", "L1_gnn_W", "L1_gnn_att_src",
          "L1_gnn_att_dst", "L1_gnn_gat_b", "L1_gnn_ln2_g", "L1_gnn_ln2_b", "L1_gnn_w1", "L1_gnn_b1",
          "L1_gnn_w2", "L1_gnn_b2", "L2_gnn_eps", "L2_gnn_W1", "L2_gnn_g1", "L2_gnn_b1", "L2_gnn_W2",
          "L2_gnn_g2", "L2_gnn_b2"]


def kernel(**inputs):
    import numpy as np
    import concourse.bacc as bacc
    from concourse.bass_utils import run_bass_kernel_spmd

    nc = bacc.Bacc("TRN2", target_bir_lowering=False, num_devices=1)
    arrays, dram = {}, {}
    for name in INPUTS:
        a = np.ascontiguousarray(inputs[name])
        if a.ndim == 0:
            a = a.reshape(1)
        arrays[f"in_{name}"] = a
        dram[name] = nc.dram_tensor(f"in_{name}", a.shape, mybir.dt.from_np(a.dtype),
                                    kind="ExternalInput").ap()
    out = nc.dram_tensor("out", [N, D], F32, kind="ExternalOutput").ap()
    program(nc, dram, out)
    r = run_bass_kernel_spmd(nc, [arrays], core_ids=[0])
    return r.results[0]["out"]
```

```python
from contextlib import ExitStack, contextmanager

import concourse.bass as bass
from concourse import mybir

F32 = mybir.dt.float32
I32 = mybir.dt.int32
ALU = mybir.AluOpType
ACT = mybir.ActivationFunctionType
AX_X = mybir.AxisListType.X

N = 12500
E = 200000
D = 128
P = 128
CH = 500
NCH = N // CH
SUB = 125
NSUB = N // SUB
TILE = 128
HALF = 16
GT = 4
GPH = HALF // GT
NHALF = 98
NIT = NHALF // 2
NTILE = NHALF * HALF
NGRP = NTILE // GT
EP = NTILE * TILE
GE = GT * TILE
W = 64
EPP = EP // P
H = 4
C = D // H
XW = D + 2 * H
EPS = 1e-5
BIG = 1e38
NSC = -(-(EP + N) // P) * P
REG = 12800


class Net:

    def __init__(self, nc, ctx, dram):
        self.nc, self.ctx, self.dram = nc, ctx, dram
        self.pool_sems = [ctx.enter_context(nc.semaphore(f"pool_dma{k}")) for k in range(23)]
        self.stage_sems, self.stage_ctx = [], None

    @contextmanager
    def stage(self):
        with ExitStack() as self.stage_ctx:
            yield
            sems, self.stage_sems = self.stage_sems, []
            with self.nc.Block() as block:
                @block.sync
                def _(sp):
                    for x in sems:
                        sp.sem_clear(x)

    def sem(self, name):
        x = self.stage_ctx.enter_context(self.nc.semaphore(name))
        self.stage_sems.append(x)
        return x

    def pool_sem(self):
        return self.pool_sems.pop()

    def sb(self, name, shape, dt=F32):
        return self.ctx.enter_context(self.nc.sbuf_tensor(name, shape, dt))

    def hbm(self, name, shape, dt=F32):
        return self.nc.dram_tensor(name, shape, dt, kind="Internal").ap()

    def col(self, t, c):
        return t[:, bass.ds(c * CH, CH)]

    def bank(self, first, c, n=CH):
        return self.psum[:, bass.ds((c % 2) * 512 + first * 512, n)]


def allocate(net):
    net.A = net.sb("regionA", [P, REG])
    net.B = net.sb("regionB", [P, REG])
    net.C = net.sb("regionC", [P, NSUB * XW])
    net.work = net.sb("work", [P, 2 * HALF * XW])
    net.onehot = net.sb("onehot", [P, 2, HALF, W])
    net.src_n = net.sb("src_n", [P, NTILE])
    net.rel_n = net.sb("rel_n", [P, NTILE])
    net.index = net.sb("index", [P, 2, HALF], I32)
    net.base = net.sb("base", [1, NGRP], I32)
    net.base_now = net.sb("base_now", [1, NGRP], I32)
    net.rounds = net.sb("rounds", [1, 1], I32)
    net.due = net.sb("due", [1, NIT + 1], I32)
    net.window0 = net.sb("window0", [P, W])
    net.window = net.sb("window", [P, W])
    net.ident = net.sb("ident", [P, P])
    net.mean_w = net.sb("mean_w", [P, P])
    net.ones = net.sb("ones", [P, P])
    net.eps = net.sb("eps", [P, 1])
    net.psum = net.ctx.enter_context(net.nc.psum_tensor("psum", [P, 8 * 512], F32))
    net.p_self = net.sb("p_self", [SUB, NSUB * H])
    net.wtmp = net.sb("weights", [P, 2 * 2 * D + 4 * D + 24])
    net.small = net.sb("small", [P, 160])
    net.turn = net.sb("turn", [P, CH])
    net.rows = net.sb("rows", [P, 4 * XW])

    net.XT = net.hbm("x_transposed", [D, N])
    net.HT = net.hbm("h_transposed", [D, N])
    net.ES = net.hbm("edge_sum", [D, N])
    net.TA = net.hbm("rows_a", [N, D])
    net.TB = net.hbm("rows_b", [N, D])
    net.XH = net.hbm("attention_rows", [N, XW])
    net.G = net.hbm("gathered_rows", [NHALF, P, HALF * XW])
    net.SH = net.hbm("scores_by_head", [H, EP])
    net.PH = net.hbm("probs_by_head", [H, EP])
    net.FD = net.hbm("running_max", [EP, H])
    net.SC = net.hbm("segment_starts", [NSC, 2 * H])
    net.NV = net.hbm("node_values", [N, 2 * H])
    net.DEALT = net.hbm("dealt_lists", [2, P, NTILE])
    net.DST = net.hbm("dst_padded", [EP])
    net.BASE = net.hbm("group_bases", [NGRP], I32)
    net.CUM = net.hbm("segment_ends", [2, N])


def each_chunk(eng, body, count=NCH):
    with eng.Fori(0, count // 2) as i:
        for k in range(2):
            body(eng.snap(i * 2 + k), k)
    for c in range(count // 2 * 2, count):
        body(c, c % 2)


def slot(net, k, width=CH):
    return net.work[:, k * 512:k * 512 + width]



def rows_bring(net, pool, s, region, ready):
    pool.sem_inc(s["turned"], 2)

    def bring(c, k):
        pool.wait_ge(ready, c + 3)
        pool.wait_ge(s["turned"], c + 1)
        net.nc.gpsimd.tensor_copy(slot(net, k), net.col(region, c)).then_inc(s["brought"], 1)
    each_chunk(pool, bring)


def rows_turn_step(net, pe, s, first):
    def turn(c, k):
        pe.wait_ge(s["brought"], c + 1)
        pe.wait_ge(s["rows"], c + 1)
        for j in range(4):
            t = net.nc.tensor.transpose(
                net.psum[0:SUB, (first + k) * 512 + j * D:(first + k) * 512 + (j + 1) * D],
                net.work[:, k * 512 + j * SUB:k * 512 + (j + 1) * SUB], net.ident[:, :])
        t.then_inc(s["turned"], 1)
    return turn


def rows_copy_step(net, eng, copy, s, first, region):
    def out(c, k):
        eng.wait_ge(s["turned"], c + 3)
        copy(region[0:SUB, bass.ds(c * 4 * D, 4 * D)],
             net.psum[0:SUB, (first + k) * 512:(first + k + 1) * 512]).then_inc(s["rows"], 1)
    return out



def staggered(eng, *steps):
    steps = sorted(steps, key=lambda x: -x[0])
    lead, least = steps[0][0], steps[-1][0]

    def turn(t, parity):
        for lag, step in steps:
            if not isinstance(t, int):
                step(eng.snap(t - lag), (parity - lag) % 2)
            elif 0 <= t - lag < NCH:
                step(t - lag, (parity - lag) % 2)

    pairs = (NCH + least - lead) // 2
    for t in range(least, lead):
        turn(t, t)
    with eng.Fori(0, pairs) as i:
        for k in range(2):
            turn(eng.snap(i * 2 + (lead + k)), lead + k)
    for t in range(lead + 2 * pairs, NCH + lead):
        turn(t, t)


def square_slot(net, k):
    return net.work[:, 2048 + k * 512:2048 + k * 512 + CH]


def inverse_slot(net, k):
    return net.work[:, 3072 + k * P:3072 + k * P + SUB]


def selectors(net):
    return net.onehot[:, :, :, :].rearrange("p a t w -> p (a t w)")[:, 0:4 * P]


def make_selectors(net, dve, s):
    net.nc.vector.memset(selectors(net), 0.0).then_inc(s["selectors"], 1)
    dve.wait_ge(s["selectors"], 1)
    for j in range(4):
        net.nc.vector.memset(selectors(net)[32 * j:32 * j + 1, j * P:(j + 1) * P], 1.0
                             ).then_inc(s["selectors"], 1)


def inverse_steps_tensor(net, pe, s, used, spread_bank=lambda k: 2 + k):
    banks = 1 + spread_bank(1) - spread_bank(0)

    def variance(c, k):
        pe.wait_ge(s["squared"], c + 1)
        pe.wait_ge(s["dev"], c + 1)
        for j in range(4):
            m = net.nc.tensor.matmul(net.psum[32 * j:32 * j + 32, (4 + k) * 512:(4 + k) * 512 + SUB],
                                     net.mean_w[:, 0:32], square_slot(net, k)[:, j * SUB:(j + 1) * SUB],
                                     start=True, stop=True)
        m.then_inc(s["var"], 1)

    def spread(c, k):
        pe.wait_ge(s["inverse"], c + 1)
        pe.wait_ge(used, c + 3 - banks)
        at = spread_bank(k) * 512
        for j in range(4):
            m = net.nc.tensor.matmul(net.psum[:, at + j * SUB:at + (j + 1) * SUB],
                                     selectors(net)[:, j * P:(j + 1) * P], inverse_slot(net, k),
                                     start=True, stop=True)
        m.then_inc(s["spread"], 1)

    return (4, variance), (6, spread)


def inverse_steps_scalar(net, act, s, centred, tokens=2):
    def square(c, k):
        act.wait_ge(s["centred"], c + 1 + tokens)
        act.wait_ge(s["var"], c + 1)
        net.nc.scalar.activation(square_slot(net, k), net.col(centred, c), ACT.Square
                                 ).then_inc(s["squared"], 1)

    def deviation(c, k):
        act.wait_ge(s["var"], c + 3)
        act.wait_ge(s["spread"], c + 1)
        net.nc.scalar.activation(inverse_slot(net, k), net.psum[:, (4 + k) * 512:(4 + k) * 512 + SUB],
                                 ACT.Sqrt, bias=net.eps[:, 0:1]).then_inc(s["dev"], 1)

    return (3, square), (4, deviation)


def inverse_steps_vector(net, dve, s, use, spread_bank=lambda k: 2 + k):
    def invert(c, k):
        dve.wait_ge(s["dev"], c + 3)
        net.nc.vector.reciprocal(inverse_slot(net, k), inverse_slot(net, k)).then_inc(s["inverse"], 1)

    def take(c, k):
        dve.wait_ge(s["spread"], c + 3)
        use(c, net.psum[:, spread_bank(k) * 512:spread_bank(k) * 512 + CH])

    return (5, invert), (6, take)


def prepare(net):
    nc = net.nc
    GP = NGRP // GPH
    built, masked, filled = net.sem("pre_built"), net.sem("pre_masked"), net.sem("pre_filled")
    loaded_d, loaded_s = net.sem("pre_dst"), net.sem("pre_src")
    step, spread, wrote = net.sem("pre_step"), net.sem("pre_spread"), net.sem("pre_wrote")
    loaded_b, turned, copied = net.sem("pre_base"), net.sem("pre_turned"), net.sem("pre_copied")
    dst_i = net.A[0:GP, 0:GPH * GE].bitcast(I32)
    dst_f = net.A[0:GP, 2048:2048 + GPH * GE]
    rel_f = net.A[0:GP, 4096:4096 + GPH * GE]
    src_i = net.B[0:GP, 0:GPH * GE].bitcast(I32)
    src_f = net.B[0:GP, 2048:2048 + GPH * GE]
    dealt = [net.B[:, 4096 + k * NTILE:4096 + (k + 1) * NTILE] for k in range(2)]
    least, most = net.small[0:GP, 0:GPH], net.small[0:GP, 4:8]
    span = net.small[0:GP, 8:9]
    least_i = net.small[0:GP, 12:16].bitcast(I32)
    row = net.small[0:1, 16:20]
    it_i = net.work[:, 0:W].bitcast(I32)
    zeros = net.C[:, 0:2 * H * NSC // P // 2]
    whole = E // (GPH * GE)
    left = E - whole * GPH * GE
    lists = [(src_f, net.src_n, False), (rel_f, net.rel_n, False), (src_f, dealt[0], True), (rel_f, dealt[1], True)]
    tiles = [(fr, to, deal, g, k) for fr, to, deal in lists for g in range(GPH) for k in range(GT)]

    with nc.Block() as block:
        @block.gpsimd
        def _(pool):
            pool.memset(net.ident[:, :], 0.0).then_inc(built, 1)
            pool.iota(it_i, pattern=[[1, W]], base=0, channel_multiplier=0).then_inc(built, 1)
            pool.wait_ge(built, 2)
            pool.affine_select(out=net.ident[:, :], in_=net.ident[:, :], compare_op=ALU.not_equal,
                               fill=1.0, base=0, pattern=[[-1, P]],
                               channel_multiplier=1).then_inc(masked, 1)

        @block.sync
        def _(sp):
            sp.wait_ge(filled, 2)
            for name, to, sem in (("dst", dst_i, loaded_d), ("src", src_i, loaded_s)):
                sp.dma_start(to[0:whole, :], net.dram[name][0:whole * GPH * GE]
                             .rearrange("(p f) -> p f", p=whole)).then_inc(sem, 16)
                sp.dma_start(to[whole:whole + 1, 0:left], net.dram[name][whole * GPH * GE:E]
                             .rearrange("(p f) -> p f", p=1)).then_inc(sem, 16)
            sp.wait_ge(step, 4)
            sp.dma_start(net.DST.rearrange("(p f) -> p f", p=GP), dst_f).then_inc(wrote, 16)
            sp.dma_start(net.BASE.rearrange("(p f) -> p f", p=GP), least_i).then_inc(loaded_b, 16)
            sp.wait_ge(filled, 3)
            flat = net.SC.rearrange("(k p r) f -> k p (r f)", k=2, p=P)
            for k in range(2):
                sp.dma_start(flat[k], zeros).then_inc(wrote, 16)
            sp.wait_ge(loaded_b, 16)
            sp.dma_start(net.base[:, :], net.BASE.rearrange("(a g) -> a g", a=1)).then_inc(loaded_b, 16)
            sp.wait_ge(copied, len(tiles))
            for k in range(2):
                sp.dma_start(net.DEALT[k], dealt[k]).then_inc(wrote, 16)
            sp.wait_ge(wrote, 80)
            sp.wait_ge(loaded_b, 32)

        @block.vector
        def _(dve):
            nc.vector.memset(dst_i, N).then_inc(filled, 1)
            nc.vector.memset(src_i, 0).then_inc(filled, 1)
            nc.vector.memset(zeros, 0.0).then_inc(filled, 1)
            nc.vector.memset(net.ones[:, :], 1.0)
            nc.vector.memset(net.mean_w[:, :], 1.0 / D)
            nc.vector.memset(net.eps[:, :], EPS)
            dve.wait_ge(built, 2)
            nc.vector.tensor_copy(net.window0[:, :], it_i)
            dve.wait_ge(loaded_d, 32)
            nc.vector.tensor_copy(dst_f, dst_i).then_inc(step, 1)
            dve.wait_ge(step, 1)
            df = dst_f.rearrange("p (g e) -> p g e", g=GPH)
            nc.vector.tensor_reduce(least, df, AX_X, ALU.min)
            nc.vector.tensor_reduce(most, df, AX_X, ALU.max).then_inc(step, 1)
            dve.wait_ge(step, 2)
            nc.vector.tensor_copy(least_i, least).then_inc(step, 1)
            nc.vector.tensor_tensor(rel_f.rearrange("p (g e) -> p g e", g=GPH), df,
                                    least.unsqueeze(2).broadcast_to([GP, GPH, GE]),
                                    ALU.subtract).then_inc(step, 1)
            nc.vector.tensor_tensor(most, most, least, ALU.subtract).then_inc(step, 1)
            dve.wait_ge(step, 5)
            nc.vector.tensor_reduce(span, most, AX_X, ALU.max).then_inc(step, 1)
            dve.wait_ge(spread, 1)
            nc.vector.tensor_reduce(row[:, 0:1], net.psum[0:1, 0:GP], AX_X, ALU.max).then_inc(step, 1)
            dve.wait_ge(step, 7)
            nc.vector.tensor_scalar(row[:, 1:2], row[:, 0:1], 1.0 / W, 0.5 + 0.5 / W,
                                    ALU.mult, ALU.add).then_inc(step, 1)
            dve.wait_ge(step, 8)
            nc.vector.tensor_copy(net.rounds[:, :], row[:, 1:2])
            dve.wait_ge(loaded_s, 32)
            nc.vector.tensor_copy(src_f, src_i).then_inc(step, 1)
            dve.wait_ge(loaded_b, 32)
            low = [net.work[0:1, 512 * k:512 * k + 128] for k in range(2)]
            bases = net.work[0:1, 1024:1024 + NGRP]
            nc.vector.tensor_copy(bases, net.base[:, :])
            nc.vector.memset(low[0], N)
            nc.vector.memset(low[1], N).then_inc(step, 1)
            dve.wait_ge(step, 10)
            nc.vector.tensor_reduce(low[0][:, 0:NIT], bases.rearrange("a (i g) -> a i g", i=NIT), AX_X,
                                    ALU.min).then_inc(step, 1)
            for j in range(6):
                dve.wait_ge(step, 11 + j)
                nc.vector.tensor_tensor(low[(j + 1) % 2][:, 0:NIT], low[j % 2][:, 0:NIT],
                                        low[j % 2][:, 2 ** j:2 ** j + NIT], ALU.min).then_inc(step, 1)
            nc.vector.tensor_scalar(row[:, 2:3], row[:, 0:1], float(W), None, ALU.is_lt)
            dve.wait_ge(step, 17)
            nc.vector.tensor_scalar(low[1][:, 0:NIT], low[0][:, 0:NIT], 1.0 / CH, 0.5 / CH - 0.5,
                                    ALU.mult, ALU.add).then_inc(step, 1)
            dve.wait_ge(step, 18)
            nc.vector.tensor_copy(net.due[:, 0:NIT], low[1][:, 0:NIT]).then_inc(step, 1)
            dve.wait_ge(step, 19)
            nc.vector.tensor_copy(low[1][:, 0:NIT], net.due[:, 0:NIT]).then_inc(step, 1)
            dve.wait_ge(step, 20)
            nc.vector.tensor_scalar(low[1][:, 0:NIT], low[1][:, 0:NIT], row[:, 2:3], None,
                                    ALU.mult).then_inc(step, 1)
            dve.wait_ge(step, 21)
            nc.vector.tensor_copy(net.due[:, 0:NIT], low[1][:, 0:NIT])
            for n, (_, to, _, g, k) in enumerate(tiles):
                dve.wait_ge(turned, n + 1)
                nc.vector.tensor_copy(to[:, :].rearrange("p (a t) -> p a t", t=HALF)[:, :, g * GT + k],
                                      net.psum[:, (n % 2 + 2) * 512:(n % 2 + 2) * 512 + GP]
                                      ).then_inc(copied, 1)

        @block.tensor
        def _(pe):
            pe.wait_ge(masked, 1)
            pe.wait_ge(step, 6)
            nc.tensor.transpose(net.psum[0:1, 0:GP], span, net.ident[0:GP, 0:GP]).then_inc(spread, 1)
            pe.wait_ge(step, 9)
            for n, (fr, _, deal, g, k) in enumerate(tiles):
                if n >= 2:
                    pe.wait_ge(copied, n - 1)
                group = fr[:, g * GE:(g + 1) * GE]
                tile = (group.rearrange("a (p k) -> a k p", k=GT)[:, k, :] if deal
                        else group[:, k * TILE:(k + 1) * TILE])
                nc.tensor.transpose(net.psum[:, (n % 2 + 2) * 512:(n % 2 + 2) * 512 + GP], tile,
                                    net.ident[0:GP, 0:GP]).then_inc(turned, 1)


def normalise(net, tag, first=False, keep=False, table=None):
    nc = net.nc
    A, B, Cc = net.A, net.B, net.C
    s = {k: net.sem(f"{tag}_{k}") for k in
         ("loaded", "x_brought", "x_turned", "x_ready", "brought", "mean", "centred", "squared", "var", "dev",
          "inverse", "selectors", "spread", "h", "turned", "rows", "saved", "stored", "kept", "carried")}
    in_slot = lambda k: net.work[0:SUB, (k + 2) * 512:(k + 3) * 512]

    with nc.Block() as block:
        @block.sync
        def _(sp):
            if first:
                for k in range(5):
                    sp.dma_start(Cc[0:SUB, k * 20 * D:(k + 1) * 20 * D].rearrange("p (t f) -> p t f", f=D),
                                 net.dram["x"][k * 2500:(k + 1) * 2500, :]
                                 .rearrange("(t p) f -> p t f", p=SUB)).then_inc(s["loaded"], 16)
            else:
                sp.dma_start(A[:, 0:N], net.XT).then_inc(s["loaded"], 16)
            with sp.Fori(0, NCH) as c:
                sp.wait_ge(s["x_ready"], c + 3)
                sp.sem_inc(s["carried"], 1)
                sp.dma_start(net.XT[:, bass.ds(c * CH, CH)], net.col(A, c)).then_inc(s["saved"], 16)
                if keep:
                    sp.wait_ge(s["h"], c + 3)
                    sp.sem_inc(s["carried"], 1)
                    sp.dma_start(net.HT[:, bass.ds(c * CH, CH)], net.col(B, c)).then_inc(s["kept"], 16)
                sp.wait_ge(s["rows"], c + 3)
                sp.sem_inc(s["carried"], 1)
                sp.dma_start(table[bass.ds(c * CH, CH), :].rearrange("(t p) f -> p t f", p=SUB),
                             Cc[0:SUB, bass.ds(c * 4 * D, 4 * D)].rearrange("p (t f) -> p t f", f=D)
                             ).then_inc(s["stored"], 16)
            sp.wait_ge(s["stored"], 16 * NCH)
            sp.wait_ge(s["saved"], 16 * NCH)
            if keep:
                sp.wait_ge(s["kept"], 16 * NCH)

        @block.tensor
        def _(pe):
            def turn_in(c, k):
                pe.wait_ge(s["x_brought"], c + 1)
                pe.wait_ge(s["x_ready"], c + 1)
                for j in range(4):
                    t = nc.tensor.transpose(net.psum[:, k * 512 + j * SUB:k * 512 + (j + 1) * SUB],
                                            in_slot(k)[:, j * D:(j + 1) * D], net.ident[0:SUB, 0:SUB])
                t.then_inc(s["x_turned"], 1)

            def mean(c, k):
                pe.wait_ge(s["x_ready"], c + 3)
                pe.wait_ge(s["centred"], c + 1)
                nc.tensor.matmul(net.psum[:, 1024:1024 + CH], net.mean_w[:, :], net.col(A, c),
                                 start=True, stop=True).then_inc(s["mean"], 1)

            pe.sem_inc(s["var"], 2)
            pe.sem_inc(s["spread"], 2)
            pe.wait_ge(s["selectors"], 5)
            steps = [(2, mean), *inverse_steps_tensor(net, pe, s, s["h"], lambda k: 3),
                     (8, rows_turn_step(net, pe, s, 6))]
            staggered(pe, *([(1, turn_in)] if first else []), *steps)

        @block.vector
        def _(dve):
            make_selectors(net, dve, s)
            dve.sem_inc(s["centred"], 1)
            dve.sem_inc(s["h"], 2)

            def bring_in(c, k):
                dve.wait_ge(s["x_turned"], c + 1)
                nc.vector.tensor_copy(in_slot(k), Cc[0:SUB, bass.ds(c * 4 * D, 4 * D)]
                                      ).then_inc(s["x_brought"], 1)

            def add_x(c, k):
                nc.vector.tensor_tensor(net.col(A, c), net.col(A, c), net.col(B, c),
                                        ALU.add).then_inc(s["x_ready"], 1)

            def centre(c, k):
                dve.wait_ge(s["mean"], c + 1)
                nc.vector.tensor_tensor(net.col(B, c), net.col(A, c), net.psum[:, 1024:1024 + CH],
                                        ALU.subtract).then_inc(s["centred"], 1)

            if first:
                dve.sem_inc(s["x_turned"], 2)
                dve.wait_ge(s["loaded"], 80)
            else:
                dve.sem_inc(s["x_ready"], 2)
                dve.wait_ge(s["loaded"], 16)
            invert, take = inverse_steps_vector(net, dve, s, lambda c, bank: nc.vector.scalar_tensor_tensor(
                out=net.col(B, c), in0=net.col(B, c), scalar=0.0, in1=bank, op0=ALU.max,
                op1=ALU.mult).then_inc(s["h"], 1), lambda k: 3)
            staggered(dve, (0 if first else 1, bring_in if first else add_x), (2, centre), invert, take)

        @block.scalar
        def _(act):
            act.sem_inc(s["dev"], 2)
            act.sem_inc(s["rows"], 2)
            if first:
                act.sem_inc(s["x_ready"], 2)

            def copy_in(c, k):
                act.wait_ge(s["x_turned"], c + 3)
                nc.scalar.copy(net.col(A, c), net.psum[:, k * 512:k * 512 + CH]).then_inc(s["x_ready"], 1)

            staggered(act, *([(1, copy_in)] if first else []), *inverse_steps_scalar(net, act, s, B, 1),
                      (8, rows_copy_step(net, act, nc.scalar.copy, s, 6, Cc)))

        @block.gpsimd
        def _(pool):
            rows_bring(net, pool, s, B, s["h"])


def due_chunks(net, eng, first, past, body, before=None):
    lo = eng.value_load(net.due[0:1, bass.ds(first, 1)], min_val=0, max_val=NCH)
    hi = NCH if past is None else eng.value_load(net.due[0:1, bass.ds(past, 1)], min_val=0, max_val=NCH)
    if before:
        before()
    with eng.If(lo < hi):
        with eng.Fori(lo, hi) as c:
            body(c)


def aggregate(net, tag, table=None, extra=None, follow=None):
    nc = net.nc
    A, Cc = net.A, net.C
    attention, edges = extra == "attention", extra == "edges"
    width = XW if attention else D
    S = 2 if attention or edges else 4
    ST, SG = 2 * HALF // S, 2 * GPH // S
    rows = [net.work[:, h * ST * XW:h * ST * XW + ST * width] for h in range(S)]
    rows3 = [r.rearrange("p (t f) -> p t f", f=width) for r in rows]
    attr = [net.B[:, h * HALF * D:(h + 1) * HALF * D] for h in range(2)]
    piles = [net.C[:, REG + h * SG * W:REG + (h + 1) * SG * W] for h in range(S)]
    onehot = net.onehot[:, :, :, :].rearrange("p a t w -> p (a t) w")
    at0 = EPP * H if attention else 2 * HALF * D
    msgs = [net.B[:, at0 + h * HALF * width:at0 + (h + 1) * HALF * width] for h in range(2)] if (
        attention or edges) else rows
    msgs3 = [m.rearrange("p (t f) -> p t f", f=width) for m in msgs]
    high = [P, H if attention else P]
    dense = follow and follow.dense
    NB = 4 if dense else 8
    bank_of = lambda h, q, k: net.psum[0:high[k], (h * SG + q) % NB * 512 + k * W:(h * SG + q) % NB * 512 + (k + 1) * W]
    name = lambda k: [net.sem(f"{tag}_{k}{h}") for h in range(S)]
    index_ready, onehot_ready = name("index"), name("onehot")
    gathered = name("gathered") if attention else [net.pool_sem() for _ in range(S)]
    summed = name("summed")
    message, attr_loaded, relued = name("message"), name("attr"), name("relued")
    added = net.sem(f"{tag}_added")
    lists = net.sem(f"{tag}_lists")
    cleared, moved = net.sem(f"{tag}_cleared"), net.sem(f"{tag}_moved")
    piled = name("piled") if extra == "count" else onehot_ready
    ready = relued if edges else message if attention else gathered

    with nc.Block() as block:
        if dense:
            @block.scalar
            def _(act):
                follow.scalar(act)

        if not attention:
            if edges:
                @block.scalar
                def _(act):
                    R = act.value_load(net.rounds[0:1, 0:1], min_val=1, max_val=256)
                    with act.Fori(0, R) as r:
                        with act.Fori(0, NIT) as i:
                            n = act.snap(r * NIT + i)
                            for h in range(2):
                                act.wait_ge(message[h], n + 2)
                                nc.scalar.activation(msgs[h], msgs[h], ACT.Relu).then_inc(relued[h], 1)

            @block.gpsimd
            def _(pool):
                if edges:
                    pool.wait_ge(lists, 32)
                R = pool.value_load(net.rounds[0:1, 0:1], min_val=1, max_val=256)
                with pool.Fori(0, R) as r:
                    with pool.Fori(0, NIT) as i:
                        n = pool.snap(r * NIT + i)
                        for h in range(S):
                            if edges:
                                pool.wait_ge(message[h], n + 1)
                            else:
                                pool.wait_ge(summed[h], n * SG + SG)
                            index = net.index[:, :, :].rearrange("p a t -> p (a t)")[:, h * ST:(h + 1) * ST]
                            nc.gpsimd.tensor_copy(index, net.src_n[:, bass.ds(i * 2 * HALF + h * ST, ST)]
                                                  ).then_inc(index_ready[h], 1)
                            pool.wait_ge(index_ready[h], n + 1)
                            pool.sem_inc(moved, 1)
                            for t in range(ST):
                                pool.indirect_dma_start(
                                    rows3[h][:, t, :], None, table,
                                    bass.IndirectOffsetOnAxis(ap=index[:, t:t + 1], axis=0)
                                ).then_inc(gathered[h], 16)

        @block.sync
        def _(sp):
            if not (attention or edges):
                if dense:
                    follow.sync(sp)
                return
            if edges:
                sp.dma_start(net.src_n[:, :], net.DEALT[0]).then_inc(lists, 16)
                sp.dma_start(net.rel_n[:, :], net.DEALT[1]).then_inc(lists, 16)
                sp.wait_ge(cleared, 1)
            R = sp.value_load(net.rounds[0:1, 0:1], min_val=1, max_val=256)
            with sp.Fori(0, R) as r:
                with sp.Fori(0, NIT) as i:
                    n = sp.snap(r * NIT + i)
                    for h in range(2):
                        if attention:
                            sp.wait_ge(message[h], n + 1)
                            sp.dma_start(rows[h], net.G[bass.ds(i * 2 + h, 1), :, :]
                                         .rearrange("a p f -> (a p) f")).then_inc(gathered[h], 16)
                        else:
                            sp.wait_ge(summed[h], n * GPH + GPH)
                            lane = "(q p k) f -> p q (k f)"
                            slots = attr[h].rearrange("p (q f) -> p q f", q=GPH)
                            edge = net.dram["edge_attr_128"]
                            at = (2 * i + h) * HALF * TILE
                            sp.dma_start(slots[:, 0:2, :], edge[bass.ds(at, 2 * GE), :].rearrange(
                                lane, q=2, p=P)).then_inc(attr_loaded[h], 16)
                            if h == 0:
                                sp.dma_start(slots[:, 2:4, :], edge[bass.ds(at + 2 * GE, 2 * GE), :].rearrange(
                                    lane, q=2, p=P)).then_inc(attr_loaded[h], 16)
                                continue
                            with sp.If(i < NIT - 1):
                                more = nc.s_assert_within(at + 2 * GE, 0, E - 2 * GE)
                                sp.dma_start(slots[:, 2:4, :], edge[bass.ds(more, 2 * GE), :].rearrange(
                                    lane, q=2, p=P)).then_inc(attr_loaded[h], 16)
                            with sp.Else():
                                rest = E - (NGRP - 2) * GE
                                sp.dma_start(slots[0:rest // GT, 2, :], edge[E - rest:E, :].rearrange(
                                    "(p k) f -> p (k f)", k=GT)).then_inc(attr_loaded[h], 16)

        @block.tensor
        def _(pe):
            for h in range(S):
                pe.sem_inc(summed[h], SG)
            if dense:
                follow.tensor_begin(pe)
            R = pe.value_load(net.rounds[0:1, 0:1], min_val=1, max_val=256)
            with pe.Fori(0, R) as r:
                with pe.Fori(0, NIT) as i:
                    n = pe.snap(r * NIT + i)
                    for h in range(S):
                        pe.wait_ge(piled[h], n + 1)
                        if ready is gathered:
                            pe.wait_ge(gathered[h], n * 16 * ST + 16 * ST)
                        else:
                            pe.wait_ge(ready[h], n + (2 if ready is message else 1))
                        for q in range(SG):
                            pe.wait_ge(added, n * 2 * GPH + h * SG + q + 1 + 2 * GPH - NB)
                            for k in range(GT):
                                t = q * GT + k
                                last = nc.tensor.matmul(bank_of(h, q, 0),
                                                        msgs3[h][:, t, 0:D], onehot[:, h * ST + t, :],
                                                        start=(k == 0), stop=(k == GT - 1))
                            if extra:
                                if extra == "count":
                                    last = nc.tensor.matmul(bank_of(h, q, 1), net.ones[:, :],
                                                            piles[h][:, q * W:(q + 1) * W],
                                                            start=True, stop=True)
                                for k in range(0 if extra == "count" else GT):
                                    t = q * GT + k
                                    if edges:
                                        lhs = attr[h][:, t * D:(t + 1) * D]
                                    else:
                                        lhs = msgs3[h][:, t, D:D + H]
                                    last = nc.tensor.matmul(bank_of(h, q, 1),
                                                            lhs, onehot[:, h * ST + t, :],
                                                            start=(k == 0), stop=(k == GT - 1))
                            last.then_inc(summed[h], 1)
                    if dense:
                        with pe.If(i < NIT - 1):
                            due_chunks(net, pe, i, i + 1, lambda c: follow.tensor(pe, c))
            if dense:
                due_chunks(net, pe, NIT - 1, None, lambda c: follow.tensor(pe, c))

        @block.vector
        def _(dve):
            if not attention:
                nc.vector.memset(A[:, :], 0.0)
                if extra:
                    nc.vector.memset(Cc[:, 0:REG], 1.0 if extra == "count" else 0.0)
            if edges:
                nc.vector.memset(net.B[:, 0:2 * HALF * D], 0.0)
            nc.vector.tensor_copy(net.window[:, :], net.window0[:, :])
            nc.vector.tensor_copy(net.base_now[:, :], net.base[:, :]).then_inc(cleared, 1)
            dve.wait_ge(cleared, 1)
            if edges:
                dve.wait_ge(lists, 32)
            dve.sem_inc(added, 2 * GPH)
            if attention or edges:
                for h in range(S):
                    dve.sem_inc(message[h], 1)
            if follow:
                follow.vector_begin(dve)
            R = dve.value_load(net.rounds[0:1, 0:1], min_val=1, max_val=256)
            with dve.Fori(0, R) as r:
                def compare(i, h):
                    dve.wait_ge(summed[h], (r * NIT + i) * SG + SG)
                    nc.vector.tensor_tensor(
                        onehot[:, h * ST:(h + 1) * ST, :],
                        net.rel_n[:, bass.ds(i * 2 * HALF + h * ST, ST)].unsqueeze(2)
                        .broadcast_to([P, ST, W]),
                        net.window[:, :].unsqueeze(1).broadcast_to([P, ST, W]),
                        ALU.is_equal).then_inc(onehot_ready[h], 1)
                    if extra == "count":
                        dve.wait_ge(onehot_ready[h], r * NIT + i + 1)
                        nc.vector.tensor_reduce(
                            piles[h].rearrange("p (q w) -> p q w", w=W),
                            onehot[:, h * ST:(h + 1) * ST, :].rearrange("p (q k) w -> p q w k", k=GT),
                            AX_X, ALU.add).then_inc(piled[h], 1)

                def messages(i, h):
                    n = r * NIT + i
                    if attention:
                        dve.wait_ge(gathered[h], n * 16 + 16)
                        pr3 = net.B[:, bass.ds(i * 2 * HALF * H, 2 * HALF * H)].rearrange(
                            "p (h t) -> p t h", h=H)[:, h * HALF:(h + 1) * HALF, :]
                        by_head = lambda x: x[:, :, 0:D].rearrange("p t (h c) -> p t h c", h=H)
                        nc.vector.tensor_copy(msgs3[h][:, :, D:D + H], pr3)
                        nc.vector.tensor_tensor(by_head(msgs3[h]), by_head(rows3[h]),
                                                pr3.unsqueeze(3).broadcast_to([P, HALF, H, C]),
                                                ALU.mult).then_inc(message[h], 1)
                    elif edges:
                        dve.wait_ge(gathered[h], n * 16 * ST + 16 * ST)
                        dve.wait_ge(attr_loaded[h], n * 32 + 32)
                        nc.vector.tensor_tensor(msgs[h], rows[h], attr[h], ALU.add).then_inc(message[h], 1)

                def add(i, h):
                    n = r * NIT + i
                    for q in range(SG):
                        at = dve.value_load(net.base_now[0:1, bass.ds(i * 2 * GPH + h * SG + q, 1)],
                                            min_val=0, max_val=N)
                        dve.wait_ge(summed[h], n * SG + SG + q + 1)
                        dve.wait_ge(added, n * 2 * GPH + 2 * GPH + h * SG + q)
                        if extra:
                            nc.vector.tensor_tensor(Cc[0:high[1], bass.ds(at, W)], Cc[0:high[1], bass.ds(at, W)],
                                                    bank_of(h, q, 1),
                                                    ALU.add)
                        nc.vector.tensor_tensor(A[:, bass.ds(at, W)], A[:, bass.ds(at, W)],
                                                bank_of(h, q, 0), ALU.add
                                                ).then_inc(added, 1)

                def all_added(count):
                    dve.wait_ge(added, count + 2 * GPH)
                    dve.sem_inc(moved, 1)

                for h in range(S):
                    compare(0, h)
                    messages(0, h)
                with dve.Fori(0, NIT - 1) as i:
                    for h in range(S):
                        add(i, h)
                        if follow and h == S - 1:
                            due_chunks(net, dve, i, i + 1, lambda c: follow.vector(dve, c),
                                       lambda: all_added((r * NIT + i) * 2 * GPH + 2 * GPH))
                        compare(dve.snap(i + 1), h)
                        messages(dve.snap(i + 1), h)
                for h in range(S):
                    add(NIT - 1, h)
                nc.vector.tensor_scalar(net.window[:, :], net.window[:, :], float(W), None, ALU.add)
                nc.vector.tensor_scalar(net.base_now[:, :], net.base_now[:, :], float(W), float(N),
                                        ALU.add, ALU.min).then_inc(cleared, 1)
                dve.wait_ge(cleared, r + 2)
            if follow:
                due_chunks(net, dve, NIT - 1, None, lambda c: follow.vector(dve, c),
                           lambda: all_added(R * (NIT * 2 * GPH)))


class Shares:
    dense = False

    def __init__(self, net, tag):
        self.net, self.inverted = net, net.sem(f"{tag}_inverted")

    def vector_begin(self, dve):
        pass

    def vector(self, dve, c):
        chunk = self.net.C[0:H, bass.ds(c * CH, CH)]
        self.net.nc.vector.reciprocal(chunk, chunk).then_inc(self.inverted, 1)


class Sage:

    dense = True

    def __init__(self, net, tag, weight, bias, table, first=False):
        self.net, self.table, self.first = net, table, first
        self.weight, self.bias = net.dram[weight], net.dram[bias]
        self.w, self.b = net.wtmp[:, 0:2 * D], net.small[:, 0:1]
        self.last = net.small[0:1, 20:21]
        self.ends, self.count = net.wtmp[0:1, 512:512 + CH], net.wtmp[32:33, 512:512 + CH]
        s = lambda k: net.sem(f"{tag}_{k}")
        self.weights, self.scanned, self.counted = s("weights"), s("scanned"), s("counted")
        self.ends_free, self.ends_stored, self.counts_stored = s("ends_free"), s("ends_stored"), s("counts_stored")
        self.carried, self.inverse, self.mean, self.product = s("carried"), s("inverse"), s("mean"), s("product")
        self.h, self.brought, self.turned, self.rows = s("h"), s("brought"), s("turned"), s("rows")
        self.rows_free, self.stored = s("rows_free"), s("stored")

    def sync(self, sp):
        net = self.net
        sp.dma_start(self.w.rearrange("p (k n) -> p k n", k=2),
                     self.weight.rearrange("(k p) n -> p k n", k=2)).then_inc(self.weights, 16)
        sp.dma_start(self.b, self.bias.rearrange("(p a) -> p a", a=1)).then_inc(self.weights, 16)
        sp.sem_inc(self.rows_free, 1)
        sp.sem_inc(self.ends_free, 1)
        with sp.Fori(0, NCH) as c:
            if self.first:
                sp.wait_ge(self.counted, c + 1)
                sp.dma_start(net.CUM[0:1, bass.ds(c * CH, CH)], self.ends).then_inc(self.ends_stored, 16)
                sp.dma_start(net.CUM[1:2, bass.ds(c * CH, CH)], self.count).then_inc(self.counts_stored, 16)
                sp.wait_ge(self.ends_stored, c * 16 + 16)
                sp.wait_ge(self.counts_stored, c * 16 + 16)
                sp.sem_inc(self.ends_free, 1)
            store_rows(sp, self, c, self.table, D)

    def vector_begin(self, dve):
        if self.first:
            self.net.nc.vector.memset(self.last, 0.0).then_inc(self.scanned, 1)

    def vector(self, dve, c):
        net = self.net
        V = net.nc.vector
        if self.first:
            dve.wait_ge(self.ends_free, c + 1)
            dve.wait_ge(self.scanned, c + 1)
            V.tensor_copy(self.count, net.C[32:33, bass.ds(c * CH, CH)])
            V.tensor_tensor_scan(self.ends, net.C[0:1, bass.ds(c * CH, CH)],
                                 net.ones[0:1, 0:1].broadcast_to([1, CH]), self.last,
                                 ALU.add, ALU.subtract).then_inc(self.carried, 1)
            dve.wait_ge(self.carried, c + 1)
            V.tensor_copy(self.last, self.ends[:, CH - 1:CH]).then_inc(self.scanned, 1)
            dve.sem_inc(self.counted, 1)
            V.reciprocal(net.col(net.C, c), net.col(net.C, c)).then_inc(self.inverse, 1)
            dve.wait_ge(self.inverse, c + 1)
        V.tensor_tensor(net.col(net.A, c), net.col(net.A, c), net.col(net.C, c),
                        ALU.mult).then_inc(self.mean, 1)

    def tensor_begin(self, pe):
        pe.wait_ge(self.weights, 32)

    def tensor(self, pe, c):
        net = self.net
        pe.wait_ge(self.mean, c + 1)
        pe.wait_ge(self.brought, c + 1)
        net.nc.tensor.matmul(dense(net, 0), self.w[:, 0:D], net.col(net.B, c), start=True, stop=False)
        net.nc.tensor.matmul(dense(net, 0), self.w[:, D:2 * D], net.col(net.A, c),
                             start=False, stop=True).then_inc(self.product, 1)
        pe.wait_ge(self.brought, c + 2)
        turn_rows(net, pe, self, c)

    def scalar(self, act):
        net = self.net
        act.sem_inc(self.brought, 1)
        act.sem_inc(self.turned, 1)
        act.sem_inc(self.rows, 1)
        act.wait_ge(self.weights, 32)
        with act.Fori(0, NCH) as c:
            act.wait_ge(self.product, c + 1)
            act.wait_ge(self.turned, c + 1)
            net.nc.scalar.activation(net.turn[:, :], dense(net, 0), ACT.Relu, bias=self.b)
            net.nc.scalar.activation(net.col(net.B, c), dense(net, 0), ACT.Relu,
                                     bias=self.b).then_inc(self.brought, 1)
            copy_rows(net, act, self, c)



def dense(net, k, n=CH, high=P):
    return net.psum[0:high, (4 + k) * 512:(4 + k) * 512 + n]


def turn_rows(net, pe, f, c, k=3):
    pe.wait_ge(f.rows, c + 1)
    for j in range(4):
        t = net.nc.tensor.transpose(net.psum[0:SUB, (4 + k) * 512 + j * D:(4 + k) * 512 + (j + 1) * D],
                                    net.turn[:, j * SUB:(j + 1) * SUB], net.ident[:, :])
    t.then_inc(f.turned, 1)


def copy_rows(net, act, f, c, k=3):
    act.wait_ge(f.turned, c + 2)
    act.wait_ge(f.rows_free, c + 1)
    net.nc.scalar.copy(net.rows[0:SUB, 0:4 * D], dense(net, k, 4 * D, SUB)).then_inc(f.rows, 1)


def store_rows(sp, f, c, table, width):
    sp.wait_ge(f.rows, c + 2)
    sp.dma_start(table[bass.ds(c * CH, CH), :].rearrange("(t p) f -> p t f", p=SUB),
                 f.net.rows[0:SUB, 0:4 * width].rearrange("p (t f) -> p t f", f=width)
                 ).then_inc(f.stored, 16)
    sp.wait_ge(f.stored, c * 16 + 16)
    sp.sem_inc(f.rows_free, 1)


class Project:

    dense = True

    def __init__(self, net, tag):
        self.net = net
        s = lambda k: net.sem(f"{tag}_{k}")
        self.weights, self.masked, self.w_turned, self.select = s("weights"), s("masked"), s("w_turned"), s("select")
        self.w_ready, self.att_done, self.joined, self.average = s("w_ready"), s("att_done"), s("joined"), s("average")
        self.product, self.y, self.x_loaded, self.x = s("product"), s("y"), s("x_loaded"), s("x")
        self.x_saved, self.mean1, self.centred1, self.squared1 = s("x_saved"), s("mean1"), s("centred1"), s("squared1")
        self.var1, self.dev1, self.inverse1, self.h = s("var1"), s("dev1"), s("inverse1"), s("h")
        self.h_saved, self.mean2, self.centred2, self.squared2 = s("h_saved"), s("mean2"), s("centred2"), s("squared2")
        self.var2, self.dev2, self.inverse2, self.scaled = s("var2"), s("dev2"), s("inverse2"), s("scaled")
        self.brought, self.turned, self.rows, self.rows_free = s("brought"), s("turned"), s("rows"), s("rows_free")
        self.stored, self.carried = s("stored"), s("carried")
        self.ws, self.bs = net.wtmp[:, 0:2 * D], net.small[:, 5:6]
        self.w = net.wtmp[:, 264:264 + XW]
        self.wt = net.wtmp[:, 400:400 + D]
        self.att = net.wtmp[:, 528:528 + 2 * H]
        self.mask = net.wtmp[:, 536:536 + H]
        self.gain, self.shift = net.small[:, 0:1], net.small[:, 1:2]
        self.a_s, self.a_d = net.small[:, 2:3], net.small[:, 3:4]

    def sync(self, sp):
        net = self.net
        sp.dma_start(self.ws.rearrange("p (k n) -> p k n", k=2),
                     net.dram["L0_gnn_W2"].rearrange("(k p) n -> p k n", k=2)).then_inc(self.weights, 16)
        sp.dma_start(self.w[:, 0:D], net.dram["L1_gnn_W"]).then_inc(self.weights, 16)
        for to, name in ((self.bs, "L0_gnn_b2"), (self.gain, "L1_gnn_ln1_g"), (self.shift, "L1_gnn_ln1_b")):
            sp.dma_start(to, net.dram[name].rearrange("(p a) -> p a", a=1)).then_inc(self.weights, 16)
        for to, name in ((self.a_s, "L1_gnn_att_src"), (self.a_d, "L1_gnn_att_dst")):
            sp.dma_start(to, net.dram[name].rearrange("h (c a) -> (h c) a", a=1)).then_inc(self.weights, 16)
        sp.sem_inc(self.rows_free, 1)
        with sp.Fori(0, NCH) as c:
            at = sp.snap(c * CH)
            sp.wait_ge(self.average, c + 1)
            sp.dma_start(net.C[:, bass.ds(at, CH)], net.XT[:, bass.ds(at, CH)]).then_inc(self.x_loaded, 16)
            sp.wait_ge(self.x, c + 1)
            sp.sem_inc(self.carried, 1)
            sp.dma_start(net.XT[:, bass.ds(at, CH)], net.B[:, bass.ds(at, CH)]).then_inc(self.x_saved, 16)
            sp.wait_ge(self.h, c + 1)
            sp.dma_start(net.HT[:, bass.ds(at, CH)], net.B[:, bass.ds(at, CH)]).then_inc(self.h_saved, 16)
            sp.wait_ge(self.h_saved, c * 16 + 16)
            sp.sem_inc(self.carried, 1)
            store_rows(sp, self, c, net.XH, XW)

    def vector_begin(self, dve):
        V, net = self.net.nc.vector, self.net
        V.memset(self.mask, 0.0).then_inc(self.masked, 1)
        dve.wait_ge(self.masked, 1)
        for h in range(H):
            V.memset(self.mask[h * C:(h + 1) * C, h:h + 1], 1.0).then_inc(self.masked, 1)
        dve.wait_ge(self.masked, 1 + H)
        dve.wait_ge(self.weights, 112)
        V.tensor_scalar(self.att[:, 0:H], self.mask, self.a_s, None, ALU.mult)
        V.tensor_scalar(self.att[:, H:2 * H], self.mask, self.a_d, None, ALU.mult)
        dve.wait_ge(self.w_turned, 1)
        V.tensor_copy(self.wt, dense(net, 0, D)).then_inc(self.w_ready, 1)
        dve.wait_ge(self.select, 1)
        V.tensor_copy(head_select(net), dense(net, 1, D, H))
        dve.wait_ge(self.att_done, 1)
        V.tensor_copy(self.w[:, D:XW], dense(net, 2, 2 * H)).then_inc(self.joined, 1)

    def vector(self, dve, c):
        net = self.net
        V, A, B, Cc = net.nc.vector, net.col(net.A, c), net.col(net.B, c), net.col(net.C, c)
        V.tensor_tensor(A, A, Cc, ALU.mult).then_inc(self.average, 1)
        dve.wait_ge(self.y, c + 1)
        dve.wait_ge(self.x_loaded, c * 16 + 16)
        V.tensor_tensor(B, B, Cc, ALU.add).then_inc(self.x, 1)
        dve.wait_ge(self.mean1, c + 1)
        V.tensor_tensor(Cc, B, dense(net, 1), ALU.subtract).then_inc(self.centred1, 1)
        dve.wait_ge(self.dev1, c + 1)
        dve.wait_ge(self.x_saved, c * 16 + 16)
        dve.sem_inc(self.carried, 1)
        V.reciprocal(A, A).then_inc(self.inverse1, 1)
        dve.wait_ge(self.inverse1, c + 1)
        V.scalar_tensor_tensor(out=B, in0=Cc, scalar=0.0, in1=A, op0=ALU.max, op1=ALU.mult).then_inc(self.h, 1)
        dve.wait_ge(self.mean2, c + 1)
        V.tensor_tensor(Cc, B, dense(net, 1), ALU.subtract).then_inc(self.centred2, 1)
        dve.wait_ge(self.dev2, c + 1)
        dve.sem_inc(self.carried, 1)
        V.reciprocal(A, A).then_inc(self.inverse2, 1)
        dve.wait_ge(self.inverse2, c + 1)
        V.tensor_tensor(A, Cc, A, ALU.mult).then_inc(self.scaled, 1)

    def tensor_begin(self, pe):
        T, net = self.net.nc.tensor, self.net
        pe.wait_ge(self.weights, 112)
        T.transpose(dense(net, 0, D), self.w[:, 0:D], net.ident[:, :]).then_inc(self.w_turned, 1)
        pe.wait_ge(self.masked, 1 + H)
        T.transpose(dense(net, 1, D, H), self.mask, net.ident[:, :]).then_inc(self.select, 1)
        pe.wait_ge(self.w_ready, 1)
        T.matmul(dense(net, 2, 2 * H), self.wt, self.att, start=True, stop=True).then_inc(self.att_done, 1)
        pe.wait_ge(self.joined, 1)

    def tensor(self, pe, c):
        net = self.net
        T, A, B = net.nc.tensor, net.col(net.A, c), net.col(net.B, c)
        pe.wait_ge(self.average, c + 1)
        pe.wait_ge(self.rows, c + 1)
        T.matmul(dense(net, 0), self.ws[:, 0:D], B, start=True, stop=False)
        T.matmul(dense(net, 0), self.ws[:, D:2 * D], A, start=False, stop=True).then_inc(self.product, 1)
        for operand, result, mean, squared, var in ((self.x, 1, self.mean1, self.squared1, self.var1),
                                                    (self.h, 1, self.mean2, self.squared2, self.var2)):
            pe.wait_ge(operand, c + 1)
            T.matmul(dense(net, 1), net.mean_w[:, :], B, start=True, stop=True).then_inc(mean, 1)
            pe.wait_ge(squared, c + 1)
            T.matmul(dense(net, 2), net.mean_w[:, :], A, start=True, stop=True).then_inc(var, 1)
        pe.wait_ge(self.brought, c + 1)
        for j in range(4):
            bank = 4 + j // 2 * 3
            m = T.matmul(net.psum[0:SUB, bank * 512 + j % 2 * XW:bank * 512 + (j % 2 + 1) * XW],
                         net.turn[:, j * SUB:(j + 1) * SUB], self.w, start=True, stop=True)
        m.then_inc(self.turned, 1)

    def scalar(self, act):
        net = self.net
        S = net.nc.scalar
        act.sem_inc(self.turned, 1)
        act.sem_inc(self.rows, 1)
        act.wait_ge(self.weights, 112)
        with act.Fori(0, NCH) as c:
            act.wait_ge(self.product, c + 1)
            S.activation(net.col(net.B, c), dense(net, 0), ACT.Relu, bias=self.bs).then_inc(self.y, 1)
            for centred, squared, var, dev in ((self.centred1, self.squared1, self.var1, self.dev1),
                                               (self.centred2, self.squared2, self.var2, self.dev2)):
                act.wait_ge(centred, c + 1)
                act.sem_inc(self.carried, 1)
                S.activation(net.col(net.A, c), net.col(net.C, c), ACT.Square).then_inc(squared, 1)
                act.wait_ge(var, c + 1)
                act.sem_inc(self.carried, 1)
                S.activation(net.col(net.A, c), dense(net, 2), ACT.Sqrt, bias=net.eps[:, 0:1]).then_inc(dev, 1)
            act.wait_ge(self.scaled, c + 1)
            act.wait_ge(self.turned, c + 1)
            act.sem_inc(self.carried, 1)
            S.activation(net.turn[:, :], net.col(net.A, c), ACT.Identity, bias=self.shift, scale=self.gain)
            S.activation(net.col(net.A, c), net.col(net.A, c), ACT.Identity, bias=self.shift, scale=self.gain).then_inc(self.brought, 1)
            act.wait_ge(self.turned, c + 2)
            act.wait_ge(self.rows_free, c + 1)
            S.copy(net.rows[0:SUB, 0:2 * XW], dense(net, 0, 2 * XW, SUB))
            S.copy(net.rows[0:SUB, 2 * XW:4 * XW], dense(net, 3, 2 * XW, SUB)).then_inc(self.rows, 1)


def gat_gather(net):
    nc = net.nc
    rows = [net.work[:, h * HALF * XW:(h + 1) * HALF * XW] for h in range(2)]
    rows3 = [r.rearrange("p (t f) -> p t f", f=XW) for r in rows]
    name = lambda k: [net.sem(f"gg_{k}{h}") for h in range(2)]
    index_ready, stored, free, copied = name("index"), name("stored"), name("free"), name("copied")
    gathered = [net.pool_sem(), net.pool_sem()]
    moved, own = net.sem("gg_moved"), net.sem("gg_own")

    with nc.Block() as block:
        @block.gpsimd
        def _(pool):
            with pool.Fori(0, NIT) as i:
                for h in range(2):
                    pool.wait_ge(free[h], i + 1)
                    pool.wait_ge(copied[h], i + 1)
                    nc.gpsimd.tensor_copy(net.index[:, h, :],
                                          net.src_n[:, bass.ds(i * 2 * HALF + h * HALF, HALF)]
                                          ).then_inc(index_ready[h], 1)
                    pool.wait_ge(index_ready[h], i + 1)
                    pool.sem_inc(moved, 1)
                    for t in range(HALF):
                        pool.indirect_dma_start(
                            rows3[h][:, t, :], None, net.XH,
                            bass.IndirectOffsetOnAxis(ap=net.index[:, h, t:t + 1], axis=0)
                        ).then_inc(gathered[h], 16)

        @block.sync
        def _(sp):
            sp.dma_start(net.onehot[0:SUB, :, :, :].rearrange("p a t w -> p (a t w)")[:, 0:NSUB * 2 * H]
                         .rearrange("p (t f) -> p t f", f=2 * H),
                         net.XH[:, D:XW].rearrange("(t p) f -> p t f", p=SUB)).then_inc(own, 16)
            for h in range(2):
                sp.sem_inc(free[h], 1)
            with sp.Fori(0, NIT) as i:
                for h in range(2):
                    sp.wait_ge(gathered[h], i * 256 + 256)
                    sp.dma_start(net.G[bass.ds(i * 2 + h, 1), :, :].rearrange("a p f -> (a p) f"),
                                 rows[h]).then_inc(stored[h], 16)
                    sp.wait_ge(stored[h], i * 16 + 16)
                    sp.sem_inc(free[h], 1)
            sp.wait_ge(own, 16)

        @block.scalar
        def _(act):
            for h in range(2):
                act.sem_inc(copied[h], 1)
            with act.Fori(0, NIT) as i:
                for h in range(2):
                    act.wait_ge(gathered[h], i * 256 + 256)
                    nc.scalar.copy(
                        net.B[:, bass.ds(i * 2 * HALF * H, 2 * HALF * H)].rearrange(
                            "p (h t) -> p h t", h=H)[:, :, h * HALF:(h + 1) * HALF],
                        rows3[h][:, :, D:D + H].rearrange("p t h -> p h t")).then_inc(copied[h], 1)


def gat_softmax(net):
    nc = net.nc
    B, Cc = net.B, net.C
    SEG = 4 * EPP
    turned_rows = Cc[:, 0:SEG]
    score = Cc[:, SEG:2 * SEG].rearrange("p (h k) -> p h k", h=H)
    trial = Cc[:, 0:SEG].rearrange("p (h k) -> p h k", h=H)
    running = Cc[:, 0:SEG].rearrange("p (k h) -> p k h", h=H)
    dst = net.work[:, 1024:1024 + EPP]
    flag = net.work[:, 1024 + EPP:1024 + 2 * EPP]
    scratch = net.onehot[:, :, :, :].rearrange("p a t w -> p (a t w)")
    a_own = scratch[0:SUB, 0:NSUB * 2 * H].rearrange("p (t f) -> p t f", f=2 * H)
    ends3 = scratch[0:H, 800:800 + 3 * P]
    e_first, e_last, e_max = (ends3[:, k * P:(k + 1) * P] for k in range(3))
    before, value = scratch[0:H, 1184:1184 + P], scratch[0:H, 1312:1312 + P]
    joins, single = scratch[0:H, 1440:1440 + P - 1], scratch[0:H, 1568:1568 + P - 1]
    carry_row = scratch[0:H, 1696:1696 + P]
    first4, last4, max4 = (net.small[:, 24 + 4 * k:28 + 4 * k] for k in range(3))
    carry = net.small[:, 36:40]
    fix_i = net.small[:, 40:41].bitcast(I32)
    fix = net.small[:, 48:56]
    at = [Cc[0:SUB, k * NSUB:(k + 1) * NSUB] for k in range(8)]
    ends, counts, some, node, pos = at[0], at[1], at[2], at[3], at[4]
    last_i, start_i, node_i = (at[k].bitcast(I32) for k in (5, 6, 7))
    four = lambda k: Cc[0:SUB, 800 + k * 400:1200 + k * 400].rearrange("p (t h) -> p t h", h=H)
    found, peak, own = four(0), four(1), four(2)
    values = Cc[0:SUB, 2000:2800].rearrange("p (t f) -> p t f", f=2 * H)
    wide = lambda a: a.unsqueeze(2).broadcast_to([SUB, NSUB, H])
    BATCH = 10
    idx10 = net.small[0:SUB, 60:60 + BATCH].bitcast(I32)
    got10 = net.small[0:SUB, 72:72 + BATCH * H]
    put10 = net.work[0:SUB, 0:BATCH * 2 * H]
    p_self = net.p_self[:, :].rearrange("p (t h) -> p t h", h=H)

    s = {k: net.sem(f"gs_{k}") for k in
         ("brought", "turned", "copied", "by_head", "loaded", "dve", "ends", "carried", "stored",
          "positions", "index", "go", "kept", "values", "put_ready", "fix_ready",
          "starts", "exps", "exps_stored", "rows_loaded", "brought2", "turned2", "copied2")}
    s.update(found=net.pool_sem(), put=net.pool_sem(), fixed=net.pool_sem())
    v = [0]

    with nc.Block() as block:
        @block.gpsimd
        def _(pool):
            pool.iota(node_like(net), pattern=[[SUB, NSUB]], base=0, channel_multiplier=1).then_inc(s["go"], 1)
            pool.sem_inc(s["turned"], 2)

            def bring(c, k):
                pool.wait_ge(s["turned"], c + 1)
                nc.gpsimd.tensor_copy(slot(net, k, P), B[:, bass.ds(c * P, P)]).then_inc(s["brought"], 1)
            each_chunk(pool, bring, NIT)
            pool.wait_ge(s["positions"], 1)
            pool.wait_ge(s["stored"], 16)
            with pool.Fori(0, NSUB // BATCH) as i:
                pool.wait_ge(s["kept"], i + 1)
                nc.gpsimd.tensor_copy(idx10, last_i[:, bass.ds(i * BATCH, BATCH)]).then_inc(s["index"], 1)
                pool.wait_ge(s["index"], i + 1)
                pool.sem_inc(s["go"], 1)
                for t in range(BATCH):
                    pool.indirect_dma_start(
                        got10[:, t * H:(t + 1) * H], None, net.FD,
                        bass.IndirectOffsetOnAxis(ap=idx10[:, t:t + 1], axis=0)).then_inc(s["found"], 16)
            pool.wait_ge(s["kept"], NSUB // BATCH + 1)
            with pool.Fori(0, NSUB // BATCH) as i:
                nc.gpsimd.tensor_copy(idx10, start_i[:, bass.ds(i * BATCH, BATCH)]).then_inc(s["index"], 1)
                pool.wait_ge(s["index"], i + 1 + NSUB // BATCH)
                pool.wait_ge(s["put_ready"], i + 1)
                pool.sem_inc(s["go"], 1)
                for t in range(BATCH):
                    pool.indirect_dma_start(
                        net.SC, bass.IndirectOffsetOnAxis(ap=idx10[:, t:t + 1], axis=0),
                        put10[:, t * 2 * H:(t + 1) * 2 * H], None).then_inc(s["put"], 16)
                pool.wait_ge(s["put"], i * 16 * BATCH + 16 * BATCH)
            pool.wait_ge(s["values"], 16)
            pool.wait_ge(s["fix_ready"], 1)
            pool.indirect_dma_start(fix, None, net.NV, bass.IndirectOffsetOnAxis(ap=fix_i, axis=0)
                                    ).then_inc(s["fixed"], 16)
            pool.sem_inc(s["turned2"], 2)
            pool.wait_ge(s["rows_loaded"], 16 * H)

            def back(c, k):
                pool.wait_ge(s["turned2"], c + 1)
                nc.gpsimd.tensor_copy(slot(net, k, P), turned_rows[:, bass.ds(c * P, P)]
                                      ).then_inc(s["brought2"], 1)
            each_chunk(pool, back, NIT)

        @block.tensor
        def _(pe):
            def turn(c, k):
                pe.wait_ge(s["brought"], c + 1)
                pe.wait_ge(s["copied"], c + 1)
                nc.tensor.transpose(net.psum[:, k * 512:k * 512 + P], slot(net, k, P),
                                    net.ident[:, :]).then_inc(s["turned"], 1)
            each_chunk(pe, turn, NIT)
            pe.wait_ge(s["ends"], 1)
            for k, x in enumerate((first4, last4, max4)):
                t = nc.tensor.transpose(net.psum[0:H, 1024 + k * P:1024 + (k + 1) * P], x, net.ident[:, :])
            t.then_inc(s["carried"], 1)
            pe.wait_ge(s["ends"], 2)
            nc.tensor.transpose(net.psum[:, 1536:1536 + H], carry_row, net.ident[0:H, 0:H]
                                ).then_inc(s["carried"], 1)

            def turn2(c, k):
                pe.wait_ge(s["brought2"], c + 1)
                pe.wait_ge(s["copied2"], c + 1)
                nc.tensor.transpose(net.psum[:, k * 512:k * 512 + P], slot(net, k, P),
                                    net.ident[:, :]).then_inc(s["turned2"], 1)
            each_chunk(pe, turn2, NIT)

        @block.scalar
        def _(act):
            act.sem_inc(s["copied"], 2)

            def out(c, k):
                act.wait_ge(s["turned"], c + 3)
                nc.scalar.copy(turned_rows[:, bass.ds(c * P, P)], net.psum[:, k * 512:k * 512 + P]
                               ).then_inc(s["copied"], 1)
            each_chunk(act, out, NIT)
            act.sem_inc(s["copied2"], 2)
            act.wait_ge(s["fixed"], 16)

            def out2(c, k):
                act.wait_ge(s["turned2"], c + 3)
                nc.scalar.copy(B[:, bass.ds(c * P, P)], net.psum[:, k * 512:k * 512 + P]
                               ).then_inc(s["copied2"], 1)
            act.wait_ge(s["exps"], 2)
            nc.scalar.activation(p_self, own, ACT.Exp).then_inc(s["exps"], 1)
            nc.scalar.activation(Cc[:, SEG:2 * SEG], Cc[:, SEG:2 * SEG], ACT.Exp).then_inc(s["exps"], 1)
            each_chunk(act, out2, NIT)

        @block.sync
        def _(sp):
            sp.wait_ge(s["copied"], NIT + 2)
            for h in range(H):
                sp.dma_start(net.SH[h, :].rearrange("(b t e) -> t b e", t=2 * HALF, e=TILE),
                             turned_rows[h * 2 * HALF:(h + 1) * 2 * HALF, :]
                             .rearrange("t (b e) -> t b e", e=TILE)).then_inc(s["by_head"], 16)
            sp.dma_start(dst, net.DST.rearrange("(p k) -> p k", p=P)).then_inc(s["loaded"], 16)
            sp.wait_ge(s["by_head"], 16 * H)
            sp.dma_start(score, net.SH.rearrange("h (p k) -> p h k", p=P)).then_inc(s["loaded"], 16)
            sp.wait_ge(s["ends"], 3)
            sp.dma_start(net.FD.rearrange("(p k) h -> p (k h)", p=P), Cc[:, 0:SEG]).then_inc(s["stored"], 16)
            sp.wait_ge(s["stored"], 16)
            with nc.allow_non_contiguous_dma(reason="one node per element"):
                for k, x in enumerate((ends, counts)):
                    sp.dma_start(x, net.CUM[k, :].rearrange("(t p) -> p t", p=SUB),
                                 allow_slow_non_contiguous=True).then_inc(s["loaded"], 16)
            sp.wait_ge(s["ends"], 4)
            sp.dma_start(net.NV.rearrange("(t p) f -> p t f", p=SUB), values).then_inc(s["values"], 16)
            sp.wait_ge(s["put"], 16 * NSUB)
            sp.dma_start(B[:, 0:EPP * 2 * H], net.SC[0:EP, :].rearrange("(p k) f -> p (k f)", p=P)
                         ).then_inc(s["starts"], 16)
            sp.wait_ge(s["exps"], 4)
            sp.dma_start(net.PH.rearrange("h (p k) -> p h k", p=P), score).then_inc(s["exps_stored"], 16)
            sp.wait_ge(s["exps_stored"], 16)
            for h in range(H):
                sp.dma_start(turned_rows[h * 2 * HALF:(h + 1) * 2 * HALF, :].rearrange("t (b e) -> t b e", e=TILE),
                             net.PH[h, :].rearrange("(b t e) -> t b e", t=2 * HALF, e=TILE)
                             ).then_inc(s["rows_loaded"], 16)

        @block.vector
        def _(dve):
            def done(ins):
                v[0] += 1
                ins.then_inc(s["dve"], 1)
                dve.wait_ge(s["dve"], v[0])

            V = nc.vector
            dve.wait_ge(s["loaded"], 32)
            done(V.tensor_tensor(flag[:, 1:], dst[:, 1:], dst[:, 0:EPP - 1], ALU.is_equal))
            done(V.tensor_scalar(flag[:, 1:], flag[:, 1:], -1.0, BIG, ALU.add, ALU.mult))
            done(V.memset(flag[:, 0:1], 0.0))
            for h in range(H):
                done(V.tensor_tensor_scan(trial[:, h, :], flag, score[:, h, :], -BIG, ALU.add, ALU.max))
            done(V.tensor_copy(first4, dst[:, 0:1].broadcast_to([P, H])))
            done(V.tensor_copy(last4, dst[:, EPP - 1:EPP].broadcast_to([P, H])))
            V.tensor_copy(max4, trial[:, :, EPP - 1]).then_inc(s["ends"], 1)
            dve.wait_ge(s["carried"], 1)
            done(V.tensor_copy(ends3, net.psum[0:H, 1024:1024 + 3 * P]))
            done(V.memset(before, -BIG))
            done(V.memset(value, -BIG))
            for out, a in ((joins, e_first[:, 1:]), (single, e_first[:, 0:P - 1])):
                done(V.tensor_tensor(out, a, e_last[:, 0:P - 1], ALU.is_equal))
                done(V.tensor_scalar(out, out, -1.0, BIG, ALU.add, ALU.mult))
            done(V.tensor_tensor(before[:, 1:], joins, single, ALU.add))
            done(V.tensor_tensor(value[:, 1:], joins, e_max[:, 0:P - 1], ALU.add))
            V.tensor_tensor_scan(carry_row, before, value, -BIG, ALU.add, ALU.max).then_inc(s["ends"], 1)
            dve.wait_ge(s["carried"], 2)
            done(V.tensor_copy(carry, net.psum[:, 1536:1536 + H]))
            for h in range(H):
                done(V.tensor_tensor_scan(running[:, :, h], flag, score[:, h, :], carry[:, h:h + 1],
                                          ALU.add, ALU.max))
            dve.sem_inc(s["ends"], 1)
            dve.wait_ge(s["loaded"], 64)
            done(V.tensor_scalar(counts, counts, -1.0, None, ALU.add))
            done(V.tensor_scalar(pos, ends, -1.0, 0.0, ALU.add, ALU.max))
            done(V.tensor_copy(last_i, pos))
            done(V.tensor_scalar(some, counts, 0.0, None, ALU.is_gt))
            done(V.tensor_tensor(ends, ends, counts, ALU.subtract))
            done(V.tensor_copy(node, node_like(net)))
            done(V.tensor_scalar(node, node, float(EP), None, ALU.add))
            done(V.tensor_tensor(ends, ends, node, ALU.subtract))
            done(V.tensor_tensor(ends, ends, some, ALU.mult))
            done(V.tensor_tensor(ends, ends, node, ALU.add))
            done(V.tensor_copy(start_i, ends))
            dve.sem_inc(s["positions"], 1)
            dve.sem_inc(s["kept"], 1)
            with dve.Fori(0, NSUB // BATCH) as i:
                dve.wait_ge(s["found"], i * 16 * BATCH + 16 * BATCH)
                V.tensor_copy(Cc[0:SUB, bass.ds(i * BATCH * H + 800, BATCH * H)], got10).then_inc(s["kept"], 1)
            dve.wait_ge(s["kept"], NSUB // BATCH + 1)
            a_src, a_dst = a_own[:, :, 0:H], a_own[:, :, H:2 * H]
            done(V.tensor_tensor(found, found, wide(some), ALU.mult))
            done(V.tensor_scalar(some, some, -1.0, BIG, ALU.add, ALU.mult))
            done(V.tensor_tensor(found, found, wide(some), ALU.add))
            done(V.tensor_tensor(found, found, a_src, ALU.max))
            done(V.tensor_tensor(found, found, a_dst, ALU.add))
            done(V.scalar_tensor_tensor(out=peak, in0=found, scalar=0.2, in1=found, op0=ALU.mult, op1=ALU.max))
            done(V.tensor_tensor(own, a_src, a_dst, ALU.add))
            done(V.scalar_tensor_tensor(out=own, in0=own, scalar=0.2, in1=own, op0=ALU.mult, op1=ALU.max))
            done(V.tensor_tensor(own, own, peak, ALU.subtract))
            done(V.tensor_copy(values[:, :, 0:H], a_dst))
            done(V.tensor_copy(values[:, :, H:2 * H], peak))
            dve.sem_inc(s["ends"], 1)
            dve.sem_inc(s["exps"], 1)
            with dve.Fori(0, NSUB // BATCH) as i:
                dve.wait_ge(s["index"], i + 1 + NSUB // BATCH)
                V.tensor_copy(put10, Cc[0:SUB, bass.ds(i * BATCH * 2 * H + 2000, BATCH * 2 * H)]
                              ).then_inc(s["put_ready"], 1)
            done(V.tensor_copy(fix_i, dst[:, 0:1]))
            dve.sem_inc(s["fix_ready"], 1)
            done(V.tensor_tensor(flag[:, 1:], dst[:, 1:], dst[:, 0:EPP - 1], ALU.is_equal))
            spread = B[:, 0:EPP * 2 * H].rearrange("p (k f) -> p k f", f=2 * H)
            dve.wait_ge(s["starts"], 16)
            dve.wait_ge(s["fixed"], 16)
            done(V.tensor_copy(spread[:, 0, :], fix))
            for f in range(2 * H):
                done(V.tensor_tensor_scan(spread[:, :, f], flag, spread[:, :, f], 0.0, ALU.mult, ALU.add))
            sp_dst = spread[:, :, 0:H].rearrange("p k h -> p h k")
            sp_max = spread[:, :, H:2 * H].rearrange("p k h -> p h k")
            done(V.tensor_tensor(score, score, sp_dst, ALU.add))
            done(V.scalar_tensor_tensor(out=score, in0=score, scalar=0.2, in1=score, op0=ALU.mult, op1=ALU.max))
            done(V.tensor_tensor(score, score, sp_max, ALU.subtract))
            done(V.tensor_scalar(score, score, 0.0, None, ALU.min))
            dve.sem_inc(s["exps"], 1)


def node_like(net):
    return net.wtmp[0:SUB, 700:700 + NSUB].bitcast(I32)


def head_select(net):
    return net.wtmp[0:H, 540:540 + D]


def gat_begin(net):
    nc = net.nc
    A, Cc = net.A, net.C
    s = {k: net.sem(f"gb_{k}") for k in ("brought", "used", "spread", "product", "begun")}

    with nc.Block() as block:
        @block.gpsimd
        def _(pool):
            pool.sem_inc(s["used"], 2)

            def bring(c, k):
                pool.wait_ge(s["used"], c + 1)
                own = net.p_self[:, bass.ds(c * 4 * H, 4 * H)]
                nc.gpsimd.tensor_copy(net.work[0:SUB, 1024 + k * 4 * H:1024 + (k + 1) * 4 * H], own)
                nc.gpsimd.tensor_copy(net.work[0:SUB, k * 512:(k + 1) * 512].rearrange("p (t c) -> p t c", c=C),
                                      own.unsqueeze(2).broadcast_to([SUB, 4 * H, C])).then_inc(s["brought"], 1)
            each_chunk(pool, bring)

        @block.tensor
        def _(pe):
            def products(c, k):
                pe.wait_ge(s["brought"], c + 1)
                pe.wait_ge(s["begun"], c + 1)
                nc.tensor.matmul(net.bank(2, c), net.wtmp[:, 264:264 + D], net.col(A, c), start=True, stop=True)
                for j in range(4):
                    m = nc.tensor.matmul(
                        net.psum[:, k * 512 + j * SUB:k * 512 + (j + 1) * SUB],
                        net.work[0:SUB, k * 512 + j * D:k * 512 + (j + 1) * D],
                        net.ident[0:SUB, 0:SUB], start=True, stop=True)
                for j in range(4):
                    m = nc.tensor.matmul(
                        net.psum[0:H, (4 + k) * 512 + j * SUB:(4 + k) * 512 + (j + 1) * SUB],
                        net.work[0:SUB, 1024 + (4 * k + j) * H:1024 + (4 * k + j + 1) * H],
                        net.ident[0:SUB, 0:SUB], start=True, stop=True)
                m.then_inc(s["used"], 1)
            each_chunk(pe, products)

        @block.scalar
        def _(act):
            with act.Fori(0, NCH) as c:
                act.wait_ge(s["used"], c + 3)
                nc.scalar.copy(net.work[:, bass.ds((c % 2) * 512 + 1536, CH)], net.bank(0, c))
                nc.scalar.copy(Cc[0:H, bass.ds(c * CH, CH)],
                               net.psum[0:H, bass.ds((c % 2) * 512 + 4 * 512, CH)]).then_inc(s["spread"], 1)

        @block.vector
        def _(dve):
            nc.vector.memset(A[:, N:REG], 0.0)
            nc.vector.memset(Cc[:, N:REG], 1.0)
            dve.sem_inc(s["begun"], 2)
            with dve.Fori(0, NCH) as c:
                dve.wait_ge(s["spread"], c + 1)
                nc.vector.tensor_tensor(net.col(A, c), net.bank(2, c),
                                        net.work[:, bass.ds((c % 2) * 512 + 1536, CH)],
                                        ALU.mult).then_inc(s["begun"], 1)


def gat_output(net):
    nc = net.nc
    A, B, Cc = net.A, net.B, net.C
    w1, w2 = net.wtmp[:, 0:2 * D], net.wtmp[:, 2 * D:4 * D]
    gain, bias, gat_b, b1, b2 = (net.small[:, 0:1], net.small[:, 1:2], net.small[:, 2:3],
                                 net.small[:, 4:6], net.small[:, 3:4])
    s = {k: net.sem(f"go_{k}") for k in
         ("weights", "h", "shares", "selectors", "spread", "inverse", "ratio", "sum", "mean", "centred", "squared", "var", "dev",
          "carried", "scaled", "normed", "up", "gelu", "down", "out")}
    hidden = [net.work[:, k * 1024:(k + 1) * 1024] for k in range(2)]

    with nc.Block() as block:
        @block.sync
        def _(sp):
            sp.dma_start(B[:, 0:N], net.HT).then_inc(s["h"], 16)
            sp.dma_start(w1, net.dram["L1_gnn_w1"]).then_inc(s["weights"], 16)
            sp.dma_start(w2.rearrange("p (k n) -> p k n", k=2),
                         net.dram["L1_gnn_w2"].rearrange("(k p) n -> p k n", k=2)).then_inc(s["weights"], 16)
            for to, name in ((gain, "L1_gnn_ln2_g"), (bias, "L1_gnn_ln2_b"), (gat_b, "L1_gnn_gat_b"),
                             (b2, "L1_gnn_b2")):
                sp.dma_start(to, net.dram[name].rearrange("(p a) -> p a", a=1)).then_inc(s["weights"], 16)
            for k in range(2):
                sp.dma_start(b1[:, k:k + 1], net.dram["L1_gnn_b1"][k * D:(k + 1) * D]
                             .rearrange("(p a) -> p a", a=1)).then_inc(s["weights"], 16)

        @block.tensor
        def _(pe):
            pe.sem_inc(s["down"], 2)
            pe.sem_inc(s["var"], 2)
            pe.sem_inc(s["spread"], 2)
            pe.wait_ge(s["selectors"], 5)
            pe.wait_ge(s["weights"], 128)

            def shares(c, k):
                pe.wait_ge(s["ratio"], c + 1)
                nc.tensor.matmul(net.psum[:, 0:CH], head_select(net), Cc[0:H, bass.ds(c * CH, CH)],
                                 start=True, stop=True).then_inc(s["shares"], 1)

            def mean(c, k):
                pe.wait_ge(s["sum"], c + 1)
                pe.wait_ge(s["centred"], c + 1)
                nc.tensor.matmul(net.psum[:, 512:512 + CH], net.mean_w[:, :], net.col(B, c),
                                 start=True, stop=True).then_inc(s["mean"], 1)

            def up(c, k):
                pe.wait_ge(s["normed"], c + 1)
                pe.wait_ge(s["gelu"], c + 1)
                for j in range(2):
                    m = nc.tensor.matmul(net.psum[:, (6 + j) * 512:(6 + j) * 512 + CH],
                                         w1[:, j * D:(j + 1) * D], net.col(A, c), start=True, stop=True)
                m.then_inc(s["up"], 1)

            def down(c, k):
                pe.wait_ge(s["gelu"], c + 2)
                pe.wait_ge(s["out"], c + 1)
                for j in range(2):
                    m = nc.tensor.matmul(net.psum[:, 1024:1024 + CH], w2[:, j * D:(j + 1) * D],
                                         hidden[k][:, j * 512:j * 512 + CH], start=(j == 0), stop=(j == 1))
                m.then_inc(s["down"], 1)

            staggered(pe, (1, shares), (2, mean), *inverse_steps_tensor(net, pe, s, s["scaled"], lambda k: 3),
                      (8, up), (9, down))

        @block.vector
        def _(dve):
            make_selectors(net, dve, s)
            for x in ("ratio", "centred", "out"):
                dve.sem_inc(s[x], 1)
            dve.sem_inc(s["scaled"], 2)
            dve.wait_ge(s["weights"], 128)
            dve.wait_ge(s["h"], 16)

            def ratio(c, k):
                dve.wait_ge(s["shares"], c + 1)
                nc.vector.tensor_tensor(net.col(A, c), net.col(A, c), net.psum[:, 0:CH],
                                        ALU.mult).then_inc(s["ratio"], 1)
                dve.wait_ge(s["ratio"], c + 2)
                nc.vector.scalar_tensor_tensor(out=net.col(B, c), in0=net.col(A, c), scalar=gat_b,
                                               in1=net.col(B, c), op0=ALU.add,
                                               op1=ALU.add).then_inc(s["sum"], 1)

            def centre(c, k):
                dve.wait_ge(s["mean"], c + 1)
                nc.vector.tensor_tensor(net.col(Cc, c), net.col(B, c), net.psum[:, 512:512 + CH],
                                        ALU.subtract).then_inc(s["centred"], 1)

            def out(c, k):
                dve.wait_ge(s["down"], c + 3)
                nc.vector.scalar_tensor_tensor(out=net.col(B, c), in0=net.psum[:, 1024:1024 + CH],
                                               scalar=b2, in1=net.col(B, c), op0=ALU.add,
                                               op1=ALU.add).then_inc(s["out"], 1)

            staggered(dve, (1, ratio), (2, centre), *inverse_steps_vector(
                net, dve, s, lambda c, bank: nc.vector.tensor_tensor(
                    net.col(A, c), net.col(Cc, c), bank, ALU.mult).then_inc(s["scaled"], 1), lambda k: 3),
                (9, out))

        @block.scalar
        def _(act):
            act.sem_inc(s["dev"], 2)
            act.sem_inc(s["gelu"], 1)
            act.wait_ge(s["weights"], 128)

            def normed(c, k):
                act.wait_ge(s["scaled"], c + 3)
                nc.scalar.activation(net.col(A, c), net.col(A, c), ACT.Identity,
                                     bias=bias, scale=gain).then_inc(s["normed"], 1)

            def gelu(c, k):
                act.wait_ge(s["up"], c + 1)
                act.wait_ge(s["down"], c + 1)
                for j in range(2):
                    g = nc.scalar.activation(hidden[k][:, j * 512:j * 512 + CH],
                                             net.psum[:, (6 + j) * 512:(6 + j) * 512 + CH],
                                             ACT.Gelu, bias=b1[:, j:j + 1])
                g.then_inc(s["gelu"], 1)

            staggered(act, *inverse_steps_scalar(net, act, s, Cc, 1), (7, normed), (8, gelu))


def gin_output(net):
    nc = net.nc
    A, B, Cc = net.A, net.B, net.C
    w1, w2 = net.wtmp[:, 0:2 * D], net.wtmp[:, 2 * D:4 * D]
    vec = net.small
    g1, b1, g2, b2, onep = vec[:, 0:2], vec[:, 2:4], vec[:, 4:5], vec[:, 5:6], vec[:, 6:7]
    mv = [vec[:, 8 + 2 * k:10 + 2 * k] for k in range(3)]
    scale, shift = vec[:, 16:19], vec[:, 20:23]
    stats = [net.onehot[:, :, :, :].rearrange("p a t w -> p (a t w)")[:, k * 6 * NCH:(k + 1) * 6 * NCH]
             for k in range(3)]
    hidden = [net.work[:, k * 1024:(k + 1) * 1024] for k in range(2)]
    s = {k: net.sem(f"gi_{k}") for k in
         ("weights", "h", "step", "z", "first", "stat", "deviation", "up", "hid", "down", "out", "last",
          "sum", "kept")}

    def fold(dve, k, gain, bias, wait, count):
        V = nc.vector
        V.bn_aggr(mv[k], stats[k]).then_inc(s["step"], 1)
        dve.wait_ge(s["step"], count + 1)
        dve.sem_inc(s["deviation"], 1)
        dve.wait_ge(s["deviation"], wait)
        V.reciprocal(scale[:, k:k + 1], scale[:, k:k + 1]).then_inc(s["step"], 1)
        dve.wait_ge(s["step"], count + 2)
        V.tensor_tensor(scale[:, k:k + 1], scale[:, k:k + 1], gain, ALU.mult).then_inc(s["step"], 1)
        dve.wait_ge(s["step"], count + 3)
        V.tensor_tensor(shift[:, k:k + 1], mv[k][:, 0:1], scale[:, k:k + 1], ALU.mult).then_inc(s["step"], 1)
        dve.wait_ge(s["step"], count + 4)
        V.tensor_tensor(shift[:, k:k + 1], bias, shift[:, k:k + 1], ALU.subtract).then_inc(s["step"], 1)

    with nc.Block() as block:
        @block.sync
        def _(sp):
            sp.dma_start(net.ES, Cc[:, 0:N]).then_inc(s["kept"], 16)
            sp.dma_start(B[:, 0:N], net.HT).then_inc(s["h"], 16)
            sp.dma_start(w1, net.dram["L2_gnn_W1"]).then_inc(s["weights"], 16)
            sp.dma_start(w2.rearrange("p (k n) -> p k n", k=2),
                         net.dram["L2_gnn_W2"].rearrange("(k p) n -> p k n", k=2)).then_inc(s["weights"], 16)
            for to, name in ((g1, "L2_gnn_g1"), (b1, "L2_gnn_b1")):
                for k in range(2):
                    sp.dma_start(to[:, k:k + 1], net.dram[name][k * D:(k + 1) * D]
                                 .rearrange("(p a) -> p a", a=1)).then_inc(s["weights"], 16)
            for to, name in ((g2, "L2_gnn_g2"), (b2, "L2_gnn_b2")):
                sp.dma_start(to, net.dram[name].rearrange("(p a) -> p a", a=1)).then_inc(s["weights"], 16)
            sp.dma_start(onep, net.dram["L2_gnn_eps"].rearrange("(a b) -> a b", a=1)
                         .broadcast_to([P, 1])).then_inc(s["weights"], 16)
            sp.wait_ge(s["kept"], 16)

        @block.vector
        def _(dve):
            dve.wait_ge(s["weights"], 144)
            nc.vector.tensor_scalar(onep, onep, 1.0, None, ALU.add).then_inc(s["step"], 1)
            dve.wait_ge(s["step"], 1)
            dve.wait_ge(s["h"], 16)
            with dve.Fori(0, NCH) as c:
                nc.vector.scalar_tensor_tensor(out=net.col(A, c), in0=net.col(B, c), scalar=onep,
                                               in1=net.col(A, c), op0=ALU.mult,
                                               op1=ALU.add).then_inc(s["z"], 1)
            dve.sem_inc(s["stat"], 2)

            def statistics(c, k):
                dve.wait_ge(s["first"], c + 1)
                for j in range(2):
                    last = nc.vector.bn_stats(stats[j][:, bass.ds(c * 6, 6)],
                                              net.psum[:, (2 * k + j) * 512:(2 * k + j) * 512 + CH])
                last.then_inc(s["stat"], 1)
            each_chunk(dve, statistics)
            dve.wait_ge(s["stat"], NCH + 2)
            fold(dve, 0, g1[:, 0:1], b1[:, 0:1], 2, 1)
            fold(dve, 1, g1[:, 1:2], b1[:, 1:2], 4, 6)
            dve.sem_inc(s["out"], 2)

            def out(c, k):
                dve.wait_ge(s["down"], c + 1)
                bank = net.psum[:, (4 + k) * 512:(4 + k) * 512 + CH]
                nc.vector.tensor_copy(net.col(A, c), bank)
                nc.vector.bn_stats(stats[2][:, bass.ds(c * 6, 6)], bank).then_inc(s["out"], 1)
            each_chunk(dve, out)
            dve.wait_ge(s["out"], NCH + 2)
            fold(dve, 2, g2, b2, 6, 11)
            with dve.Fori(0, NCH) as c:
                dve.wait_ge(s["last"], c + 1)
                nc.vector.tensor_tensor(net.col(B, c), net.col(A, c), net.col(B, c),
                                        ALU.add).then_inc(s["sum"], 1)

        @block.scalar
        def _(act):
            for k in range(3):
                if k == 2:
                    act.wait_ge(s["step"], 11)
                    act.sem_inc(s["hid"], 2)

                    def normed(c, kk):
                        act.wait_ge(s["up"], c + 1)
                        act.wait_ge(s["out"], c + 1)
                        for j in range(2):
                            last = nc.scalar.activation(
                                hidden[kk][:, j * 512:j * 512 + CH],
                                net.psum[:, (2 * kk + j) * 512:(2 * kk + j) * 512 + CH], ACT.Relu,
                                bias=shift[:, j:j + 1], scale=scale[:, j:j + 1])
                        last.then_inc(s["hid"], 1)
                    each_chunk(act, normed)
                act.wait_ge(s["deviation"], 2 * k + 1)
                nc.scalar.activation(scale[:, k:k + 1], mv[k][:, 1:2], ACT.Sqrt,
                                     bias=net.eps[:, 0:1]).then_inc(s["deviation"], 1)
            act.wait_ge(s["step"], 16)
            with act.Fori(0, NCH) as c:
                nc.scalar.activation(net.col(A, c), net.col(A, c), ACT.Relu,
                                     bias=shift[:, 2:3], scale=scale[:, 2:3]).then_inc(s["last"], 1)

        @block.tensor
        def _(pe):
            pe.wait_ge(s["weights"], 144)

            def up(c, k, done, free):
                pe.wait_ge(s["z"], c + 1)
                pe.wait_ge(free, c + 1)
                for j in range(2):
                    m = nc.tensor.matmul(net.psum[:, (2 * k + j) * 512:(2 * k + j) * 512 + CH],
                                         w1[:, j * D:(j + 1) * D], net.col(A, c), start=True, stop=True)
                m.then_inc(done, 1)

            def down(c, k):
                pe.wait_ge(s["hid"], c + 3)
                pe.wait_ge(s["out"], c + 1)
                for j in range(2):
                    m = nc.tensor.matmul(net.psum[:, (4 + k) * 512:(4 + k) * 512 + CH],
                                         w2[:, j * D:(j + 1) * D],
                                         hidden[k][:, j * 512:j * 512 + CH], start=(j == 0), stop=(j == 1))
                m.then_inc(s["down"], 1)

            each_chunk(pe, lambda c, k: up(c, k, s["first"], s["stat"]))
            pe.wait_ge(s["stat"], NCH + 2)
            up(0, 0, s["up"], s["hid"])
            with pe.Fori(0, NCH // 2) as i:
                c = pe.snap(i * 2)
                up(c + 1, 1, s["up"], s["hid"])
                down(c, 0)
                up(c + 2, 0, s["up"], s["hid"])
                down(c + 1, 1)
            down(NCH - 1, 0)


class Finish:

    dense = True

    def __init__(self, net, tag, out):
        self.net, self.out = net, out
        s = lambda k: net.sem(f"{tag}_{k}")
        self.x_loaded, self.es_loaded, self.summed, self.half = s("x"), s("edge_sum"), s("summed"), s("half")
        self.brought, self.turned, self.rows = s("brought"), s("turned"), s("rows")
        self.rows_free, self.stored = s("rows_free"), s("stored")
        self.x, self.es = net.wtmp[:, 0:CH], net.wtmp[:, 512:512 + CH]

    def sync(self, sp):
        net = self.net
        sp.sem_inc(self.rows_free, 1)
        with sp.Fori(0, NCH) as c:
            sp.wait_ge(self.summed, c + 1)
            sp.dma_start(self.x, net.XT[:, bass.ds(c * CH, CH)]).then_inc(self.x_loaded, 16)
            sp.dma_start(self.es, net.ES[:, bass.ds(c * CH, CH)]).then_inc(self.es_loaded, 16)
            store_rows(sp, self, c, self.out, D)

    def vector_begin(self, dve):
        dve.sem_inc(self.summed, 1)

    def vector(self, dve, c):
        net = self.net
        V = net.nc.vector
        V.tensor_tensor(net.col(net.A, c), net.col(net.A, c), net.col(net.B, c), ALU.add).then_inc(self.half, 1)
        dve.wait_ge(self.x_loaded, c * 16 + 16)
        dve.wait_ge(self.es_loaded, c * 16 + 16)
        V.tensor_tensor(self.x, self.x, self.es, ALU.add).then_inc(self.half, 1)
        dve.wait_ge(self.half, c * 2 + 2)
        dve.wait_ge(self.turned, c + 1)
        V.tensor_tensor(net.turn[:, :], net.col(net.A, c), self.x, ALU.add).then_inc(self.summed, 1)

    def tensor_begin(self, pe):
        pe.sem_inc(self.turned, 1)

    def tensor(self, pe, c):
        pe.wait_ge(self.summed, c + 2)
        turn_rows(self.net, pe, self, c)

    def scalar(self, act):
        act.sem_inc(self.rows, 1)
        with act.Fori(0, NCH) as c:
            copy_rows(self.net, act, self, c)


def program(nc, dram, out):
    with ExitStack() as ctx:
        net = Net(nc, ctx, dram)
        allocate(net)
        for step in (
                lambda: prepare(net),
                lambda: normalise(net, "n0", first=True, table=net.TA),
                lambda: aggregate(net, "agg0", net.TA, "count",
                                  Sage(net, "sage0", "L0_gnn_W0", "L0_gnn_b0", net.TB, first=True)),
                lambda: aggregate(net, "agg1", net.TB, None,
                                  Sage(net, "sage1", "L0_gnn_W1", "L0_gnn_b1", net.TA)),
                lambda: aggregate(net, "agg2", net.TA, None, Project(net, "project")),
                lambda: gat_gather(net),
                lambda: gat_softmax(net),
                lambda: gat_begin(net),
                lambda: aggregate(net, "agg3", extra="attention", follow=Shares(net, "shares")),
                lambda: gat_output(net),
                lambda: normalise(net, "n2", keep=True, table=net.TB),
                lambda: aggregate(net, "agg4", net.TB, "edges"),
                lambda: gin_output(net),
                lambda: normalise(net, "n3", table=net.TA),
                lambda: aggregate(net, "agg5", net.TA, None, Finish(net, "finish", out))):
            with net.stage():
                step()


INPUTS = ["x", "src", "dst", "edge_attr_128", "L0_gnn_W0", "L0_gnn_b0", "L0_gnn_W1", "L0_gnn_b1",
          "L0_gnn_W2", "L0_gnn_b2", "L1_gnn_ln1_g", "L1_gnn_ln1_b", "L1_gnn_W", "L1_gnn_att_src",
          "L1_gnn_att_dst", "L1_gnn_gat_b", "L1_gnn_ln2_g", "L1_gnn_ln2_b", "L1_gnn_w1", "L1_gnn_b1",
          "L1_gnn_w2", "L1_gnn_b2", "L2_gnn_eps", "L2_gnn_W1", "L2_gnn_g1", "L2_gnn_b1", "L2_gnn_W2",
          "L2_gnn_g2", "L2_gnn_b2"]


def kernel(**inputs):
    import numpy as np
    import concourse.bacc as bacc
    from concourse.bass_utils import run_bass_kernel_spmd

    nc = bacc.Bacc("TRN2", target_bir_lowering=False, num_devices=1)
    arrays, dram = {}, {}
    for name in INPUTS:
        a = np.ascontiguousarray(inputs[name])
        if a.ndim == 0:
            a = a.reshape(1)
        arrays[f"in_{name}"] = a
        dram[name] = nc.dram_tensor(f"in_{name}", a.shape, mybir.dt.from_np(a.dtype),
                                    kind="ExternalInput").ap()
    out = nc.dram_tensor("out", [N, D], F32, kind="ExternalOutput").ap()
    program(nc, dram, out)
    r = run_bass_kernel_spmd(nc, [arrays], core_ids=[0])
    return r.results[0]["out"]
```
